# Optimizing a Trainium2 kernel written in Bass

```python
import numpy as np
import jax
import jax.numpy as jnp

def _softmax(x, axis=-1):
    return jax.nn.softmax(x, axis=axis)

def _gelu(x):
    return jax.nn.gelu(x, approximate=True)

def _silu(x):
    return jax.nn.silu(x)

def _sigmoid(x):
    return jax.nn.sigmoid(x)

def _layernorm(x, axis=-1, eps=1e-05):
    m = jnp.mean(x, axis=axis, keepdims=True)
    v = jnp.var(x, axis=axis, keepdims=True)
    return (x - m) / jnp.sqrt(v + eps)

def _scatter_add(tgt, idx, src, axis=0):
    return tgt.at[idx].add(src)

def _segment_sum(src, seg, n):
    return jax.ops.segment_sum(src, seg, n)
kernel_name = 'mk_metaformer_d4_conv_nchw256_r2_1d916c'

def setup_inputs(seed: int=0):
    np.random.seed(seed)
    _w = jnp.asarray

    def _rec_inputs():
        import jax
        import jax.numpy as jnp
        _gk = jax.random.key(seed)
        x = 7.22e-05 + 1 * jax.random.normal(jax.random.fold_in(_gk, 1), (8, 128, 32, 32), jnp.float32)
        return x
    x = _rec_inputs()

    def _L0_conv_setup():
        import jax, jax.numpy as jnp
        import numpy as np
        B, C, H, W = (8, 128, 32, 32)
        OUT_C = 128
        K = 3
        DG = 1
        CPG = C // DG
        KK = K * K

        def _sample_group(img, py, px):
            Hh, Ww = (img.shape[1], img.shape[2])
            flat = img.reshape(img.shape[0], Hh * Ww)
            y0 = jnp.floor(py)
            x0 = jnp.floor(px)
            wy = py - y0
            wx = px - x0

            def gather(yi, xi):
                valid = ((yi >= 0) & (yi < Hh) & (xi >= 0) & (xi < Ww)).astype(img.dtype)
                idx = (jnp.clip(yi, 0, Hh - 1) * Ww + jnp.clip(xi, 0, Ww - 1)).astype(jnp.int32)
                v = jnp.take(flat, idx.reshape(-1), axis=1).reshape(img.shape[0], *yi.shape)
                return v * valid
            out = gather(y0, x0) * ((1.0 - wy) * (1.0 - wx)) + gather(y0, x0 + 1.0) * ((1.0 - wy) * wx) + gather(y0 + 1.0, x0) * (wy * (1.0 - wx)) + gather(y0 + 1.0, x0 + 1.0) * (wy * wx)
            return jnp.transpose(out, (1, 0, 2, 3))

        def _forward(x, w_off, b_off, w_conv):
            b = x.shape[0]
            pad = K // 2
            out = jax.lax.conv_general_dilated(x, w_off, window_strides=(1, 1), padding=[(pad, pad), (pad, pad)], dimension_numbers=('NCHW', 'OIHW', 'NCHW')) + b_off[None, :, None, None]
            o1, o2, m = jnp.split(out, 3, axis=1)
            dy = o1.reshape(b, DG, KK, H, W)
            dx = o2.reshape(b, DG, KK, H, W)
            mask = jax.nn.sigmoid(m).reshape(b, DG, KK, 1, H, W)
            ys = jnp.arange(H, dtype=x.dtype)[None, None, None, :, None]
            xs = jnp.arange(W, dtype=x.dtype)[None, None, None, None, :]
            py = ys + dy
            px = xs + dx
            xg = x.reshape(b, DG, CPG, H, W)
            sampled = jax.vmap(jax.vmap(_sample_group))(xg, py, px)
            y = sampled * mask
            y = y.reshape(b, C * KK, H, W)
            return jnp.einsum('bkhw,ok->bohw', y, w_conv)
        key = jax.random.key(seed)
        k1, k2, k3 = jax.random.split(key, 3)
        x = jax.random.normal(k1, (B, C, H, W), jnp.float32)
        w_off = jax.random.normal(k2, (DG * 3 * KK, C, K, K), jnp.float32) * 0.01
        b_off = jnp.zeros((DG * 3 * KK,), jnp.float32)
        w_conv = jax.random.normal(k3, (OUT_C, C * KK), jnp.float32) / np.sqrt(C * KK).astype(np.float32)
        return {'x': x, 'w_off': w_off, 'b_off': b_off, 'w_conv': w_conv}
    _L0_conv_all = _L0_conv_setup()
    _L0_conv_in = {k: v for k, v in _L0_conv_all.items() if k in ('w_off', 'b_off', 'w_conv')}
    del _L0_conv_all

    def _L0_ffn_setup():
        import jax, jax.numpy as jnp
        import numpy as np
        B, T, D, H, E = (16, 2048, 128, 256, 8)
        key = jax.random.key(seed)
        ks = jax.random.split(key, 5)
        x = jax.random.normal(ks[0], (B, T, D), dtype=jnp.float32)
        gate_w = jax.random.normal(ks[1], (D, E), dtype=jnp.float32) * 0.02
        gate_b = jnp.zeros((E,), dtype=jnp.float32)
        W1 = jax.random.normal(ks[2], (E, D, H), dtype=jnp.float32) * 0.02
        b1 = jnp.zeros((E, H), dtype=jnp.float32)
        W2 = jax.random.normal(ks[3], (E, H, D), dtype=jnp.float32) * 0.02
        b2 = jnp.zeros((E, D), dtype=jnp.float32)
        return {'x': x, 'gate_w': gate_w, 'gate_b': gate_b, 'W1': W1, 'b1': b1, 'W2': W2, 'b2': b2}
    _L0_ffn_all = _L0_ffn_setup()
    _L0_ffn_in = {k: v for k, v in _L0_ffn_all.items() if k in ('gate_w', 'gate_b', 'W1', 'b1', 'W2', 'b2')}
    del _L0_ffn_all

    def _L1_conv_setup():
        import jax, jax.numpy as jnp
        import numpy as np
        from jax import lax

        def _affine8bit_dequant(weight):
            min_val = jnp.min(weight)
            max_val = jnp.max(weight)
            scale = (max_val - min_val) / 255.0
            zero_point = jnp.round(jnp.clip(255.0 - max_val / scale, 0.0, 255.0))
            w_q = jnp.round(jnp.clip(zero_point + weight / scale, 0.0, 255.0))
            return scale * (w_q - zero_point)
        key = jax.random.key(seed)
        k1, k2, k3 = jax.random.split(key, 3)
        x = jax.random.normal(k1, (32, 128, 56, 56), dtype=jnp.float32)
        weight = jax.random.normal(k2, (128, 128, 3, 3), dtype=jnp.float32)
        bias = jax.random.normal(k3, (128,), dtype=jnp.float32)
        return {'x': x, 'weight': weight, 'bias': bias}
    _L1_conv_all = _L1_conv_setup()
    _L1_conv_in = {k: v for k, v in _L1_conv_all.items() if k in ('weight', 'bias')}
    del _L1_conv_all

    def _L1_ffn_setup():
        import jax, jax.numpy as jnp
        import numpy as np
        B, N, D = (16, 2048, 128)
        NUM_EXPERTS, TOP_K, HEADS = (4, 2, 4)
        N_EDGES = 524288
        LN_EPS = 1e-05

        def _layernorm(x, g, b):
            mu = x.mean(-1, keepdims=True)
            var = ((x - mu) ** 2).mean(-1, keepdims=True)
            return (x - mu) * jax.lax.rsqrt(var + LN_EPS) * g + b

        def _forward(x, edge_index, W_gat, att_src, att_dst, b_gat, ln_gamma, ln_beta, W1, b1, W2, b2):
            Bc, Nc, Dc = x.shape
            M = Bc * Nc
            x_flat = x.reshape(M, Dc)
            h = (x_flat @ W_gat).reshape(M, HEADS, NUM_EXPERTS)
            loops = jnp.arange(M, dtype=edge_index.dtype)
            src = jnp.concatenate([edge_index[0], loops])
            dst = jnp.concatenate([edge_index[1], loops])
            a_src = (h * att_src).sum(-1)
            a_dst = (h * att_dst).sum(-1)
            e = jax.nn.leaky_relu(a_src[src] + a_dst[dst], negative_slope=0.2)
            e_max = jax.ops.segment_max(e, dst, num_segments=M)
            ee = jnp.exp(e - e_max[dst])
            denom = jax.ops.segment_sum(ee, dst, num_segments=M)
            alpha = ee / (denom[dst] + 1e-16)
            msg = h[src] * alpha[:, :, None]
            agg = jax.ops.segment_sum(msg, dst, num_segments=M).reshape(M, HEADS * NUM_EXPERTS) + b_gat
            scores = _layernorm(agg, ln_gamma, ln_beta).reshape(M, HEADS, NUM_EXPERTS).mean(1)
            scores = scores.reshape(Bc, Nc, NUM_EXPERTS)
            topk_s, topk_i = jax.lax.top_k(scores, TOP_K)
            w = jax.nn.softmax(topk_s, axis=-1)
            out = jnp.zeros_like(x)
            for ei in range(NUM_EXPERTS):
                g = jnp.where(topk_i == ei, w, 0.0).sum(-1)
                hh = jax.nn.gelu(x @ W1[ei] + b1[ei], approximate=False)
                out = out + g[..., None] * (hh @ W2[ei] + b2[ei])
            return out
        key = jax.random.key(seed)
        ks = jax.random.split(key, 8)
        s = 0.05
        return {'x': jax.random.normal(ks[0], (B, N, D), jnp.float32), 'W_gat': jax.random.normal(ks[1], (D, HEADS * NUM_EXPERTS), jnp.float32) * s, 'att_src': jax.random.normal(ks[2], (HEADS, NUM_EXPERTS), jnp.float32) * s, 'att_dst': jax.random.normal(ks[3], (HEADS, NUM_EXPERTS), jnp.float32) * s, 'b_gat': jnp.zeros((HEADS * NUM_EXPERTS,), jnp.float32), 'ln_gamma': jnp.ones((HEADS * NUM_EXPERTS,), jnp.float32), 'ln_beta': jnp.zeros((HEADS * NUM_EXPERTS,), jnp.float32), 'W1': jax.random.normal(ks[4], (NUM_EXPERTS, D, 2 * D), jnp.float32) * s, 'b1': jnp.zeros((NUM_EXPERTS, 2 * D), jnp.float32), 'W2': jax.random.normal(ks[5], (NUM_EXPERTS, 2 * D, D), jnp.float32) * s, 'b2': jnp.zeros((NUM_EXPERTS, D), jnp.float32), 'edge_index': jax.random.randint(ks[6], (2, N_EDGES), 0, B * N, jnp.int32)}
    _L1_ffn_all = _L1_ffn_setup()
    _L1_ffn_in = {k: v for k, v in _L1_ffn_all.items() if k in ('W_gat', 'att_src', 'att_dst', 'b_gat', 'ln_gamma', 'ln_beta', 'W1', 'b1', 'W2', 'b2', 'edge_index')}
    del _L1_ffn_all

    def _L2_conv_setup():
        import jax, jax.numpy as jnp
        import numpy as np
        D_MODEL = 128
        D_STATE = 16
        D_CONV = 4
        D_INNER = 2 * D_MODEL
        DT_RANK = (D_MODEL + 15) // 16
        B, H, W = (2, 32, 32)

        def _mamba(z, W_in, conv_w, conv_b, W_x, W_dt, b_dt, A_log, Dp, W_out):
            Bt = z.shape[0]
            xz = z @ W_in
            xm, gate = jnp.split(xz, 2, axis=-1)
            xc = jnp.transpose(xm, (0, 2, 1))
            xc = jnp.pad(xc, ((0, 0), (0, 0), (D_CONV - 1, 0)))
            xc = jax.lax.conv_general_dilated(xc, conv_w, (1,), 'VALID', dimension_numbers=('NCH', 'OIH', 'NCH'), feature_group_count=D_INNER)
            xc = xc + conv_b[None, :, None]
            xs = jax.nn.silu(jnp.transpose(xc, (0, 2, 1)))
            dbl = xs @ W_x
            dt = jax.nn.softplus(dbl[..., :DT_RANK] @ W_dt + b_dt)
            Bm = dbl[..., DT_RANK:DT_RANK + D_STATE]
            Cm = dbl[..., DT_RANK + D_STATE:]
            A = -jnp.exp(A_log)

            def step(state, ins):
                dt_t, B_t, C_t, x_t = ins
                dA = jnp.exp(dt_t[..., None] * A)
                state = dA * state + (dt_t * x_t)[..., None] * B_t[:, None, :]
                y_t = jnp.einsum('bds,bs->bd', state, C_t)
                return (state, y_t)
            tm = lambda a: jnp.moveaxis(a, 1, 0)
            init = jnp.zeros((Bt, D_INNER, D_STATE), z.dtype)
            _, ys = jax.lax.scan(step, init, (tm(dt), tm(Bm), tm(Cm), tm(xs)))
            y = jnp.moveaxis(ys, 0, 1) + xs * Dp
            y = y * jax.nn.silu(gate)
            return y @ W_out
        key = jax.random.key(seed)
        ks = jax.random.split(key, 8)

        def rnd(k, shape, scale):
            return jax.random.normal(k, shape, jnp.float32) * scale
        A_log = jnp.log(jnp.tile(jnp.arange(1, D_STATE + 1, dtype=jnp.float32), (D_INNER, 1)))
        return {'x': jax.random.normal(ks[0], (B, D_MODEL, H, W), jnp.float32), 'W_in': rnd(ks[1], (D_MODEL, 2 * D_INNER), 0.02), 'conv_w': rnd(ks[2], (D_INNER, 1, D_CONV), 0.1), 'conv_b': jnp.zeros((D_INNER,), jnp.float32), 'W_x': rnd(ks[3], (D_INNER, DT_RANK + 2 * D_STATE), 0.02), 'W_dt': rnd(ks[4], (DT_RANK, D_INNER), 0.02), 'b_dt': rnd(ks[5], (D_INNER,), 0.1), 'A_log': A_log, 'D': jnp.ones((D_INNER,), jnp.float32), 'W_out': rnd(ks[6], (D_INNER, D_MODEL), 0.02)}
    _L2_conv_all = _L2_conv_setup()
    _L2_conv_in = {k: v for k, v in _L2_conv_all.items() if k in ('W_in', 'conv_w', 'conv_b', 'W_x', 'W_dt', 'b_dt', 'A_log', 'D', 'W_out')}
    del _L2_conv_all

    def _L2_ffn_setup():
        import jax, jax.numpy as jnp
        import numpy as np
        NUM_EXPERTS = 8
        TOP_K = 2
        B, S, D = (8, 4096, 128)

        def _moe(tokens, router_w, w1, b1, w2, b2):
            N = tokens.shape[0]
            E = router_w.shape[0]
            logits = tokens.astype(jnp.float32) @ router_w.astype(jnp.float32).T
            probs = jax.nn.softmax(logits, axis=-1)
            rw, re = jax.lax.top_k(probs, TOP_K)
            if TOP_K > 1:
                rw = rw / jnp.maximum(rw.sum(-1, keepdims=True), 1e-12)
            rw = rw.astype(tokens.dtype)
            combine = jnp.zeros((N, E), tokens.dtype).at[jnp.arange(N)[:, None], re].set(rw)
            out = tokens
            for e in range(E):
                h = jax.nn.gelu(tokens @ w1[e] + b1[e], approximate=False)
                y = h @ w2[e] + b2[e]
                out = out + combine[:, e:e + 1] * y
            return out
        key = jax.random.key(seed)
        ks = jax.random.split(key, 4)
        scale = 1.0 / np.sqrt(D).astype(np.float32)
        return {'input_embeddings': jax.random.normal(ks[0], (B, S, D), jnp.float32), 'router_w': jax.random.normal(ks[1], (NUM_EXPERTS, D), jnp.float32) * scale, 'w1': jax.random.normal(ks[2], (NUM_EXPERTS, D, D), jnp.float32) * scale, 'b1': jnp.zeros((NUM_EXPERTS, D), jnp.float32), 'w2': jax.random.normal(ks[3], (NUM_EXPERTS, D, D), jnp.float32) * scale, 'b2': jnp.zeros((NUM_EXPERTS, D), jnp.float32)}
    _L2_ffn_all = _L2_ffn_setup()
    _L2_ffn_in = {k: v for k, v in _L2_ffn_all.items() if k in ('router_w', 'w1', 'b1', 'w2', 'b2')}
    del _L2_ffn_all

    def _L3_conv_setup():
        import jax, jax.numpy as jnp
        import numpy as np
        STRIDE = 1
        PADDING = 1
        DILATION = 1
        key = jax.random.key(seed)
        k1, k2 = jax.random.split(key)
        x = jax.random.normal(k1, (32, 128, 56, 56), dtype=jnp.float32)
        W = jax.random.normal(k2, (128, 128, 3, 3), dtype=jnp.float32) * 0.05
        return {'x': x, 'W': W}
    _L3_conv_all = _L3_conv_setup()
    _L3_conv_in = {k: v for k, v in _L3_conv_all.items() if k in ('W',)}
    del _L3_conv_all

    def _L3_ffn_setup():
        import math
        import jax, jax.numpy as jnp
        import numpy as np
        CAPACITY_FACTOR = 1.25
        key = jax.random.key(seed)
        ks = jax.random.split(key, 5)
        B, L, D, F, E = (8, 4096, 128, 512, 8)
        h = jax.random.normal(ks[0], (B, L, D), dtype=jnp.float32)
        gate_w = jax.random.normal(ks[1], (D, E), dtype=jnp.float32) * 0.02
        gate_b = jnp.zeros((E,), dtype=jnp.float32)
        w1 = jax.random.normal(ks[2], (E, D, F), dtype=jnp.float32) * (1.0 / math.sqrt(D))
        b1 = jnp.zeros((E, F), dtype=jnp.float32)
        w2 = jax.random.normal(ks[3], (E, F, D), dtype=jnp.float32) * (1.0 / math.sqrt(F))
        b2 = jnp.zeros((E, D), dtype=jnp.float32)
        return {'h': h, 'gate_w': gate_w, 'gate_b': gate_b, 'w1': w1, 'b1': b1, 'w2': w2, 'b2': b2}
    _L3_ffn_all = _L3_ffn_setup()
    _L3_ffn_in = {k: v for k, v in _L3_ffn_all.items() if k in ('gate_w', 'gate_b', 'w1', 'b1', 'w2', 'b2')}
    del _L3_ffn_all
    return {'x': x, 'L0_conv_w_off': _L0_conv_in['w_off'], 'L0_conv_b_off': _L0_conv_in['b_off'], 'L0_conv_w_conv': _L0_conv_in['w_conv'], 'L0_ffn_gate_w': _L0_ffn_in['gate_w'], 'L0_ffn_gate_b': _L0_ffn_in['gate_b'], 'L0_ffn_W1': _L0_ffn_in['W1'], 'L0_ffn_b1': _L0_ffn_in['b1'], 'L0_ffn_W2': _L0_ffn_in['W2'], 'L0_ffn_b2': _L0_ffn_in['b2'], 'L1_conv_weight': _L1_conv_in['weight'], 'L1_conv_bias': _L1_conv_in['bias'], 'L1_ffn_W_gat': _L1_ffn_in['W_gat'], 'L1_ffn_att_src': _L1_ffn_in['att_src'], 'L1_ffn_att_dst': _L1_ffn_in['att_dst'], 'L1_ffn_b_gat': _L1_ffn_in['b_gat'], 'L1_ffn_ln_gamma': _L1_ffn_in['ln_gamma'], 'L1_ffn_ln_beta': _L1_ffn_in['ln_beta'], 'L1_ffn_W1': _L1_ffn_in['W1'], 'L1_ffn_b1': _L1_ffn_in['b1'], 'L1_ffn_W2': _L1_ffn_in['W2'], 'L1_ffn_b2': _L1_ffn_in['b2'], 'L1_ffn_edge_index': _L1_ffn_in['edge_index'], 'L2_conv_W_in': _L2_conv_in['W_in'], 'L2_conv_conv_w': _L2_conv_in['conv_w'], 'L2_conv_conv_b': _L2_conv_in['conv_b'], 'L2_conv_W_x': _L2_conv_in['W_x'], 'L2_conv_W_dt': _L2_conv_in['W_dt'], 'L2_conv_b_dt': _L2_conv_in['b_dt'], 'L2_conv_A_log': _L2_conv_in['A_log'], 'L2_conv_D': _L2_conv_in['D'], 'L2_conv_W_out': _L2_conv_in['W_out'], 'L2_ffn_router_w': _L2_ffn_in['router_w'], 'L2_ffn_w1': _L2_ffn_in['w1'], 'L2_ffn_b1': _L2_ffn_in['b1'], 'L2_ffn_w2': _L2_ffn_in['w2'], 'L2_ffn_b2': _L2_ffn_in['b2'], 'L3_conv_W': _L3_conv_in['W'], 'L3_ffn_gate_w': _L3_ffn_in['gate_w'], 'L3_ffn_gate_b': _L3_ffn_in['gate_b'], 'L3_ffn_w1': _L3_ffn_in['w1'], 'L3_ffn_b1': _L3_ffn_in['b1'], 'L3_ffn_w2': _L3_ffn_in['w2'], 'L3_ffn_b2': _L3_ffn_in['b2']}

def reference(x, L0_conv_w_off, L0_conv_b_off, L0_conv_w_conv, L0_ffn_gate_w, L0_ffn_gate_b, L0_ffn_W1, L0_ffn_b1, L0_ffn_W2, L0_ffn_b2, L1_conv_weight, L1_conv_bias, L1_ffn_W_gat, L1_ffn_att_src, L1_ffn_att_dst, L1_ffn_b_gat, L1_ffn_ln_gamma, L1_ffn_ln_beta, L1_ffn_W1, L1_ffn_b1, L1_ffn_W2, L1_ffn_b2, L1_ffn_edge_index, L2_conv_W_in, L2_conv_conv_w, L2_conv_conv_b, L2_conv_W_x, L2_conv_W_dt, L2_conv_b_dt, L2_conv_A_log, L2_conv_D, L2_conv_W_out, L2_ffn_router_w, L2_ffn_w1, L2_ffn_b1, L2_ffn_w2, L2_ffn_b2, L3_conv_W, L3_ffn_gate_w, L3_ffn_gate_b, L3_ffn_w1, L3_ffn_b1, L3_ffn_w2, L3_ffn_b2):
    import jax
    import jax.numpy as jnp

    def _L0_conv_ref(x, w_off, b_off, w_conv):
        import jax, jax.numpy as jnp
        import numpy as np
        B, C, H, W = (8, 128, 32, 32)
        OUT_C = 128
        K = 3
        DG = 1
        CPG = C // DG
        KK = K * K

        def _sample_group(img, py, px):
            Hh, Ww = (img.shape[1], img.shape[2])
            flat = img.reshape(img.shape[0], Hh * Ww)
            y0 = jnp.floor(py)
            x0 = jnp.floor(px)
            wy = py - y0
            wx = px - x0

            def gather(yi, xi):
                valid = ((yi >= 0) & (yi < Hh) & (xi >= 0) & (xi < Ww)).astype(img.dtype)
                idx = (jnp.clip(yi, 0, Hh - 1) * Ww + jnp.clip(xi, 0, Ww - 1)).astype(jnp.int32)
                v = jnp.take(flat, idx.reshape(-1), axis=1).reshape(img.shape[0], *yi.shape)
                return v * valid
            out = gather(y0, x0) * ((1.0 - wy) * (1.0 - wx)) + gather(y0, x0 + 1.0) * ((1.0 - wy) * wx) + gather(y0 + 1.0, x0) * (wy * (1.0 - wx)) + gather(y0 + 1.0, x0 + 1.0) * (wy * wx)
            return jnp.transpose(out, (1, 0, 2, 3))

        def _forward(x, w_off, b_off, w_conv):
            b = x.shape[0]
            pad = K // 2
            out = jax.lax.conv_general_dilated(x, w_off, window_strides=(1, 1), padding=[(pad, pad), (pad, pad)], dimension_numbers=('NCHW', 'OIHW', 'NCHW')) + b_off[None, :, None, None]
            o1, o2, m = jnp.split(out, 3, axis=1)
            dy = o1.reshape(b, DG, KK, H, W)
            dx = o2.reshape(b, DG, KK, H, W)
            mask = jax.nn.sigmoid(m).reshape(b, DG, KK, 1, H, W)
            ys = jnp.arange(H, dtype=x.dtype)[None, None, None, :, None]
            xs = jnp.arange(W, dtype=x.dtype)[None, None, None, None, :]
            py = ys + dy
            px = xs + dx
            xg = x.reshape(b, DG, CPG, H, W)
            sampled = jax.vmap(jax.vmap(_sample_group))(xg, py, px)
            y = sampled * mask
            y = y.reshape(b, C * KK, H, W)
            return jnp.einsum('bkhw,ok->bohw', y, w_conv)
        return _forward(x, w_off, b_off, w_conv)

    def _L0_ffn_ref(x, gate_w, gate_b, W1, b1, W2, b2):
        import jax, jax.numpy as jnp
        import numpy as np
        B, T, D, H, E = (16, 2048, 128, 256, 8)
        Bb, Tt, Dd = x.shape
        Ee = gate_w.shape[1]
        xf = x.reshape(-1, Dd)
        N = xf.shape[0]
        logits = xf @ gate_w + gate_b
        probs = jax.nn.softmax(logits, axis=-1)
        top2_vals, top2_idx = jax.lax.top_k(probs, 2)
        cw = jnp.zeros((N, Ee), dtype=xf.dtype).at[jnp.arange(N)[:, None], top2_idx].add(top2_vals)

        def step(acc, params):
            w1, bb1, w2, bb2, we = params
            h = jax.nn.gelu(xf @ w1 + bb1, approximate=False)
            y = h @ w2 + bb2
            return (acc + we[:, None] * y, None)
        out, _ = jax.lax.scan(step, jnp.zeros_like(xf), (W1, b1, W2, b2, cw.T))
        return out.reshape(Bb, Tt, Dd)

    def _L1_conv_ref(x, weight, bias):
        import jax, jax.numpy as jnp
        import numpy as np
        from jax import lax

        def _affine8bit_dequant(weight):
            min_val = jnp.min(weight)
            max_val = jnp.max(weight)
            scale = (max_val - min_val) / 255.0
            zero_point = jnp.round(jnp.clip(255.0 - max_val / scale, 0.0, 255.0))
            w_q = jnp.round(jnp.clip(zero_point + weight / scale, 0.0, 255.0))
            return scale * (w_q - zero_point)
        w_dq = _affine8bit_dequant(weight)
        out = lax.conv_general_dilated(x, w_dq, window_strides=(1, 1), padding=((1, 1), (1, 1)), lhs_dilation=(1, 1), rhs_dilation=(1, 1), dimension_numbers=('NCHW', 'OIHW', 'NCHW'), feature_group_count=1)
        return out + bias[None, :, None, None]

    def _L1_ffn_ref(x, W_gat, att_src, att_dst, b_gat, ln_gamma, ln_beta, W1, b1, W2, b2, edge_index):
        import jax, jax.numpy as jnp
        import numpy as np
        B, N, D = (16, 2048, 128)
        NUM_EXPERTS, TOP_K, HEADS = (4, 2, 4)
        N_EDGES = 524288
        LN_EPS = 1e-05

        def _layernorm(x, g, b):
            mu = x.mean(-1, keepdims=True)
            var = ((x - mu) ** 2).mean(-1, keepdims=True)
            return (x - mu) * jax.lax.rsqrt(var + LN_EPS) * g + b

        def _forward(x, edge_index, W_gat, att_src, att_dst, b_gat, ln_gamma, ln_beta, W1, b1, W2, b2):
            Bc, Nc, Dc = x.shape
            M = Bc * Nc
            x_flat = x.reshape(M, Dc)
            h = (x_flat @ W_gat).reshape(M, HEADS, NUM_EXPERTS)
            loops = jnp.arange(M, dtype=edge_index.dtype)
            src = jnp.concatenate([edge_index[0], loops])
            dst = jnp.concatenate([edge_index[1], loops])
            a_src = (h * att_src).sum(-1)
            a_dst = (h * att_dst).sum(-1)
            e = jax.nn.leaky_relu(a_src[src] + a_dst[dst], negative_slope=0.2)
            e_max = jax.ops.segment_max(e, dst, num_segments=M)
            ee = jnp.exp(e - e_max[dst])
            denom = jax.ops.segment_sum(ee, dst, num_segments=M)
            alpha = ee / (denom[dst] + 1e-16)
            msg = h[src] * alpha[:, :, None]
            agg = jax.ops.segment_sum(msg, dst, num_segments=M).reshape(M, HEADS * NUM_EXPERTS) + b_gat
            scores = _layernorm(agg, ln_gamma, ln_beta).reshape(M, HEADS, NUM_EXPERTS).mean(1)
            scores = scores.reshape(Bc, Nc, NUM_EXPERTS)
            topk_s, topk_i = jax.lax.top_k(scores, TOP_K)
            w = jax.nn.softmax(topk_s, axis=-1)
            out = jnp.zeros_like(x)
            for ei in range(NUM_EXPERTS):
                g = jnp.where(topk_i == ei, w, 0.0).sum(-1)
                hh = jax.nn.gelu(x @ W1[ei] + b1[ei], approximate=False)
                out = out + g[..., None] * (hh @ W2[ei] + b2[ei])
            return out
        return _forward(x, edge_index, W_gat, att_src, att_dst, b_gat, ln_gamma, ln_beta, W1, b1, W2, b2)

    def _L2_conv_ref(x, W_in, conv_w, conv_b, W_x, W_dt, b_dt, A_log, D, W_out):
        import jax, jax.numpy as jnp
        import numpy as np
        D_MODEL = 128
        D_STATE = 16
        D_CONV = 4
        D_INNER = 2 * D_MODEL
        DT_RANK = (D_MODEL + 15) // 16
        B, H, W = (2, 32, 32)

        def _mamba(z, W_in, conv_w, conv_b, W_x, W_dt, b_dt, A_log, Dp, W_out):
            Bt = z.shape[0]
            xz = z @ W_in
            xm, gate = jnp.split(xz, 2, axis=-1)
            xc = jnp.transpose(xm, (0, 2, 1))
            xc = jnp.pad(xc, ((0, 0), (0, 0), (D_CONV - 1, 0)))
            xc = jax.lax.conv_general_dilated(xc, conv_w, (1,), 'VALID', dimension_numbers=('NCH', 'OIH', 'NCH'), feature_group_count=D_INNER)
            xc = xc + conv_b[None, :, None]
            xs = jax.nn.silu(jnp.transpose(xc, (0, 2, 1)))
            dbl = xs @ W_x
            dt = jax.nn.softplus(dbl[..., :DT_RANK] @ W_dt + b_dt)
            Bm = dbl[..., DT_RANK:DT_RANK + D_STATE]
            Cm = dbl[..., DT_RANK + D_STATE:]
            A = -jnp.exp(A_log)

            def step(state, ins):
                dt_t, B_t, C_t, x_t = ins
                dA = jnp.exp(dt_t[..., None] * A)
                state = dA * state + (dt_t * x_t)[..., None] * B_t[:, None, :]
                y_t = jnp.einsum('bds,bs->bd', state, C_t)
                return (state, y_t)
            tm = lambda a: jnp.moveaxis(a, 1, 0)
            init = jnp.zeros((Bt, D_INNER, D_STATE), z.dtype)
            _, ys = jax.lax.scan(step, init, (tm(dt), tm(Bm), tm(Cm), tm(xs)))
            y = jnp.moveaxis(ys, 0, 1) + xs * Dp
            y = y * jax.nn.silu(gate)
            return y @ W_out
        b, c, h, w = x.shape
        l = h * w
        zs = jnp.stack([x, jnp.flip(x, 3), jnp.flip(x, 2), jnp.flip(x, (2, 3))], axis=0)
        zs = zs.reshape(4 * b, c, l).transpose(0, 2, 1)
        y = _mamba(zs, W_in, conv_w, conv_b, W_x, W_dt, b_dt, A_log, D, W_out)
        y = y.transpose(0, 2, 1).reshape(4, b, c, h, w)
        y0 = y[0]
        y1 = jnp.flip(y[1], 3)
        y2 = jnp.flip(y[2], 2)
        y3 = jnp.flip(y[3], (2, 3))
        return (y0 + y1 + y2 + y3) / 4.0

    def _L2_ffn_ref(input_embeddings, router_w, w1, b1, w2, b2):
        import jax, jax.numpy as jnp
        import numpy as np
        NUM_EXPERTS = 8
        TOP_K = 2
        B, S, D = (8, 4096, 128)

        def _moe(tokens, router_w, w1, b1, w2, b2):
            N = tokens.shape[0]
            E = router_w.shape[0]
            logits = tokens.astype(jnp.float32) @ router_w.astype(jnp.float32).T
            probs = jax.nn.softmax(logits, axis=-1)
            rw, re = jax.lax.top_k(probs, TOP_K)
            if TOP_K > 1:
                rw = rw / jnp.maximum(rw.sum(-1, keepdims=True), 1e-12)
            rw = rw.astype(tokens.dtype)
            combine = jnp.zeros((N, E), tokens.dtype).at[jnp.arange(N)[:, None], re].set(rw)
            out = tokens
            for e in range(E):
                h = jax.nn.gelu(tokens @ w1[e] + b1[e], approximate=False)
                y = h @ w2[e] + b2[e]
                out = out + combine[:, e:e + 1] * y
            return out
        b, s, d = input_embeddings.shape
        tokens = input_embeddings.reshape(b * s, d)
        return _moe(tokens, router_w, w1, b1, w2, b2).reshape(b, s, d)

    def _L3_conv_ref(x, W):
        import jax, jax.numpy as jnp
        import numpy as np
        STRIDE = 1
        PADDING = 1
        DILATION = 1
        out = jax.lax.conv_general_dilated(x, W, window_strides=(STRIDE, STRIDE), padding=[(PADDING, PADDING), (PADDING, PADDING)], rhs_dilation=(DILATION, DILATION), dimension_numbers=('NCHW', 'OIHW', 'NCHW'))
        return out

    def _L3_ffn_ref(h, gate_w, gate_b, w1, b1, w2, b2):
        import math
        import jax, jax.numpy as jnp
        import numpy as np
        CAPACITY_FACTOR = 1.25
        B, L, D = h.shape
        E = gate_w.shape[1]
        T = B * L
        C = max(1, math.ceil(CAPACITY_FACTOR * T / E))
        x = h.reshape(T, D)
        logits = x @ gate_w + gate_b
        probs = jax.nn.softmax(logits, axis=-1)
        idx = jnp.argmax(probs, axis=-1)
        prb = jnp.take_along_axis(probs, idx[:, None], axis=1)[:, 0]
        one_hot = jax.nn.one_hot(idx, E, dtype=jnp.float32)
        pos = (jnp.cumsum(one_hot, axis=0) * one_hot).sum(-1).astype(jnp.int32) - 1
        kept = pos < C
        pos_safe = jnp.where(kept, pos, C)
        buf = jnp.zeros((E, C, D), dtype=h.dtype).at[idx, pos_safe].set(x, mode='drop')
        hmid = jax.nn.relu(jnp.einsum('ecd,edf->ecf', buf, w1) + b1[:, None, :])
        ybuf = jnp.einsum('ecf,efd->ecd', hmid, w2) + b2[:, None, :]
        pos_g = jnp.minimum(pos, C - 1)
        y_tok = ybuf[idx, pos_g] * (prb * kept)[:, None]
        y = y_tok.reshape(B, L, D)
        y = jnp.nan_to_num(y, nan=0.0, posinf=10000.0, neginf=-10000.0)
        return y

    def _gn(v, G=32, eps=1e-05):
        B_, C_, H_, W_ = v.shape
        g = v.reshape(B_, G, C_ // G, H_, W_)
        m = jnp.mean(g, axis=(2, 3, 4), keepdims=True)
        s = jnp.var(g, axis=(2, 3, 4), keepdims=True)
        return ((g - m) / jnp.sqrt(s + eps)).reshape(v.shape)

    def _ln_c(v, eps=1e-06):
        m = jnp.mean(v, axis=1, keepdims=True)
        s = jnp.var(v, axis=1, keepdims=True)
        return (v - m) / jnp.sqrt(s + eps)

    def _ln_t(v, eps=1e-05):
        m = jnp.mean(v, axis=-1, keepdims=True)
        s = jnp.var(v, axis=-1, keepdims=True)
        return (v - m) / jnp.sqrt(s + eps)

    def _to_tokens(v):
        B_, C_, H_, W_ = v.shape
        return v.reshape(B_, C_, H_ * W_).transpose(0, 2, 1)

    def _from_tokens(t, like):
        B_, C_, H_, W_ = like.shape
        return t.transpose(0, 2, 1).reshape(B_, C_, H_, W_)
    x = x + _L0_conv_ref(_ln_c(x), L0_conv_w_off, L0_conv_b_off, L0_conv_w_conv)
    t = _to_tokens(x)
    t = t + _L0_ffn_ref(_ln_t(t), L0_ffn_gate_w, L0_ffn_gate_b, L0_ffn_W1, L0_ffn_b1, L0_ffn_W2, L0_ffn_b2)
    x = _from_tokens(t, x)
    x = x + _L1_conv_ref(_ln_c(x), L1_conv_weight, L1_conv_bias)
    t = _to_tokens(x)
    t = t + _L1_ffn_ref(_ln_t(t), L1_ffn_W_gat, L1_ffn_att_src, L1_ffn_att_dst, L1_ffn_b_gat, L1_ffn_ln_gamma, L1_ffn_ln_beta, L1_ffn_W1, L1_ffn_b1, L1_ffn_W2, L1_ffn_b2, L1_ffn_edge_index)
    x = _from_tokens(t, x)
    x = x + _L2_conv_ref(_ln_c(x), L2_conv_W_in, L2_conv_conv_w, L2_conv_conv_b, L2_conv_W_x, L2_conv_W_dt, L2_conv_b_dt, L2_conv_A_log, L2_conv_D, L2_conv_W_out)
    t = _to_tokens(x)
    t = t + _L2_ffn_ref(_ln_t(t), L2_ffn_router_w, L2_ffn_w1, L2_ffn_b1, L2_ffn_w2, L2_ffn_b2)
    x = _from_tokens(t, x)
    x = x + _L3_conv_ref(_ln_c(x), L3_conv_W)
    t = _to_tokens(x)
    t = t + _L3_ffn_ref(_ln_t(t), L3_ffn_gate_w, L3_ffn_gate_b, L3_ffn_w1, L3_ffn_b1, L3_ffn_w2, L3_ffn_b2)
    x = _from_tokens(t, x)
    return x

_drawn_inputs = setup_inputs


def setup_inputs(seed=0):
    import zlib

    import numpy as np

    out = dict(_drawn_inputs(seed))
    spreads = {'L0_conv_b_off': (0.0, 0.1),
     'L0_ffn_gate_b': (0.0, 0.499),
     'L0_ffn_b1': (0.0, 0.8),
     'L0_ffn_b2': (0.0, 0.368),
     'L1_ffn_b_gat': (0.0, 0.8),
     'L1_ffn_ln_gamma': (1.0, 0.6),
     'L1_ffn_ln_beta': (0.0, 0.8),
     'L1_ffn_b1': (0.0, 0.8),
     'L1_ffn_b2': (0.0, 0.8),
     'L2_conv_conv_b': (0.0, 0.8),
     'L2_conv_D': (1.0, 0.6),
     'L2_ffn_b1': (0.0, 2.0),
     'L2_ffn_b2': (0.0, 2.0),
     'L3_ffn_gate_b': (0.0, 2.0),
     'L3_ffn_b1': (0.0, 2.0),
     'L3_ffn_b2': (0.0, 2.0)}
    factors = {'L0_ffn_gate_w': 2.89,
     'L0_ffn_W1': 6.67,
     'L0_ffn_W2': 6.036,
     'L1_ffn_W_gat': 8.0,
     'L1_ffn_att_src': 8.0,
     'L1_ffn_att_dst': 8.0,
     'L1_ffn_W1': 8.0,
     'L1_ffn_W2': 8.0,
     'L2_conv_W_in': 8.0,
     'L2_conv_conv_w': 8.0,
     'L2_conv_W_x': 8.0,
     'L2_conv_W_dt': 8.0,
     'L2_conv_b_dt': 8.0,
     'L2_conv_A_log': 8.0,
     'L2_conv_W_out': 8.0,
     'L2_ffn_router_w': 28.971,
     'L2_ffn_w1': 33.016,
     'L2_ffn_w2': 25.201,
     'L3_ffn_gate_w': 24.828,
     'L3_ffn_w1': 28.048,
     'L3_ffn_w2': 22.94,
     'L3_conv_W': 8.0}
    for name, (base, spread) in spreads.items():
        noise = np.random.default_rng([zlib.crc32(name.encode()), seed]).standard_normal(out[name].shape)
        drawn = base * np.exp(spread * noise) if base else spread * noise
        out[name] = jnp.asarray(drawn.astype(out[name].dtype))
    for name, factor in factors.items():
        out[name] = (out[name] * factor).astype(out[name].dtype)
    return out
```

```python
from contextlib import ExitStack

import numpy as np

import concourse.bass as bass
from concourse import mybir

FP32 = mybir.dt.float32
I32 = mybir.dt.int32
U32 = mybir.dt.uint32
BF16 = mybir.dt.bfloat16
ALU = mybir.AluOpType
ACT = mybir.ActivationFunctionType
AX = mybir.AxisListType

P = 128
IMAGES, SIDE = 8, 32
POS = SIDE * SIDE
TOKENS = IMAGES * POS
BLK = 512
BLOCKS = TOKENS // BLK
TILES = TOKENS // P
PADDED = SIDE + 2
TAPS = 9
HUGE = 1.0e30


class Link:

    def __init__(self, eng, sem, base=0, apart=False):
        self.eng, self.sem, self.base, self.n, self.apart = eng, sem, base, 0, apart

    def __call__(self, ins):
        self.n += 1
        ins.then_inc(self.sem, 1)
        self.eng.wait_ge(self.sem, self.base + self.n)
        if self.apart:
            self.eng.nop(nofuse=True)


class Core:

    def __init__(self, nc, a, ctx):
        self.nc, self.a, self.ctx, self.sems = nc, a, ctx, []
        self.x = ctx.enter_context(nc.sbuf_tensor("x_act", [P, TOKENS], FP32))
        self.pad = ctx.enter_context(nc.sbuf_tensor("normed", [P, IMAGES * PADDED * PADDED], FP32))
        self.ident = ctx.enter_context(nc.sbuf_tensor("identity", [P, P], FP32))
        self.ones = ctx.enter_context(nc.sbuf_tensor("ones_row", [1, P], FP32))
        self.mean = ctx.enter_context(nc.sbuf_tensor("mean_matrix", [P, P], FP32))
        self.scores = ctx.enter_context(nc.sbuf_tensor("scores", [P, TILES, 4], FP32))
        self.pair = [ctx.enter_context(nc.psum_tensor(f"banks{i}", [P, 2 * BLK], FP32)) for i in range(4)]
        self.bank = [self.pair[i // 2][:, (i % 2) * BLK:(i % 2 + 1) * BLK] for i in range(8)]

    def sem(self, name):
        self.sems.append(self.nc.alloc_semaphore(name=name))
        return self.sems[-1]

    def release(self):
        self.nc.clear_and_free_semaphores(self.sems)
        self.nc.all_engine_barrier()
        self.sems = []

    def image(self, b):
        return self.pad[:, :].rearrange("p (b y x) -> p b y x", b=IMAGES, y=PADDED)[:, b, :, :]


def start(K):
    nc, a = K.nc, K.a
    x_in, const = K.sem("x_in"), K.sem("constants_in")
    with nc.Block() as block:
        @block.sync
        def _(sp):
            for b in range(IMAGES):
                sp.dma_start(K.x[:, b * POS:(b + 1) * POS], a["x"][b].rearrange("c y x -> c (y x)")).then_inc(x_in, 16)
            sp.dma_start(K.ident[:, :], a["identity"]).then_inc(const, 16)
            sp.wait_ge(x_in, 16 * IMAGES)
            sp.wait_ge(const, 16)

        @block.vector
        def _(dve):
            dve.memset(K.mean[:, :], 1.0 / P)
            dve.memset(K.ones[:, :], 1.0)


def finish(K):
    nc, a = K.nc, K.a
    stored = K.sem("stored")
    with nc.Block() as block:
        @block.sync
        def _(sp):
            for b in range(IMAGES):
                sp.dma_start(a["out"][b].rearrange("c y x -> c (y x)"), K.x[:, b * POS:(b + 1) * POS]).then_inc(stored, 16)
            sp.wait_ge(stored, 16 * IMAGES)


def layernorm(K, tag, eps, padded):
    nc = K.nc
    sem = lambda name: K.sem(f"{tag}_{name}")
    mean_ready, centred, squared, var_ready, row_ready = sem("mean_ready"), sem("centred"), sem("squared"), sem("var_ready"), sem("row_ready")
    dealt, rooted, inverted, gathered, spread, normed, zeroed = (
        sem("dealt"), sem("rooted"), sem("inverted"), sem("gathered"), sem("spread"), sem("normed"), sem("zeroed"))

    def view(i, h):
        if padded:
            return K.image(i)[:, 1 + 16 * h:17 + 16 * h, 1:1 + SIDE]
        return K.pad[:, bass.ds(i * POS + h * BLK, BLK)]

    def grid(t):
        return t.rearrange("p (y x) -> p y x", x=SIDE) if padded else t

    with ExitStack() as ctx:
        sq = [ctx.enter_context(nc.sbuf_tensor(f"{tag}_sq{h}", [P, BLK], FP32)) for h in range(2)]
        row = ctx.enter_context(nc.sbuf_tensor(f"{tag}_row", [1, TOKENS], FP32))
        deal = ctx.enter_context(nc.sbuf_tensor(f"{tag}_deal", [P, TILES + 1], FP32))
        mean, var, scale = K.bank[0:2], K.bank[2:4], K.bank[4:6]
        with nc.Block() as block:
            @block.sync
            def _(sp):
                sp.wait_ge(row_ready, BLOCKS)
                sp.dma_start(deal[:, 0:TILES], row[:, :].rearrange("o (p t) -> o p t", p=P)).then_inc(dealt, 16)
                sp.wait_ge(inverted, 1)
                sp.dma_start(row[:, :].rearrange("o (p t) -> o p t", p=P), deal[:, 0:TILES]).then_inc(gathered, 16)

            @block.tensor
            def _(pe):
                with pe.Fori(0, IMAGES) as i:
                    for h in range(2):
                        pe.matmul(mean[h][:, :], K.mean[:, :], K.x[:, bass.ds(i * POS + h * BLK, BLK)], start=True, stop=True).then_inc(mean_ready, 1)
                    for h in range(2):
                        pe.wait_ge(squared, i * 2 + h + 1)
                        pe.matmul(var[h][0:1, :], K.mean[:, 0:1], sq[h][:, :], start=True, stop=True).then_inc(var_ready, 1)
                pe.wait_ge(gathered, 16)
                with pe.Fori(0, IMAGES) as i:
                    for h in range(2):
                        pe.wait_ge(normed, i * 2 + h + 1)
                        pe.nop()
                        pe.matmul(scale[h][:, :], K.ones[0:1, :], row[:, bass.ds(i * POS + h * BLK, BLK)], start=True, stop=True).then_inc(spread, 1)

            @block.scalar
            def _(act):
                with act.Fori(0, IMAGES) as i:
                    for h in range(2):
                        act.wait_ge(centred, i * 2 + h + 1)
                        act.activation(grid(sq[h][:, :]), view(i, h), ACT.Square).then_inc(squared, 1)
                    for h in range(2):
                        act.wait_ge(var_ready, i * 2 + h + 1)
                        act.activation(row[:, bass.ds(i * POS + h * BLK, BLK)], var[h][0:1, :], ACT.Copy).then_inc(row_ready, 1)
                act.wait_ge(dealt, 16)
                act.wait_ge(zeroed, 1)
                act.activation(deal[:, 0:TILES], deal[:, 0:TILES], ACT.Sqrt, bias=deal[:, TILES:TILES + 1]).then_inc(rooted, 1)

            @block.vector
            def _(dve):
                dve.memset(deal[:, TILES:TILES + 1], eps).then_inc(zeroed, 1)
                if padded:
                    dve.memset(K.pad[:, :], 0.0).then_inc(zeroed, 1)
                    dve.wait_ge(zeroed, 2)
                dve.sem_inc(normed, 2)
                with dve.Fori(0, IMAGES) as i:
                    for h in range(2):
                        dve.wait_ge(mean_ready, i * 2 + h + 1)
                        dve.tensor_tensor(view(i, h), grid(K.x[:, bass.ds(i * POS + h * BLK, BLK)]), grid(mean[h][:, :]), ALU.subtract).then_inc(centred, 1)
                dve.wait_ge(rooted, 1)
                dve.reciprocal(deal[:, 0:TILES], deal[:, 0:TILES]).then_inc(inverted, 1)
                with dve.Fori(0, IMAGES) as i:
                    for h in range(2):
                        dve.wait_ge(spread, i * 2 + h + 1)
                        dve.tensor_tensor(view(i, h), view(i, h), grid(scale[h][:, :]), ALU.mult).then_inc(normed, 1)


def conv_taps(pe, K, i, h, out, weights):
    for t in range(TAPS):
        ky, kx = t // 3, t % 3
        rhs = K.image(i)[:, 16 * h + ky:16 * h + ky + 16, kx:kx + SIDE]
        last = pe.matmul(out, weights[:, t, :], rhs, start=(t == 0), stop=(t == TAPS - 1))
    return last


def conv_residual(K, tag, weight, bias=None):
    nc = K.nc
    loaded, w_ready, conv_done, added = K.sem(tag + "_w_loaded"), K.sem(tag + "_w_ready"), K.sem(tag + "_conv_done"), K.sem(tag + "_added")
    chain = K.sem(tag + "_chain")
    extreme, reduced = K.sem(tag + "_extreme"), K.sem(tag + "_reduced")
    with ExitStack() as ctx:
        w = ctx.enter_context(nc.sbuf_tensor(tag + "_w", [P, TAPS, P], FP32))
        bt = ctx.enter_context(nc.sbuf_tensor(tag + "_bias", [P, 1], FP32))
        s = ctx.enter_context(nc.sbuf_tensor(tag + "_scales", [P, 8], FP32))
        acc = K.bank[0:2]
        with nc.Block() as block:
            @block.sync
            def _(sp):
                sp.dma_start(w[:, :, :], weight).then_inc(loaded, 16)
                if bias is not None:
                    sp.dma_start(bt[:, :], bias).then_inc(loaded, 16)

            @block.gpsimd
            def _(pool):
                if bias is not None:
                    pool.wait_ge(extreme, 1)
                    pool.partition_all_reduce(s[:, 2:4], s[:, 0:2], P, bass.bass_isa.ReduceOp.max).then_inc(reduced, 1)

            @block.tensor
            def _(pe):
                pe.wait_ge(w_ready, 1)
                with pe.Fori(0, IMAGES) as i:
                    for h in range(2):
                        pe.wait_ge(added, i * 2 + h + 1)
                        conv_taps(pe, K, i, h, acc[h][:, :], w).then_inc(conv_done, 1)

            @block.vector
            def _(dve):
                dve.wait_ge(loaded, 16 if bias is None else 32)
                if bias is None:
                    dve.memset(bt[:, :], 0.0).then_inc(w_ready, 1)
                    dve.wait_ge(w_ready, 1)
                else:
                    link = Link(dve, chain)
                    flat = w[:, :, :].rearrange("p t o -> p (t o)")
                    link(dve.tensor_reduce(s[:, 0:1], flat, AX.X, ALU.max))
                    link(dve.tensor_reduce(s[:, 1:2], flat, AX.X, ALU.min))
                    dve.tensor_scalar(s[:, 1:2], s[:, 1:2], -1.0, None, ALU.mult).then_inc(extreme, 1)
                    dve.wait_ge(reduced, 1)
                    magic = 12582912.0
                    link(dve.tensor_tensor(s[:, 4:5], s[:, 2:3], s[:, 3:4], ALU.add))
                    link(dve.tensor_scalar(s[:, 4:5], s[:, 4:5], 1.0 / 255.0, None, ALU.mult))
                    link(dve.reciprocal(s[:, 6:7], s[:, 4:5]))
                    link(dve.tensor_tensor(s[:, 5:6], s[:, 2:3], s[:, 6:7], ALU.mult))
                    link(dve.tensor_scalar(s[:, 5:6], s[:, 5:6], -1.0, 255.0, ALU.mult, ALU.add))
                    link(dve.tensor_scalar(s[:, 5:6], s[:, 5:6], 0.0, 255.0, ALU.max, ALU.min))
                    link(dve.tensor_scalar(s[:, 5:6], s[:, 5:6], magic, -magic, ALU.add, ALU.add))
                    link(dve.tensor_scalar(flat, flat, s[:, 6:7], s[:, 5:6], ALU.mult, ALU.add))
                    link(dve.tensor_scalar(flat, flat, 0.0, 255.0, ALU.max, ALU.min))
                    link(dve.tensor_scalar(flat, flat, magic, -magic, ALU.add, ALU.add))
                    dve.tensor_scalar(flat, flat, s[:, 5:6], s[:, 4:5], ALU.subtract, ALU.mult).then_inc(w_ready, 1)
                dve.sem_inc(added, 2)
                with dve.Fori(0, IMAGES) as i:
                    for h in range(2):
                        dve.wait_ge(conv_done, i * 2 + h + 1)
                        blk = K.x[:, bass.ds(i * POS + h * BLK, BLK)]
                        dve.scalar_tensor_tensor(blk, acc[h][:, :], bt[:, 0:1], blk, ALU.add, ALU.add).then_inc(added, 1)


MASK_ROWS, DY_ROWS, DX_ROWS, OFF_ROWS = 0, 32, 64, 96
CHUNKS = POS // P


def deformable(K, tag):
    nc, a = K.nc, K.a
    sem = lambda name: K.sem(f"{tag}_{name}")
    STEPS = 2 * TAPS
    ZS = 3
    ZW = TAPS * P // ZS
    ZN = CHUNKS * ZS
    loaded = sem("loaded")
    img_ready, off_made, off_ready, sig_ready = sem("img_ready"), sem("off_made"), sem("off_ready"), sem("sig_ready")
    z_made, z_copied = sem("z_made"), sem("z_copied")
    bc_ready, ax_ready, abs_done, masked = sem("bc_ready"), sem("ax_ready"), sem("abs_done"), sem("masked")
    b_ready, used, added, chain = sem("b_ready"), sem("used"), sem("added"), sem("chain")
    with ExitStack() as ctx:
        sb = lambda n, shape: ctx.enter_context(nc.sbuf_tensor(f"{tag}_{n}", shape, FP32))
        w_off, w_conv = sb("w_off", [P, TAPS, OFF_ROWS]), sb("w_conv", [P, TAPS * P])
        b_off, base = sb("b_off", [OFF_ROWS, 1]), sb("base", [OFF_ROWS, POS])
        neg_qy, neg_qx = sb("neg_qy", [P, CHUNKS]), sb("neg_qx", [P, 1])
        img, off, z = sb("img", [P, POS]), sb("off", [OFF_ROWS, POS]), sb("z", [P, CHUNKS, TAPS * P])
        hats = [sb(f"hats{j}", [P, CHUNKS, BLK]) for j in range(2)]
        hx = [sb(f"hx{j}", [P, BLK]) for j in range(2)]
        hxm = [sb(f"hxm{j}", [P, BLK]) for j in range(2)]
        acc, dy_bank, dx_bank, m_bank = K.bank[0:2], K.bank[2:4], K.bank[4:6], K.bank[6]
        off_bank = [K.bank[7], K.bank[6]]
        z_bank = K.bank[2:6]
        with nc.Block() as block:
            @block.sync
            def _(sp):
                for to, src in ((w_off, "L0_conv_w_off"), (w_conv, "L0_conv_w_conv")):
                    sp.dma_start(to[:, :, :] if to is w_off else to[:, :], a[src]).then_inc(loaded, 16)
                for to, src in ((b_off, "L0_conv_b_off"), (base, "position_rows"), (neg_qy, "neg_qy"), (neg_qx, "neg_qx")):
                    sp.dma_start(to[:, :], a[src]).then_inc(loaded, 16)

            @block.tensor
            def _(pe):
                pe.wait_ge(loaded, 96)
                pe.sem_inc(used, 2)
                with pe.Fori(0, IMAGES) as i:
                    pe.wait_ge(abs_done, i * STEPS + 2)
                    pe.wait_ge(masked, i * STEPS)
                    pe.nop()
                    for h in range(2):
                        for t in range(TAPS):
                            rhs = K.image(i)[:, 16 * h + t // 3:16 * h + t // 3 + 16, t % 3:t % 3 + SIDE]
                            last = pe.matmul(off_bank[h][0:OFF_ROWS, :], w_off[:, t, :], rhs, start=(t == 0), stop=(t == TAPS - 1))
                        last.then_inc(off_made, 1)
                    pe.wait_ge(img_ready, i + 1)
                    for k in range(ZN):
                        if k >= 4:
                            pe.wait_ge(z_copied, i * ZN + k - 3)
                        c, j = k // ZS, k % ZS
                        pe.matmul(z_bank[k % 4][:, 0:ZW], img[:, c * P:(c + 1) * P], w_conv[:, j * ZW:(j + 1) * ZW], start=True, stop=True).then_inc(z_made, 1)
                    pe.wait_ge(z_copied, (i + 1) * ZN)
                    pe.wait_ge(sig_ready, i + 1)
                    for s in range(STEPS + 1):
                        if s < STEPS:
                            h, t = s // TAPS, s % TAPS
                            cols = slice(h * BLK, (h + 1) * BLK)
                            pe.wait_ge(abs_done, i * STEPS + s + 1)
                            pe.wait_ge(masked, i * STEPS + s)
                            for row, bank in ((DX_ROWS, dx_bank[s % 2]), (MASK_ROWS, m_bank), (DY_ROWS, dy_bank[s % 2])):
                                last = pe.matmul(bank[:, :], K.ident[0:OFF_ROWS, row + t:row + t + 1].broadcast_to([OFF_ROWS, P]), off[:, cols], start=True, stop=True)
                            last.then_inc(bc_ready, 1)
                        if s >= 1:
                            m = s - 1
                            h, t = m // TAPS, m % TAPS
                            if t == 0:
                                pe.wait_ge(added, i * 2 + h + 1)
                            pe.wait_ge(b_ready, i * STEPS + m + 1)
                            for c in range(CHUNKS):
                                last = pe.matmul(acc[h][:, :], z[:, c, t * P:(t + 1) * P], hats[m % 2][:, c, :], start=(t == 0 and c == 0), stop=(t == TAPS - 1 and c == CHUNKS - 1))
                            last.then_inc(used, 1)

            @block.scalar
            def _(act):
                act.wait_ge(loaded, 96)
                act.sem_inc(abs_done, 2)
                with act.Fori(0, IMAGES) as i:
                    for k in range(ZN):
                        c, j = k // ZS, k % ZS
                        act.wait_ge(z_made, i * ZN + k + 1)
                        act.copy(z[:, c, j * ZW:(j + 1) * ZW], z_bank[k % 4][:, 0:ZW]).then_inc(z_copied, 1)
                    act.wait_ge(off_ready, i * 2 + 2)
                    act.activation(off[MASK_ROWS:MASK_ROWS + TAPS, :], off[MASK_ROWS:MASK_ROWS + TAPS, :], ACT.Sigmoid).then_inc(sig_ready, 1)
                    for s in range(STEPS):
                        act.wait_ge(bc_ready, i * STEPS + s + 1)
                        act.wait_ge(used, i * STEPS + s + 1)
                        act.activation(hx[s % 2][:, :], dx_bank[s % 2][:, :], ACT.Abs, bias=neg_qx[:, 0:1]).then_inc(ax_ready, 1)
                        for c in range(CHUNKS):
                            last = act.activation(hats[s % 2][:, c, :], dy_bank[s % 2][:, :], ACT.Abs, bias=neg_qy[:, c:c + 1])
                        last.then_inc(abs_done, 1)

            @block.vector
            def _(dve):
                dve.wait_ge(loaded, 96)
                dve.sem_inc(added, 2)

                def residual(i, h):
                    dve.wait_ge(used, i * STEPS + (h + 1) * TAPS + 2)
                    blk = K.x[:, bass.ds(i * POS + h * BLK, BLK)]
                    dve.tensor_tensor(blk, blk, acc[h][:, :], ALU.add).then_inc(added, 1)

                with dve.Fori(0, IMAGES) as i:
                    link = Link(dve, chain, i * 2 * STEPS)
                    dve.tensor_copy(img[:, :].rearrange("p (y x) -> p y x", x=SIDE), K.image(i)[:, 1:1 + SIDE, 1:1 + SIDE]).then_inc(img_ready, 1)
                    for h in range(2):
                        cols = slice(h * BLK, (h + 1) * BLK)
                        dve.wait_ge(off_made, i * 2 + h + 1)
                        dve.scalar_tensor_tensor(off[:, cols], off_bank[h][0:OFF_ROWS, :], b_off[:, 0:1], base[:, cols], ALU.add, ALU.add).then_inc(off_ready, 1)
                    for s in range(STEPS):
                        j = s % 2
                        dve.wait_ge(ax_ready, i * STEPS + s + 1)
                        link(dve.tensor_scalar(hx[j][:, :], hx[j][:, :], -1.0, 0.0, ALU.add, ALU.min))
                        dve.wait_ge(b_ready, i * STEPS + s)
                        dve.tensor_tensor(hxm[j][:, :], hx[j][:, :], m_bank[:, :], ALU.mult).then_inc(masked, 1)
                        dve.wait_ge(masked, i * STEPS + s + 1)
                        dve.wait_ge(abs_done, i * STEPS + s + 3)
                        link(dve.tensor_scalar(hats[j][:, :, :], hats[j][:, :, :], -1.0, 0.0, ALU.add, ALU.min))
                        dve.tensor_tensor(hats[j][:, :, :], hats[j][:, :, :], hxm[j][:, :].unsqueeze(1).broadcast_to([P, CHUNKS, BLK]), ALU.mult).then_inc(b_ready, 1)
                        if s == TAPS:
                            residual(i, 0)
                    residual(i, 1)


def first_match(dve, link, hot, v, top, idx, tmp, m):
    n = v.shape[2]
    wide = lambda t: t.unsqueeze(2).broadcast_to([P, v.shape[1], n])
    link(dve.tensor_tensor(tmp, v, wide(top), ALU.is_equal))
    link(dve.tensor_tensor(tmp, tmp, idx, ALU.mult))
    link(dve.tensor_reduce(m, tmp, AX.X, ALU.min))
    link(dve.tensor_tensor(hot, idx, wide(m), ALU.is_equal))


def moe(K, tag, E, F, kind, names):
    nc, a = K.nc, K.a
    C = F // P
    STEPS = E * C
    w1d, b1d, w2d, b2d, gwd, gbd = [a[n] if n else None for n in names]
    s = lambda n: K.sem(f"{tag}_{n}")
    loaded = s("loaded")
    with ExitStack() as ctx:
        sb = lambda n, shape, dt=FP32: ctx.enter_context(nc.sbuf_tensor(f"{tag}_{n}", shape, dt))
        gT = sb("gT", [E, TOKENS])
        L = sb("L", [P, TILES, E])
        with ExitStack() as inner:
            sc = lambda n, shape: inner.enter_context(nc.sbuf_tensor(f"{tag}_{n}", shape, FP32))
            gw, gb = sc("gw", [P, E]), sc("gb", [P, E])
            idx, tmp, hot1, hot2, p, p2 = [sc(n, [P, TILES, E]) for n in ("idx", "tmp", "hot1", "hot2", "p", "p2")]
            m, m1, m2, den = [sc(n, [P, TILES]) for n in ("m", "m1", "m2", "den")]
            hotT = sc("hotT", [E, TOKENS]) if kind == "first" else None
            zero = sc("zero", [E, 1]) if kind == "first" else None
            logits, shifted, exped, chain = s("logits"), s("shifted"), s("exped"), s("chain")
            gated, turned, copied, idx_in = s("gated"), s("turned"), s("copied"), s("idx_in")
            wide = lambda t: t[:, :].unsqueeze(2).broadcast_to([P, TILES, E])
            turns = [(L, gT)] + ([(hot1, hotT)] if kind == "first" else [])
            with nc.Block() as block:
                @block.sync
                def _(sp):
                    if kind != "given":
                        sp.dma_start(gw[:, :], gwd).then_inc(loaded, 16)
                    sp.dma_start(idx[:, :, :], a[f"index{E}"]).then_inc(idx_in, 16)
                    if gbd is not None:
                        sp.dma_start(gb[:, :], gbd).then_inc(idx_in, 16)

                @block.tensor
                def _(pe):
                    if kind != "given":
                        pe.wait_ge(loaded, 16)
                        for t in range(TILES):
                            last = pe.matmul(K.bank[0][:, t * E:(t + 1) * E], K.pad[:, t * P:(t + 1) * P], gw[:, :], start=True, stop=True)
                        last.then_inc(logits, 1)
                    pe.wait_ge(gated, 1)
                    n = 0
                    for src, _ in turns:
                        for g in range(BLOCKS):
                            if n >= 2:
                                pe.wait_ge(copied, n - 1)
                            for t in range(4):
                                last = pe.transpose(K.bank[1 + n % 2][0:E, t * P:(t + 1) * P], src[:, 4 * g + t, :], K.ident[:, :])
                            last.then_inc(turned, 1)
                            n += 1

                @block.scalar
                def _(act):
                    act.wait_ge(shifted, 1)
                    act.activation(p[:, :, :], tmp[:, :, :], ACT.Exp).then_inc(exped, 1)
                    n = 0
                    for _, dst in turns:
                        for g in range(BLOCKS):
                            act.wait_ge(turned, n + 1)
                            act.copy(dst[:, g * BLK:(g + 1) * BLK], K.bank[1 + n % 2][0:E, :]).then_inc(copied, 1)
                            n += 1

                @block.vector
                def _(dve):
                    link = Link(dve, chain)
                    v3 = lambda t: t[:, :, :]
                    dve.wait_ge(idx_in, 32 if gbd is not None else 16)
                    if kind == "given":
                        link(dve.tensor_copy(v3(L), K.scores[:, :, :]))
                        link(dve.tensor_reduce(m1[:, :], v3(L), AX.X, ALU.max))
                        first_match(dve, link, v3(hot1), v3(L), m1[:, :], v3(idx), v3(tmp), m[:, :])
                        link(dve.scalar_tensor_tensor(v3(p2), v3(hot1), -HUGE, v3(L), ALU.mult, ALU.add))
                        link(dve.tensor_reduce(m2[:, :], v3(p2), AX.X, ALU.max))
                        first_match(dve, link, v3(hot2), v3(p2), m2[:, :], v3(idx), v3(tmp), m[:, :])
                        dve.tensor_tensor(tmp[:, :, :], v3(L), wide(m1), ALU.subtract).then_inc(shifted, 1)
                        dve.wait_ge(exped, 1)
                        link(dve.tensor_tensor(v3(hot1), v3(hot1), v3(hot2), ALU.add))
                        link(dve.tensor_tensor(v3(p), v3(p), v3(hot1), ALU.mult))
                        link(dve.tensor_reduce(den[:, :], v3(p), AX.X, ALU.add))
                        link(dve.reciprocal(den[:, :], den[:, :]))
                        dve.tensor_tensor(v3(L), v3(p), wide(den), ALU.mult).then_inc(gated, 1)
                    else:
                        dve.wait_ge(logits, 1)
                        ps = K.bank[0][:, 0:TILES * E].rearrange("p (t e) -> p t e", e=E)
                        if gbd is not None:
                            link(dve.tensor_tensor(v3(L), ps, gb[:, :].unsqueeze(1).broadcast_to([P, TILES, E]), ALU.add))
                        else:
                            link(dve.tensor_copy(v3(L), ps))
                        link(dve.tensor_reduce(m1[:, :], v3(L), AX.X, ALU.max))
                        dve.tensor_tensor(tmp[:, :, :], v3(L), wide(m1), ALU.subtract).then_inc(shifted, 1)
                        dve.wait_ge(exped, 1)
                        link(dve.tensor_reduce(den[:, :], v3(p), AX.X, ALU.add))
                        link(dve.reciprocal(den[:, :], den[:, :]))
                        link(dve.tensor_tensor(v3(p), v3(p), wide(den), ALU.mult))
                        link(dve.tensor_reduce(m1[:, :], v3(p), AX.X, ALU.max))
                        first_match(dve, link, v3(hot1), v3(p), m1[:, :], v3(idx), v3(tmp), m[:, :])
                        if kind == "first":
                            dve.tensor_tensor(v3(L), v3(p), v3(hot1), ALU.mult).then_inc(gated, 1)
                        else:
                            link(dve.scalar_tensor_tensor(v3(p2), v3(hot1), -2.0, v3(p), ALU.mult, ALU.add))
                            link(dve.tensor_reduce(m2[:, :], v3(p2), AX.X, ALU.max))
                            first_match(dve, link, v3(hot2), v3(p2), m2[:, :], v3(idx), v3(tmp), m[:, :])
                            link(dve.tensor_tensor(v3(hot1), v3(hot1), v3(hot2), ALU.add))
                            if kind == "top2":
                                dve.tensor_tensor(v3(L), v3(p), v3(hot1), ALU.mult).then_inc(gated, 1)
                            else:
                                link(dve.tensor_tensor(v3(p), v3(p), v3(hot1), ALU.mult))
                                link(dve.tensor_tensor(den[:, :], m1[:, :], m2[:, :], ALU.add))
                                link(dve.tensor_scalar(den[:, :], den[:, :], 1e-12, None, ALU.max))
                                link(dve.reciprocal(den[:, :], den[:, :]))
                                dve.tensor_tensor(v3(L), v3(p), wide(den), ALU.mult).then_inc(gated, 1)
                    if kind == "first":
                        capacity = float(-(-5 * TOKENS // (4 * E)))
                        link(dve.memset(zero[:, :], 0.0))
                        dve.wait_ge(copied, 2 * BLOCKS)
                        link(dve.tensor_tensor_scan(hotT[:, :], hotT[:, :], zero[:, :].broadcast_to([E, TOKENS]), 0.0, ALU.add, ALU.add))
                        dve.scalar_tensor_tensor(gT[:, :], hotT[:, :], capacity, gT[:, :], ALU.is_le, ALU.mult)

        w1, w2 = sb("w1", [P, E, F]), sb("w2", [P, STEPS, P])
        b1, b2 = sb("b1", [P, STEPS]), sb("b2", [E, P])
        hid = [ctx.enter_context(nc.sbuf_tensor(f"{tag}_hidden{j}", [P, BLK], FP32)) for j in range(3)]
        hg = [ctx.enter_context(nc.sbuf_tensor(f"{tag}_gated{j}", [P, BLK], FP32)) for j in range(3)]
        fix = [ctx.enter_context(nc.sbuf_tensor(f"{tag}_fix{j}", [P, BLK], FP32)) for j in range(3)]
        gate_bank, h_bank, y_bank = [K.bank[0], K.bank[1], K.bank[7]], K.bank[2:5], K.bank[5:7]
        gate_spread, hid_ready, act_done, hid_gated, y_ready, added, ychain = (
            s("gate_spread"), s("hidden_ready"), s("activated"), s("hidden_gated"), s("y_ready"), s("added"), s("ychain"))
        wload = s("weights_in")
        LAG = 2
        with nc.Block() as block:
            @block.sync
            def _(sp):
                sp.dma_start(w1[:, :, :], w1d.rearrange("e d f -> d e f")).then_inc(wload, 16)
                sp.dma_start(w2[:, :, :], w2d.rearrange("e (c f) d -> f (e c) d", f=P)).then_inc(wload, 16)
                sp.dma_start(b1[:, :], b1d).then_inc(wload, 16)
                sp.dma_start(b2[:, :], b2d).then_inc(wload, 16)

            @block.tensor
            def _(pe):
                pe.wait_ge(wload, 64)
                with pe.Fori(0, IMAGES) as i:
                    for h in range(2):
                        n = i * 2 + h
                        cols = bass.ds(i * POS + h * BLK, BLK)
                        pe.wait_ge(added, n + 1)
                        for k in range(STEPS + LAG):
                            if k < STEPS:
                                e = k // C
                                if k % C == 0 and e >= 3:
                                    pe.wait_ge(hid_gated, n * STEPS + (e - 2) * C)
                                pe.matmul(h_bank[k % 3][:, :], w1[:, e, (k % C) * P:(k % C + 1) * P], K.pad[:, cols], start=True, stop=True).then_inc(hid_ready, 1)
                                if k % C == 0:
                                    pe.matmul(gate_bank[e % 3][:, :], K.ident[0:E, e:e + 1].broadcast_to([E, P]), gT[:, cols], start=True, stop=True).then_inc(gate_spread, 1)
                            if k >= LAG:
                                j = k - LAG
                                pe.wait_ge(hid_gated, n * STEPS + j + 1)
                                pe.matmul(y_bank[h][:, :], w2[:, j, :], hg[j % 3][:, :], start=(j == 0), stop=False)
                        pe.matmul(y_bank[h][:, :], b2[:, :], gT[:, cols], start=False, stop=True).then_inc(y_ready, 1)

            @block.scalar
            def _(act):
                act.wait_ge(wload, 64)
                with act.Fori(0, IMAGES) as i:
                    for h in range(2):
                        n = i * 2 + h
                        for k in range(STEPS):
                            act.wait_ge(hid_ready, n * STEPS + k + 1)
                            act.activation(hid[k % 3][:, :], h_bank[k % 3][:, :], ACT.Relu if kind == "first" else ACT.Gelu, bias=b1[:, k:k + 1]).then_inc(act_done, 1)

            @block.vector
            def _(dve):
                dve.sem_inc(added, 2)
                with dve.Fori(0, IMAGES) as i:
                    for h in range(2):
                        n = i * 2 + h
                        for k in range(STEPS):
                            e = k // C
                            dve.wait_ge(gate_spread, n * E + e + 1)
                            dve.wait_ge(act_done, n * STEPS + k + 1)
                            dve.tensor_tensor(hg[k % 3][:, :], hid[k % 3][:, :], gate_bank[e % 3][:, :], ALU.mult).then_inc(hid_gated, 1)
                        dve.wait_ge(y_ready, n + 1)
                        blk = K.x[:, bass.ds(i * POS + h * BLK, BLK)]
                        if kind == "first":
                            link = Link(dve, ychain, n * 7, apart=True)
                            y = y_bank[h][:, :]
                            clean, tested, other = [f[:, :] for f in fix]
                            dve.wait_ge(added, n + 2)
                            link(dve.tensor_copy(other, y))
                            link(dve.tensor_tensor(tested, other, other, ALU.is_equal))
                            link(dve.tensor_scalar(other, y, -1e4, 1e4, ALU.max, ALU.min))
                            link(dve.memset(clean, 0.0))
                            link(dve.copy_predicated(clean, tested.bitcast(U32), other))
                            link(dve.tensor_scalar(tested, y, 0.0, 0.0, ALU.mult, ALU.is_equal))
                            link(dve.copy_predicated(clean, tested.bitcast(U32), y))
                            dve.tensor_tensor(blk, blk, clean, ALU.add).then_inc(added, 1)
                            continue
                        if kind == "norm2":
                            link = Link(dve, ychain, n)
                            link(dve.tensor_tensor(blk, blk, K.pad[:, bass.ds(i * POS + h * BLK, BLK)], ALU.add))
                        dve.tensor_tensor(blk, blk, y_bank[h][:, :], ALU.add).then_inc(added, 1)


D_INNER, D_STATE, D_CONV, DT_RANK = 256, 16, 4, 8
HALVES = D_INNER // P
DIRECTIONS = 4
DT_ROWS = 96


def flipped(t, d):
    g = t.rearrange("p (y x) -> p y x", x=SIDE)
    if d == 0:
        return g
    if d == 1:
        return g[:, :, ::-1]
    return g[:, ::-1, :] if d == 2 else g[:, ::-1, ::-1]


def state_space(K, tag):
    nc, a = K.nc, K.a
    sem = lambda name: K.sem(f"{tag}_{name}")
    STEPS = HALVES * D_STATE
    loaded, const_ready, chain_p = sem("loaded"), sem("const_ready"), sem("chain_pool")
    pp_made, pp_used = sem("prep_bank_made"), sem("prep_bank_used")
    xm_ready, conv_done, xs_ready = sem("xm_ready"), sem("conv_done"), sem("xs_ready")
    rest_ready, split_done, low_ready, log_ready, prepared, sg_ready = (
        sem("rest_ready"), sem("split_done"), sem("low_ready"), sem("log_ready"), sem("prepared"), sem("sg_ready"))
    b_spread, c_spread, decay_ready = sem("b_spread"), sem("c_spread"), sem("decay_ready")
    fed, scanned, weighted, summed = sem("fed"), sem("scanned"), sem("weighted"), sem("summed")
    y_out, y_gated, chain_v, chain_a, added = sem("y_out"), sem("y_gated"), sem("chain_vector"), sem("chain_act"), sem("added")
    AHEAD, PER_IMAGE = 5, 3 * DIRECTIONS + 4 + 1
    use = {}
    for d in range(DIRECTIONS):
        for name in (["gate0", "gate1", "xm0", "xm1"] if d == DIRECTIONS - 1 else []) + ["dbl", "dt0", "dt1"]:
            use[d, name] = len(use)
    use[DIRECTIONS - 1, "out"] = len(use)
    assert len(use) == PER_IMAGE
    ahead = {"xm0": 0, "xm1": 1, "dbl": 2, "dt0": 3, "dt1": 4}

    with ExitStack() as ctx:
        sb = lambda n, shape, dt=FP32: ctx.enter_context(nc.sbuf_tensor(f"{tag}_{n}", shape, dt))
        w_in, w_x, w_dt, w_out = sb("w_in", [P, 2 * D_INNER]), sb("w_x", [P, HALVES, DT_ROWS + DT_RANK]), sb("w_dt", [DT_ROWS + DT_RANK, D_INNER]), sb("w_out", [P, HALVES, P])
        conv_w, conv_b, b_dt, dd = sb("conv_w", [P, HALVES, D_CONV]), sb("conv_b", [P, HALVES]), sb("b_dt", [P, HALVES]), sb("d", [P, HALVES])
        decay_rate = sb("decay_rate", [P, HALVES, D_STATE])
        pick = sb("pick", [3 * 32, 32], BF16)
        xm, xp = sb("xm", [P, HALVES, POS]), sb("xp", [P, D_CONV - 1 + POS])
        tap = sb("tap", [P, POS])
        xs, dt, dtx = [[sb(f"{n}{j}", [P, HALVES, POS]) for j in range(2)] for n in ("xs", "dt", "dtx")]
        rest, coarse = sb("rest", [DT_ROWS + DT_RANK, POS]), sb("coarse", [3 * 32, POS], BF16)
        parts = [sb(f"parts{j}", [3 * 32, POS], BF16) for j in range(2)]
        log = sb("log", [P, POS])
        decay = [sb(f"decay{j}", [P, POS]) for j in range(2)]
        st = [sb(f"state{j}", [P, POS]) for j in range(4)]
        y, sg = sb("y", [P, HALVES, POS]), sb("sg", [P, HALVES, POS])
        b_bank, c_bank, y_bank, p_bank = K.pair

        def both(pe, bank, rows, pieces):
            for half in range(2):
                cols = slice(half * BLK, (half + 1) * BLK)
                for n, (w, rhs) in enumerate(pieces):
                    last = pe.matmul(bank[rows, cols], w, rhs(half), start=(n == 0), stop=(n == len(pieces) - 1))
            return last

        with nc.Block() as block:
            @block.sync
            def _(sp):
                for to, src in ((w_in[:, :], "L2_conv_W_in"), (w_x[:, :, :], "L2_conv_W_x"), (w_dt[DT_ROWS:DT_ROWS + DT_RANK, :], "L2_conv_W_dt"), (w_out[:, :, :], "L2_conv_W_out"),
                                (conv_w[:, :, :], "L2_conv_conv_w"), (conv_b[:, :], "L2_conv_conv_b"), (b_dt[:, :], "L2_conv_b_dt"), (dd[:, :], "L2_conv_D"), (decay_rate[:, :, :], "L2_conv_A_log")):
                    sp.dma_start(to, a[src]).then_inc(loaded, 16)

            @block.gpsimd
            def _(pool):
                pool.wait_ge(loaded, 16 * 9)
                pool.memset(xp[:, 0:D_CONV - 1], 0.0).then_inc(chain_p, 1)
                pool.wait_ge(chain_p, 1)
                PER_SEQ = HALVES * 2 * D_CONV + 3

                def prepare(q, d, j, images, first=False):
                    link = Link(pool, chain_p, q * PER_SEQ + 1, apart=True)
                    if d == 0:
                        pool.wait_ge(xm_ready, images * HALVES)
                    if not first:
                        pool.wait_ge(y_out, (q - 1) * HALVES)
                    pool.nop(nofuse=True)
                    for h in range(HALVES):
                        link(pool.tensor_copy(xp[:, D_CONV - 1:].rearrange("p (y x) -> p y x", x=SIDE), flipped(xm[:, h, :], d)))
                        link(pool.tensor_scalar(xs[j][:, h, :], xp[:, 0:POS], conv_w[:, h, 0:1], None, ALU.mult))
                        for t in range(1, D_CONV):
                            link(pool.tensor_scalar(tap[:, :], xp[:, t:t + POS], conv_w[:, h, t:t + 1], None, ALU.mult))
                            link(pool.tensor_tensor(xs[j][:, h, :], xs[j][:, h, :], tap[:, :], ALU.add))
                        pool.sem_inc(conv_done, 1)
                    pool.wait_ge(rest_ready, q + 1)
                    pool.nop(nofuse=True)
                    link(pool.tensor_copy(parts[j][32:64, :], rest[32:64, :]))
                    link(pool.tensor_copy(coarse[64:96, :], rest[64:96, :]))
                    link(pool.tensor_tensor(parts[j][64:96, :], rest[64:96, :], coarse[64:96, :], ALU.subtract))
                    pool.sem_inc(split_done, 1)

                prepare(0, 0, 0, 1, first=True)
                with pool.Fori(0, IMAGES) as i:
                    for d in range(DIRECTIONS):
                        prepare(i * DIRECTIONS + d + 1, (d + 1) % DIRECTIONS, (d + 1) % 2, i + 1 + (d + 1) // DIRECTIONS)

            @block.tensor
            def _(pe):
                pe.wait_ge(loaded, 16 * 9)
                pe.wait_ge(const_ready, 4)
                pe.sem_inc(summed, 3)

                def project(which, image, n):
                    pe.wait_ge(pp_used, n)
                    both(pe, p_bank, slice(0, P), [(w_in[:, which * P:(which + 1) * P], lambda half: K.pad[:, bass.ds(image * POS + half * BLK, BLK)])]).then_inc(pp_made, 1)

                def rows_of(q, j, n):
                    pe.wait_ge(xs_ready, (q + 1) * HALVES)
                    pe.wait_ge(pp_used, n)
                    both(pe, p_bank, slice(0, DT_ROWS + DT_RANK), [(w_x[:, h, :], lambda half, h=h: xs[j][:, h, half * BLK:(half + 1) * BLK]) for h in range(HALVES)]).then_inc(pp_made, 1)

                def dt_of(q, h, n):
                    pe.wait_ge(low_ready, q + 1)
                    pe.wait_ge(pp_used, n)
                    rows = slice(DT_ROWS, DT_ROWS + DT_RANK)
                    both(pe, p_bank, slice(0, P), [(w_dt[rows, h * P:(h + 1) * P], lambda half: rest[rows, half * BLK:(half + 1) * BLK])]).then_inc(pp_made, 1)

                def spread(bank, j, row):
                    return both(pe, bank, slice(0, P), [(pick[:, row:row + 1].broadcast_to([3 * 32, P]), lambda half: parts[j][:, half * BLK:(half + 1) * BLK])])

                project(0, 0, ahead["xm0"])
                project(1, 0, ahead["xm1"])
                rows_of(0, 0, ahead["dbl"])
                dt_of(0, 0, ahead["dt0"])
                dt_of(0, 1, ahead["dt1"])
                with pe.Fori(0, IMAGES) as i:
                    for d in range(DIRECTIONS):
                        g, j, base = i * DIRECTIONS + d, d % 2, i * PER_IMAGE + AHEAD
                        pe.wait_ge(prepared, (g + 1) * HALVES)
                        pe.wait_ge(split_done, g + 1)
                        spread(b_bank, j, 0).then_inc(b_spread, 1)
                        for k in range(STEPS + 2):
                            K0 = g * STEPS + k
                            if k + 1 < STEPS:
                                pe.wait_ge(fed, K0 + 1)
                                spread(b_bank, j, (k + 1) % D_STATE).then_inc(b_spread, 1)
                            if k >= 1 and k - 1 < STEPS:
                                pe.wait_ge(weighted, K0 - 1)
                                spread(c_bank, j, D_STATE + (k - 1) % D_STATE).then_inc(c_spread, 1)
                            if k >= 2:
                                s = (k - 2) % D_STATE
                                pe.wait_ge(weighted, K0 - 1)
                                if s == 0:
                                    pe.wait_ge(y_out, g * HALVES + (k - 2) // D_STATE)
                                for half in range(2):
                                    cols = slice(half * BLK, (half + 1) * BLK)
                                    last = pe.matmul(y_bank[:, cols], K.ident[:, :], st[(k - 2) % 4][:, cols], start=(s == 0), stop=(s == D_STATE - 1))
                                last.then_inc(summed, 1)
                            if d == DIRECTIONS - 1 and k in (1, 3, 5, 7):
                                name, which, image = {1: ("gate0", 2, i), 3: ("gate1", 3, i), 5: ("xm0", 0, i + 1), 7: ("xm1", 1, i + 1)}[k]
                                project(which, image, base + use[d, name])
                            if k == 16:
                                rows_of(g + 1, 1 - j, base + use[d, "dbl"])
                            if k == 20:
                                dt_of(g + 1, 0, base + use[d, "dt0"])
                            if k == 24:
                                dt_of(g + 1, 1, base + use[d, "dt1"])
                    pe.wait_ge(y_gated, i + 1)
                    n = i * PER_IMAGE + AHEAD + use[DIRECTIONS - 1, "out"]
                    pe.wait_ge(pp_used, n)
                    both(pe, p_bank, slice(0, P), [(w_out[:, h, :], lambda half, h=h: y[:, h, half * BLK:(half + 1) * BLK]) for h in range(HALVES)]).then_inc(pp_made, 1)

            @block.scalar
            def _(act):
                act.wait_ge(loaded, 16 * 9)
                act.activation(decay_rate[:, :, :], decay_rate[:, :, :], ACT.Exp).then_inc(chain_a, 1)
                act.wait_ge(chain_a, 1)
                act.mul(decay_rate[:, :, :], decay_rate[:, :, :], -1.0).then_inc(chain_a, 1)
                act.wait_ge(chain_a, 2)

                def take_xm(h, n):
                    act.wait_ge(pp_made, n + 1)
                    act.copy(xm[:, h, :], p_bank[:, :]).then_inc(xm_ready, 1)
                    act.wait_ge(xm_ready, h + 1)
                    act.sem_inc(pp_used, 1)

                def silu_xs(q, j):
                    for h in range(HALVES):
                        act.wait_ge(conv_done, q * HALVES + h + 1)
                        act.activation(xs[j][:, h, :], xs[j][:, h, :], ACT.Silu, bias=conv_b[:, h:h + 1]).then_inc(xs_ready, 1)

                def take_low(q, n):
                    act.wait_ge(pp_made, n + 1)
                    act.copy(rest[DT_ROWS:DT_ROWS + DT_RANK, :], p_bank[DT_ROWS:DT_ROWS + DT_RANK, :]).then_inc(low_ready, 1)

                def log_of(q, h, n):
                    m = q * HALVES + h
                    act.wait_ge(pp_made, n + 1)
                    act.wait_ge(prepared, m)
                    link = Link(act, chain_a, m * 2 + 2)
                    link(act.activation(log[:, :], p_bank[:, :], ACT.Abs, bias=b_dt[:, h:h + 1]))
                    link(act.activation(log[:, :], log[:, :], ACT.Exp, scale=-1.0))
                    act.activation(log[:, :], log[:, :], ACT.Ln, bias=1.0).then_inc(log_ready, 1)

                take_xm(0, ahead["xm0"])
                take_xm(1, ahead["xm1"])
                silu_xs(0, 0)
                take_low(0, ahead["dbl"])
                log_of(0, 0, ahead["dt0"])
                log_of(0, 1, ahead["dt1"])
                with act.Fori(0, IMAGES) as i:
                    for d in range(DIRECTIONS):
                        g, j, base = i * DIRECTIONS + d, d % 2, i * PER_IMAGE + AHEAD
                        act.wait_ge(prepared, (g + 1) * HALVES)
                        for k in range(STEPS):
                            h, s = k // D_STATE, k % D_STATE
                            act.wait_ge(scanned, g * STEPS + k)
                            act.activation(decay[k % 2][:, :], dt[j][:, h, :], ACT.Exp, scale=decay_rate[:, h, s:s + 1]).then_inc(decay_ready, 1)
                            if d == DIRECTIONS - 1 and k in (2, 4):
                                hh = (k - 2) // 2
                                act.wait_ge(pp_made, base + use[d, f"gate{hh}"] + 1)
                                act.wait_ge(y_gated, i)
                                act.activation(sg[:, hh, :], p_bank[:, :], ACT.Silu).then_inc(sg_ready, 1)
                                act.wait_ge(sg_ready, i * HALVES + hh + 1)
                                act.sem_inc(pp_used, 1)
                            if d == DIRECTIONS - 1 and k in (6, 8):
                                hh = (k - 6) // 2
                                act.wait_ge(pp_made, base + use[d, f"xm{hh}"] + 1)
                                act.wait_ge(conv_done, (g + 1) * HALVES)
                                act.copy(xm[:, hh, :], p_bank[:, :]).then_inc(xm_ready, 1)
                                act.wait_ge(xm_ready, (i + 1) * HALVES + hh + 1)
                                act.sem_inc(pp_used, 1)
                            if k == 14:
                                silu_xs(g + 1, 1 - j)
                            if k == 17:
                                take_low(g + 1, base + use[d, "dbl"])
                            if k == 21:
                                log_of(g + 1, 0, base + use[d, "dt0"])
                            if k == 25:
                                log_of(g + 1, 1, base + use[d, "dt1"])

            @block.vector
            def _(dve):
                PER_SEQ = 1 + 2 * HALVES
                for m in range(3):
                    dve.tensor_copy(pick[32 * m:32 * m + 32, :], K.ident[32 * m:32 * m + 32, 32 * m:32 * m + 32]).then_inc(const_ready, 1)
                dve.memset(K.pad[:, TOKENS:TOKENS + POS], 0.0).then_inc(const_ready, 1)
                dve.sem_inc(scanned, 1)

                def link(ins, at):
                    ins.then_inc(chain_v, 1)
                    dve.wait_ge(chain_v, at)

                def split(q, j, n):
                    at = q * PER_SEQ
                    dve.wait_ge(pp_made, n + 1)
                    dve.wait_ge(split_done, q)
                    dve.tensor_copy(parts[j][0:32, :], p_bank[0:32, :])
                    link(dve.tensor_copy(coarse[:, :], p_bank[0:96, :]), at + 1)
                    dve.wait_ge(low_ready, q + 1)
                    dve.tensor_tensor(rest[0:96, :], p_bank[0:96, :], coarse[:, :], ALU.subtract).then_inc(rest_ready, 1)
                    dve.wait_ge(rest_ready, q + 1)
                    dve.sem_inc(pp_used, 1)

                def dt_half(q, j, h, n):
                    at = q * PER_SEQ + 1 + 2 * h
                    m = q * HALVES + h
                    dve.wait_ge(log_ready, m + 1)
                    link(dve.tensor_scalar(dt[j][:, h, :], p_bank[:, :], b_dt[:, h:h + 1], 0.0, ALU.add, ALU.max), at + 1)
                    dve.sem_inc(pp_used, 1)
                    link(dve.tensor_tensor(dt[j][:, h, :], dt[j][:, h, :], log[:, :], ALU.add), at + 2)
                    dve.tensor_tensor(dtx[j][:, h, :], dt[j][:, h, :], xs[j][:, h, :], ALU.mult).then_inc(prepared, 1)

                def take_y(i, d, j, h):
                    dve.wait_ge(summed, i * (DIRECTIONS * STEPS) + (d * HALVES + h + 1) * D_STATE + 3)
                    to = flipped(y[:, h, :], d)
                    grid = lambda t: t.rearrange("p (y x) -> p y x", x=SIDE)
                    if d == 0:
                        dve.scalar_tensor_tensor(to, grid(xs[j][:, h, :]), dd[:, h:h + 1], grid(y_bank[:, :]), ALU.mult, ALU.add).then_inc(y_out, 1)
                    else:
                        dve.scalar_tensor_tensor(xs[j][:, h, :], xs[j][:, h, :], dd[:, h:h + 1], y_bank[:, :], ALU.mult, ALU.add).then_inc(added, 1)
                        dve.wait_ge(added, i * (HALVES * (DIRECTIONS - 1)) + (d - 1) * HALVES + h + 1)
                        dve.tensor_tensor(to, to, grid(xs[j][:, h, :]), ALU.add).then_inc(y_out, 1)

                split(0, 0, ahead["dbl"])
                dt_half(0, 0, 0, ahead["dt0"])
                dt_half(0, 0, 1, ahead["dt1"])
                with dve.Fori(0, IMAGES) as i:
                    for d in range(DIRECTIONS):
                        g, j, base = i * DIRECTIONS + d, d % 2, i * PER_IMAGE + AHEAD
                        dve.wait_ge(prepared, (g + 1) * HALVES)
                        for k in range(STEPS + 2):
                            K0 = g * STEPS + k
                            if k < STEPS:
                                dve.wait_ge(b_spread, K0 + 1)
                                dve.wait_ge(summed, K0)
                                dve.tensor_tensor(st[k % 4][:, :], dtx[j][:, k // D_STATE, :], b_bank[:, :], ALU.mult).then_inc(fed, 1)
                            if 1 <= k <= STEPS:
                                s = (k - 1) % 4
                                dve.wait_ge(decay_ready, K0)
                                dve.wait_ge(fed, K0)
                                dve.tensor_tensor_scan(st[s][:, :], decay[(k - 1) % 2][:, :], st[s][:, :], 0.0, ALU.mult, ALU.add).then_inc(scanned, 1)
                            if k >= 2:
                                s = (k - 2) % 4
                                dve.wait_ge(c_spread, K0 - 1)
                                dve.wait_ge(scanned, K0)
                                dve.tensor_tensor(st[s][:, :], st[s][:, :], c_bank[:, :], ALU.mult).then_inc(weighted, 1)
                            if k == D_STATE + 2:
                                take_y(i, d, j, 0)
                            if k == 18:
                                split(g + 1, 1 - j, base + use[d, "dbl"])
                            if k == 23:
                                dt_half(g + 1, 1 - j, 0, base + use[d, "dt0"])
                            if k == 27:
                                dt_half(g + 1, 1 - j, 1, base + use[d, "dt1"])
                        take_y(i, d, j, 1)
                    dve.wait_ge(sg_ready, (i + 1) * HALVES)
                    dve.wait_ge(y_out, (i + 1) * DIRECTIONS * HALVES)
                    dve.tensor_tensor(y[:, :, :], y[:, :, :], sg[:, :, :], ALU.mult).then_inc(y_gated, 1)
                    dve.wait_ge(pp_made, i * PER_IMAGE + AHEAD + PER_IMAGE)
                    blk = K.x[:, bass.ds(i * POS, POS)]
                    dve.scalar_tensor_tensor(blk, p_bank[:, :], 1.0 / DIRECTIONS, blk, ALU.mult, ALU.add).then_inc(pp_used, 1)


EDGES = 524288
LANE = 128
CHUNK = P * LANE
EC = EDGES // CHUNK
RUNS = EDGES // LANE
COLS = EDGES // P
HEADS, EXPERTS1 = 4, 4
ROW = HEADS * (1 + EXPERTS1)
STATE = HEADS * (2 + EXPERTS1)
NODE_BITS, EDGE_BITS, LANE_BITS = 13, 19, 7
KEY_BASE = 0x20000000
SCAT_SKIP = 1 << 22


def sort_plan():
    plan = []
    for k in range(1, EDGE_BITS + 1):
        if k == LANE_BITS:
            plan.append(("sign", "N", 0, 0, k))
        if k > LANE_BITS:
            plan.append(("turn", "T", 0, 0, k))
            plan += [("stage", "T", j - LANE_BITS, k - LANE_BITS if k < EDGE_BITS else None, k) for j in range(k - 1, LANE_BITS - 1, -1)]
            plan.append(("turn", "N", 0, 0, k))
        for j in range(min(k, LANE_BITS) - 1, -1, -1):
            bit = k if k < LANE_BITS else None if k < 2 * LANE_BITS or k == EDGE_BITS else k - LANE_BITS
            plan.append(("stage", "N", j, bit, k))
    return plan


def compare(dve, src, dst, bit, direction):
    low = 1 << bit
    if direction is None:
        a, b = [t.rearrange("p (m h l) -> p m h l", h=2, l=low) for t in (src, dst)]
        dve.tensor_tensor(b[:, :, 0, :], a[:, :, 0, :], a[:, :, 1, :], ALU.min)
        return dve.tensor_tensor(b[:, :, 1, :], a[:, :, 0, :], a[:, :, 1, :], ALU.max)
    mid = 1 << (direction - 1 - bit)
    a, b = [t.rearrange("p (o d m h l) -> p o d m h l", d=2, m=mid, h=2, l=low) for t in (src, dst)]
    for d in range(2):
        x, z = a[:, :, d, :, 0, :], a[:, :, d, :, 1, :]
        dve.tensor_tensor(b[:, :, d, :, 0, :], x, z, ALU.max if d else ALU.min)
        last = dve.tensor_tensor(b[:, :, d, :, 1, :], x, z, ALU.min if d else ALU.max)
    return last


def sort_edges(K, tag, keys, tables):
    nc, a = K.nc, K.a
    sem = lambda name: K.sem(f"{tag}_{name}")
    loaded, steps, turned, moved = sem("edges_loaded"), sem("steps"), sem("turned"), sem("moved")
    zeros_made, cleared = sem("zeros_made"), sem("tables_cleared")
    plan = sort_plan()
    with ExitStack() as ctx:
        raw = [ctx.enter_context(nc.sbuf_tensor(f"{tag}_raw{j}", [P, COLS], I32)) for j in range(2)]
        sign = ctx.enter_context(nc.sbuf_tensor(f"{tag}_sign", [P, LANE_BITS], FP32))
        ZERO_ROWS = 64
        zeros = ctx.enter_context(nc.sbuf_tensor(f"{tag}_zeros", [P, ZERO_ROWS * max(t.shape[1] for t in tables)], FP32))
        PREP = 9
        with nc.Block() as block:
            @block.sync
            def _(sp):
                for j in range(2):
                    sp.dma_start(raw[j][:, :], a["L1_ffn_edge_index"][j].rearrange("(p f) -> p f", p=P)).then_inc(loaded, 16)
                sp.dma_start(sign[:, :], a["sort_sign"]).then_inc(loaded, 16)
                sp.wait_ge(zeros_made, 1)
                for table in tables:
                    n, width = EDGES // P // ZERO_ROWS, ZERO_ROWS * table.shape[1]
                    sp.dma_start(table.rearrange("(p n e) f -> p n (e f)", p=P, n=n), zeros[:, 0:width].unsqueeze(1).broadcast_to([P, n, width])).then_inc(cleared, 16)
                sp.wait_ge(cleared, 16 * len(tables))

            @block.gpsimd
            def _(pool):
                pool.memset(zeros[:, :], 0.0).then_inc(zeros_made, 1)

            @block.tensor
            def _(pe):
                n, cur, turns = PREP, 0, 0
                for what, layout, bit, direction, k in plan:
                    if what == "turn":
                        pe.wait_ge(steps, n)
                        if turns:
                            pe.wait_ge(moved, 2 * turns)
                        for q in range(4):
                            for c in range(8):
                                at = (8 * q + c) * P
                                last = pe.transpose(K.pair[q][:, c * P:(c + 1) * P], keys[cur][:, at:at + P], K.ident[:, :])
                            last.then_inc(turned, 1)
                        turns += 1
                    n += 1
                    cur = 1 - cur

            def move(eng, scalar, layout, k, q, dst):
                out, src = dst[:, q * 8 * P:(q + 1) * 8 * P], K.pair[q][:, :]
                if layout == "T" and LANE_BITS <= k - 1 < 2 * LANE_BITS:
                    low = 1 << (k - 1 - LANE_BITS)
                    o, s = [t.rearrange("p (m d l) -> p m d l", d=2, l=low) for t in (out, src)]
                    if scalar:
                        eng.copy(o[:, :, 0, :], s[:, :, 0, :])
                        return eng.mul(o[:, :, 1, :], s[:, :, 1, :], -1.0)
                    eng.tensor_copy(o[:, :, 0, :], s[:, :, 0, :])
                    return eng.tensor_scalar(o[:, :, 1, :], s[:, :, 1, :], -1.0, None, ALU.mult)
                if layout == "N" and k < 2 * LANE_BITS:
                    col = sign[:, k - LANE_BITS:k - LANE_BITS + 1]
                    return eng.mul(out, src, col) if scalar else eng.tensor_scalar(out, src, col, None, ALU.mult)
                return eng.copy(out, src) if scalar else eng.tensor_copy(out, src)

            @block.scalar
            def _(act):
                cur, turns = 0, 0
                for what, layout, bit, direction, k in plan:
                    if what == "turn":
                        for q in (2, 3):
                            act.wait_ge(turned, 4 * turns + q + 1)
                            move(act, True, layout, k, q, keys[1 - cur]).then_inc(moved, 1)
                        turns += 1
                    cur = 1 - cur

            @block.vector
            def _(dve):
                link = Link(dve, steps)
                dve.wait_ge(loaded, 48)
                x, z = keys[0][:, :], keys[1][:, :]
                rs, rd = raw[0][:, :], raw[1][:, :]
                link(dve.tensor_copy(x, rd))
                link(dve.tensor_scalar(z, x, 0.0, None, ALU.is_ge))
                link(dve.scalar_tensor_tensor(z, x, float(TOKENS), z, ALU.is_lt, ALU.mult))
                link(dve.scalar_tensor_tensor(z, x, -float(TOKENS), z, ALU.add, ALU.mult))
                link(dve.tensor_scalar(rd, z, float(TOKENS), None, ALU.add))
                dve.tensor_scalar(z, rs, 0.0, float(TOKENS), ALU.is_lt, ALU.mult)
                link(dve.tensor_scalar(rd, rd, NODE_BITS, KEY_BASE, ALU.logical_shift_left, ALU.bitwise_or))
                link(dve.tensor_tensor(z, z, rs, ALU.add))
                link(dve.tensor_scalar(rs, z, 0.0, float(TOKENS - 1), ALU.max, ALU.min))
                link(dve.tensor_tensor(x.bitcast(I32), rs, rd, ALU.bitwise_or))
                assert link.n == PREP
                cur, turns = 0, 0
                for what, layout, bit, direction, k in plan:
                    src, dst = keys[cur][:, :], keys[1 - cur][:, :]
                    if what == "stage":
                        link(compare(dve, src, dst, bit, direction))
                    elif what == "sign":
                        link(dve.tensor_scalar(dst, src, sign[:, 0:1], None, ALU.mult))
                    else:
                        for q in (0, 1):
                            dve.wait_ge(turned, 4 * turns + q + 1)
                            last = move(dve, False, layout, k, q, keys[1 - cur])
                        link(last)
                        turns += 1
                        dve.wait_ge(moved, 2 * turns)
                    cur = 1 - cur
    return len(plan) % 2


def graph_attention(K, tag):
    nc, a = K.nc, K.a
    sem = lambda name: K.sem(f"{tag}_{name}")
    dram = lambda n, shape: nc.dram_tensor(f"{tag}_{n}", shape, FP32, kind="Internal").ap()
    node_rows, dst_rows = dram("node_rows", (TOKENS, ROW)), dram("dst_rows", (TOKENS, HEADS))
    dst_at_start, edge_rows = dram("dst_at_start", (EDGES, HEADS)), dram("edge_rows", (EDGES, STATE))
    run_rows = dram("run_rows", (RUNS, 2 * ROW))
    with ExitStack() as ctx:
        sb = lambda n, shape, dt=FP32: ctx.enter_context(nc.sbuf_tensor(f"{tag}_{n}", shape, dt))
        count, first, end = sb("count", [P, TILES]), sb("first", [P, TILES]), sb("end", [P, TILES])
        chunks = sb("chunks", [P, 1], I32)
        h, asrc, adst = sb("h", [P, TILES, HEADS, 1 + EXPERTS1]), sb("asrc", [P, TILES, HEADS]), sb("adst", [P, TILES, HEADS])
        runs = sb("runs", [P, EC, 4, ROW])
        with ExitStack() as outer:
            src_idx = outer.enter_context(nc.sbuf_tensor(f"{tag}_src_idx", [P, EC + 2, LANE], I32))
            dstf = outer.enter_context(nc.sbuf_tensor(f"{tag}_dstf", [P, EC + 2, LANE], FP32))
            with ExitStack() as inner:
                keys = [inner.enter_context(nc.sbuf_tensor(f"{tag}_keys{j}", [P, COLS], FP32)) for j in range(2)]
                at = sort_edges(K, tag + "s", keys, (dst_at_start, edge_rows))
                count_edges(K, tag + "c", keys[at], keys[1 - at], src_idx, dstf, count, first, end, chunks)
            node_tables(K, tag + "t", h, asrc, adst, node_rows, dst_rows)
            place_starts(K, tag + "p", count, first, adst, dst_at_start)
            edge_pass(K, tag + "e", src_idx, dstf, node_rows, dst_rows, dst_at_start, edge_rows, runs, chunks)
        join_runs(K, tag + "j", runs, run_rows)
        node_scores(K, tag + "n", count, first, end, h, asrc, adst, edge_rows, run_rows)


def busy_chunks(eng, chunks, known=None):
    if known is not None:
        eng.wait_ge(known, 1)
    return eng.value_load(chunks[0:1, 0:1], min_val=1, max_val=EC)


def count_edges(K, tag, keys, lo, src_idx, dstf, count, first, end, chunks):
    nc, a = K.nc, K.a
    sem = lambda name: K.sem(f"{tag}_{name}")
    chain, loaded, hot_ready, hot_used, bank_free, added, summed = sem("chain"), sem("loaded"), sem("hot_ready"), sem("hot_used"), sem("bank_free"), sem("added"), sem("summed")
    all_ones, counted_real, chunks_known = sem("all_ones"), sem("counted_real"), sem("chunks_known")
    G = 16
    GROUPS = LANE // G
    FIRST_OTHER = float(np.array([KEY_BASE + (TOKENS << NODE_BITS)], np.int32).view(np.float32)[0])
    with ExitStack() as ctx:
        sb = lambda n, shape, dt=FP32: ctx.enter_context(nc.sbuf_tensor(f"{tag}_{n}", shape, dt))
        hi = keys
        iota, below = sb("iota", [P, P]), sb("below", [P, P])
        ones, zero = sb("ones", [P, P]), sb("zero", [P, TILES])
        hot_lo = [sb(f"hot_lo{j}", [P, G, P], BF16) for j in range(2)]
        hot_hi = [sb(f"hot_hi{j}", [P, G, TILES], BF16) for j in range(2)]
        total, real = sb("total", [P, TILES]), sb("real", [P, 1])
        with nc.Block() as block:
            @block.sync
            def _(sp):
                sp.dma_start(iota[:, :], a["column_number"]).then_inc(loaded, 16)
                sp.dma_start(below[:, :], a["strictly_below"]).then_inc(loaded, 16)

            @block.tensor
            def _(pe):
                pe.wait_ge(all_ones, 1)
                pe.matmul(K.bank[1][:, 0:1], ones[:, :], real[:, :], start=True, stop=True).then_inc(counted_real, 1)
                busy = busy_chunks(pe, chunks, chunks_known)
                with pe.Fori(0, EC) as c:
                    with pe.If(busy > c):
                        pe.wait_ge(bank_free, c + 1)
                        for g in range(GROUPS):
                            pe.wait_ge(hot_ready, c * GROUPS + g + 1)
                            for n in range(G):
                                last = pe.matmul(K.bank[0][:, 0:TILES], hot_lo[g % 2][:, n, :], hot_hi[g % 2][:, n, :], start=(g == 0 and n == 0), stop=(g == GROUPS - 1 and n == G - 1))
                            last.then_inc(hot_used, 1)
                    with pe.Else():
                        pe.nop()
                pe.wait_ge(summed, 1)
                pe.matmul(K.bank[2][:, 0:TILES], below[:, :], count[:, :], start=True, stop=True)
                pe.matmul(K.bank[3][:, 0:TILES], ones[:, :], count[:, :], start=True, stop=True).then_inc(summed, 1)

            @block.vector
            def _(dve):
                link = Link(dve, chain)
                bits = keys[:, :].bitcast(I32)
                flat = lambda t: t[:, 0:EC, :].rearrange("p c f -> p (c f)")
                dve.memset(src_idx[:, EC:, :], 0)
                dve.memset(dstf[:, EC:, :], 0.0)
                link(dve.tensor_scalar(lo[:, :], keys[:, :], FIRST_OTHER, None, ALU.is_lt))
                link(dve.tensor_reduce(real[:, :], lo[:, :], AX.X, ALU.add))
                dve.memset(ones[:, :], 1.0).then_inc(all_ones, 1)
                dve.wait_ge(counted_real, 1)
                link(dve.tensor_scalar(real[:, :], K.bank[1][:, 0:1], 1.0, float(CHUNK - 1), ALU.max, ALU.add))
                link(dve.tensor_copy(chunks[:, :], real[:, :]))
                dve.tensor_scalar(chunks[:, :], chunks[:, :], (CHUNK - 1).bit_length(), None, ALU.logical_shift_right).then_inc(chunks_known, 1)
                link(dve.tensor_scalar(flat(src_idx), bits, TOKENS - 1, None, ALU.bitwise_and))
                link(dve.tensor_scalar(bits, bits, NODE_BITS, 2 * TOKENS - 1, ALU.logical_shift_right, ALU.bitwise_and))
                link(dve.tensor_copy(flat(dstf), bits))
                link(dve.tensor_scalar(lo[:, :].bitcast(I32), bits, P - 1, None, ALU.bitwise_and))
                link(dve.tensor_scalar(hi[:, :].bitcast(I32), bits, 7, None, ALU.logical_shift_right))
                link(dve.tensor_copy(lo[:, :], lo[:, :].bitcast(I32)))
                link(dve.tensor_copy(hi[:, :], hi[:, :].bitcast(I32)))
                link(dve.memset(count[:, :], 0.0))
                link(dve.memset(zero[:, :], 0.0))
                dve.wait_ge(loaded, 32)
                busy = busy_chunks(dve, chunks, chunks_known)
                n0 = link.n
                dve.sem_inc(hot_used, 2)
                dve.sem_inc(bank_free, 1)
                with dve.Fori(0, EC) as c:
                    with dve.If(busy > c):
                        for g in range(GROUPS):
                            def one_hot(out, v, n):
                                at = v[:, bass.ds(c * LANE + g * G, G)].unsqueeze(2).broadcast_to([P, G, n])
                                return dve.tensor_tensor(out, at, iota[:, 0:n].unsqueeze(1).broadcast_to([P, G, n]), ALU.is_equal)
                            dve.wait_ge(hot_used, c * GROUPS + g + 1)
                            one_hot(hot_lo[g % 2][:, :, :], lo, P)
                            one_hot(hot_hi[g % 2][:, :, :], hi, TILES).then_inc(hot_ready, 1)
                        dve.wait_ge(hot_used, c * GROUPS + GROUPS + 2)
                        dve.tensor_tensor(count[:, :], count[:, :], K.bank[0][:, 0:TILES], ALU.add).then_inc(added, 1)
                        dve.wait_ge(added, c + 1)
                        dve.sem_inc(bank_free, 1)
                    with dve.Else():
                        dve.nop()
                dve.sem_inc(summed, 1)
                dve.wait_ge(summed, 2)
                link = Link(dve, chain, n0)
                link(dve.tensor_copy(total[:, :], K.bank[3][:, 0:TILES]))
                link(dve.tensor_tensor_scan(first[:, :], total[:, :], zero[:, :], 0.0, ALU.add, ALU.add))
                link(dve.tensor_tensor(first[:, :], first[:, :], total[:, :], ALU.subtract))
                link(dve.tensor_tensor(first[:, :], first[:, :], K.bank[2][:, 0:TILES], ALU.add))
                link(dve.tensor_tensor(end[:, :], first[:, :], count[:, :], ALU.add))


def node_tables(K, tag, h, asrc, adst, node_rows, dst_rows):
    nc, a = K.nc, K.a
    sem = lambda name: K.sem(f"{tag}_{name}")
    loaded, made, chain, stored = sem("loaded"), sem("made"), sem("chain"), sem("stored")
    HE = HEADS * EXPERTS1
    with ExitStack() as ctx:
        sb = lambda n, shape, dt=FP32: ctx.enter_context(nc.sbuf_tensor(f"{tag}_{n}", shape, dt))
        w, att = sb("w", [P, HE]), sb("att", [P, 2, HE])
        prod = sb("prod", [P, TILES, HEADS, EXPERTS1])
        with nc.Block() as block:
            @block.sync
            def _(sp):
                sp.dma_start(w[:, :], a["L1_ffn_W_gat"]).then_inc(loaded, 16)
                sp.dma_start(att[:, :, :], a["L1_ffn_att"]).then_inc(loaded, 16)
                sp.wait_ge(chain, 6)
                sp.dma_start(node_rows.rearrange("(t p) f -> p t f", p=P), h[:, :, :, :].rearrange("p t a b -> p t (a b)")).then_inc(stored, 16)
                sp.dma_start(dst_rows.rearrange("(t p) f -> p t f", p=P), adst[:, :, :]).then_inc(stored, 16)
                sp.wait_ge(stored, 16 * 2)

            @block.tensor
            def _(pe):
                pe.wait_ge(loaded, 32)
                for t in range(TILES):
                    last = pe.matmul(K.pair[0][:, t * HE:(t + 1) * HE], K.pad[:, t * P:(t + 1) * P], w[:, :], start=True, stop=True)
                last.then_inc(made, 1)

            @block.vector
            def _(dve):
                link = Link(dve, chain)
                dve.wait_ge(loaded, 32)
                dve.wait_ge(made, 1)
                ps = K.pair[0][:, :].rearrange("p (t a b) -> p t a b", a=HEADS, b=EXPERTS1)
                link(dve.tensor_copy(h[:, :, :, 1:], ps))
                for n, to in ((0, asrc), (1, adst)):
                    weights = att[:, n, :].rearrange("p (a b) -> p a b", b=EXPERTS1).unsqueeze(1).broadcast_to([P, TILES, HEADS, EXPERTS1])
                    link(dve.tensor_tensor(prod[:, :, :, :], h[:, :, :, 1:], weights, ALU.mult))
                    link(dve.tensor_reduce(to[:, :, :], prod[:, :, :, :], AX.X, ALU.add))
                link(dve.tensor_copy(h[:, :, :, 0], asrc[:, :, :]))


def place_starts(K, tag, count, first, adst, dst_at_start):
    nc = K.nc
    sem = lambda name: K.sem(f"{tag}_{name}")
    chain, placed = sem("chain"), sem("placed")
    with ExitStack() as ctx:
        t = ctx.enter_context(nc.sbuf_tensor(f"{tag}_t", [P, TILES], FP32))
        idx = ctx.enter_context(nc.sbuf_tensor(f"{tag}_idx", [P, TILES], I32))
        with nc.Block() as block:
            @block.vector
            def _(dve):
                link = Link(dve, chain)
                link(dve.tensor_scalar(t[:, :], count[:, :], 0.0, float(SCAT_SKIP), ALU.is_equal, ALU.mult))
                link(dve.tensor_tensor(idx[:, :], t[:, :], first[:, :], ALU.add))

            @block.gpsimd
            def _(pool):
                pool.wait_ge(chain, 2)
                for n in range(TILES):
                    pool.indirect_dma_start(out=dst_at_start, out_offset=bass.IndirectOffsetOnAxis(ap=idx[:, n:n + 1], axis=0),
                                            in_=adst[:, n, :], in_offset=None, bounds_check=EDGES - 1, oob_is_err=False).then_inc(placed, 16)
                pool.wait_ge(placed, 16 * TILES)


def edge_pass(K, tag, src_idx, dstf, node_rows, dst_rows, dst_at_start, edge_rows, runs, chunks):
    nc = K.nc
    sem = lambda name: K.sem(f"{tag}_{name}")
    W = 1 + EXPERTS1
    idx_ready, rows_in, start_in, used, chain = sem("idx_ready"), [sem("rows_in0"), sem("rows_in1")], [sem("start_in0"), sem("start_in1")], sem("used"), sem("chain")
    exp_in, exp_out, stored, first_in = sem("exp_in"), sem("exp_out"), [sem("stored0"), sem("stored1")], [sem("first_in0"), sem("first_in1")]
    with ExitStack() as ctx:
        sb = lambda n, shape, dt=FP32: ctx.enter_context(nc.sbuf_tensor(f"{tag}_{n}", shape, dt))
        idx = [sb(f"idx{j}", [P, LANE + 1], I32) for j in range(2)]
        rows = [sb(f"rows{j}", [P, LANE, HEADS, W]) for j in range(2)]
        start = [sb(f"start{j}", [P, LANE, HEADS]) for j in range(2)]
        begin = [sb(f"begin{j}", [P, HEADS]) for j in range(2)]
        keep, reset = sb("keep", [P, LANE]), sb("reset", [P, LANE])
        e, ex = sb("e", [P, HEADS, LANE]), [sb(f"ex{j}", [P, 2, HEADS, LANE]) for j in range(2)]
        m = sb("m", [P, HEADS, LANE + 1])
        out = [sb(f"out{j}", [P, LANE, HEADS, 1 + W]) for j in range(2)]
        LINKS = 10 + 2 * HEADS
        with nc.Block() as block:
            @block.gpsimd
            def _(pool):
                busy = busy_chunks(pool, chunks)
                with pool.Fori(0, EC // 2) as i:
                    for j in range(2):
                        c = i * 2 + j
                        with pool.If(busy > c):
                            pool.wait_ge(idx_ready, c + 1)
                            pool.wait_ge(used, c + 1)
                            pool.nop(nofuse=True)
                            pool.indirect_dma_start(out=begin[j][:, :], out_offset=None, in_=dst_rows,
                                                    in_offset=bass.IndirectOffsetOnAxis(ap=idx[j][:, LANE:LANE + 1], axis=0)).then_inc(first_in[j], 16)
                            for f in range(LANE):
                                pool.indirect_dma_start(out=rows[j][:, f, :, :].rearrange("p a b -> p (a b)"), out_offset=None, in_=node_rows,
                                                        in_offset=bass.IndirectOffsetOnAxis(ap=idx[j][:, f:f + 1], axis=0)).then_inc(rows_in[j], 16)
                        with pool.Else():
                            pool.nop()

            @block.sync
            def _(sp):
                starts = dst_at_start.rearrange("(c p f) a -> c p (f a)", p=P, f=LANE)
                outs = edge_rows.rearrange("(c p f) a -> c p (f a)", p=P, f=LANE)
                busy = busy_chunks(sp, chunks)
                with sp.Fori(0, EC // 2) as i:
                    for j in range(2):
                        c = i * 2 + j
                        with sp.If(busy > c):
                            sp.wait_ge(used, c + 1)
                            sp.dma_start(start[j][:, :, :].rearrange("p f a -> p (f a)"), starts[c]).then_inc(start_in[j], 16)
                        with sp.Else():
                            sp.nop()
                    for j in range(2):
                        c = i * 2 + j
                        with sp.If(busy > c):
                            sp.wait_ge(used, c + 3)
                            sp.dma_start(outs[c], out[j][:, :, :, :].rearrange("p f a b -> p (f a b)")).then_inc(stored[j], 16)
                            sp.wait_ge(stored[j], (i + 1) * 16)
                            sp.nop(nofuse=True)
                        with sp.Else():
                            sp.nop()

            @block.scalar
            def _(act):
                busy = busy_chunks(act, chunks)
                with act.Fori(0, EC // 2) as i:
                    for j in range(2):
                        c = i * 2 + j
                        with act.If(busy > c):
                            act.wait_ge(exp_in, c + 1)
                            act.activation(ex[j][:, :, :, :], ex[j][:, :, :, :], ACT.Exp).then_inc(exp_out, 1)
                        with act.Else():
                            act.nop()

            @block.vector
            def _(dve):
                dve.sem_inc(used, 2)
                dve.memset(m[:, :, 0:1], -HUGE)
                dve.memset(keep[:, 0:1], 0.0).then_inc(chain, 1)
                dve.wait_ge(chain, 1)

                def take_indices(c, j):
                    dve.tensor_copy(idx[j][:, 0:LANE], src_idx[:, c, :])
                    dve.tensor_scalar(idx[j][:, LANE:LANE + 1], dstf[:, c, 0:1], float(TOKENS - 1), None, ALU.min).then_inc(idx_ready, 1)

                busy = busy_chunks(dve, chunks)
                dve.memset(runs[:, :, :, :], 0.0).then_inc(chain, 1)
                dve.wait_ge(chain, 2)
                take_indices(0, 0)
                take_indices(1, 1)
                with dve.Fori(0, EC // 2) as i:
                    for j in range(2):
                        c = i * 2 + j
                        with dve.If(busy > c):
                            link = Link(dve, chain, c * LINKS + 2)
                            dcol = dstf[:, c, :]
                            link(dve.tensor_tensor(keep[:, 1:LANE], dcol[:, 1:LANE], dcol[:, 0:LANE - 1], ALU.is_equal))
                            link(dve.tensor_scalar(reset[:, :], keep[:, :], -1.0, HUGE, ALU.add, ALU.mult))
                            dve.wait_ge(start_in[j], (i + 1) * 16)
                            dve.wait_ge(first_in[j], (i + 1) * 16)
                            link(dve.tensor_copy(start[j][:, 0, :], begin[j][:, :]))
                            for a in range(HEADS):
                                link(dve.tensor_tensor_scan(e[:, a, :], keep[:, :], start[j][:, :, a], 0.0, ALU.mult, ALU.add))
                            dve.wait_ge(rows_in[j], (i + 1) * (16 * LANE))
                            link(dve.tensor_tensor(e[:, :, :], e[:, :, :], rows[j][:, :, :, 0].rearrange("p f a -> p a f"), ALU.add))
                            link(dve.scalar_tensor_tensor(e[:, :, :], e[:, :, :], 0.2, e[:, :, :], ALU.mult, ALU.max))
                            for a in range(HEADS):
                                link(dve.tensor_tensor_scan(m[:, a, 1:], reset[:, :], e[:, a, :], -HUGE, ALU.add, ALU.max))
                            both = ex[j]
                            dve.tensor_tensor(both[:, 1, :, :], e[:, :, :], m[:, :, 1:], ALU.subtract)
                            link(dve.tensor_tensor(both[:, 0, :, :], m[:, :, 0:LANE], reset[:, :].unsqueeze(1).broadcast_to([P, HEADS, LANE]), ALU.add))
                            dve.tensor_tensor(both[:, 0, :, :], both[:, 0, :, :], m[:, :, 1:], ALU.subtract).then_inc(exp_in, 1)
                            link(dve.memset(rows[j][:, :, :, 0], 1.0))
                            dve.wait_ge(stored[j], i * 16)
                            link(dve.tensor_copy(out[j][:, :, :, 0].rearrange("p f a -> p a f"), m[:, :, 1:]))
                            dve.wait_ge(exp_out, c + 1)
                            for a in range(HEADS):
                                last = dve.tensor_tensor(rows[j][:, :, a, :], rows[j][:, :, a, :], both[:, 1, a, :].unsqueeze(2).broadcast_to([P, LANE, W]), ALU.mult)
                            link(last)
                            for a in range(HEADS):
                                for b in range(W):
                                    last = dve.tensor_tensor_scan(out[j][:, :, a, 1 + b], both[:, 0, a, :], rows[j][:, :, a, b], 0.0, ALU.mult, ALU.add)
                            link(last)
                            assert link.n == LINKS
                            end = lambda n: runs[:, c, n, :].rearrange("p (a b) -> p a b", b=W)
                            dve.tensor_copy(end(0), m[:, :, LANE:LANE + 1].broadcast_to([P, HEADS, W]))
                            dve.tensor_copy(end(1), out[j][:, LANE - 1, :, 1:])
                            dve.tensor_copy(runs[:, c, 2, :], dstf[:, c, 0:1].broadcast_to([P, ROW]))
                            dve.tensor_copy(runs[:, c, 3, :], dstf[:, c, LANE - 1:LANE].broadcast_to([P, ROW])).then_inc(used, 1)
                            dve.wait_ge(used, c + 3)
                            take_indices(c + 2, j)
                        with dve.Else():
                            dve.nop()


def join_runs(K, tag, runs, run_rows):
    nc = K.nc
    sem = lambda name: K.sem(f"{tag}_{name}")
    turned, taken, chain, exp_in, exp_out, back, laid, stored = (
        sem("turned"), sem("taken"), sem("chain"), sem("exp_in"), sem("exp_out"), sem("back"), sem("laid"), sem("stored"))
    with ExitStack() as ctx:
        t = [ctx.enter_context(nc.sbuf_tensor(f"{tag}_{n}", [ROW, RUNS], FP32)) for n in ("top", "sums", "firsts", "lasts")]
        run_top = ctx.enter_context(nc.sbuf_tensor(f"{tag}_run_top", [ROW, RUNS + 1], FP32))
        top, sums, firsts, lasts = t
        GROUPS = EC // 8
        with nc.Block() as block:
            @block.tensor
            def _(pe):
                n = 0
                for s in range(4):
                    for q in range(GROUPS):
                        if n >= 4:
                            pe.wait_ge(taken, n - 3)
                        for c in range(8):
                            last = pe.transpose(K.pair[n % 4][0:ROW, c * P:(c + 1) * P], runs[:, 8 * q + c, s, :], K.ident[:, :])
                        last.then_inc(turned, 1)
                        n += 1
                pe.wait_ge(chain, 10)
                pe.wait_ge(taken, n)
                for g in range(2):
                    src = run_top[:, 1:] if g == 0 else lasts[:, :]
                    for c in range(EC):
                        at = c // 16 * BLK + c % 16 * ROW
                        last = pe.transpose(K.pair[g][:, at:at + ROW], src[:, c * P:(c + 1) * P], K.ident[0:ROW, 0:ROW])
                    last.then_inc(back, 1)

            @block.scalar
            def _(act):
                n = 0
                for s in range(4):
                    for q in range(GROUPS):
                        act.wait_ge(turned, n + 1)
                        act.copy(t[s][:, q * 8 * P:(q + 1) * 8 * P], K.pair[n % 4][0:ROW, :]).then_inc(taken, 1)
                        n += 1
                act.wait_ge(exp_in, 1)
                act.activation(firsts[:, :], firsts[:, :], ACT.Exp).then_inc(exp_out, 1)
                act.activation(lasts[:, :], lasts[:, :], ACT.Exp).then_inc(exp_out, 1)

            @block.vector
            def _(dve):
                link = Link(dve, chain)
                dve.wait_ge(taken, 4 * GROUPS)
                joins = run_top
                link(dve.memset(joins[:, 0:1], 0.0))
                link(dve.tensor_tensor(joins[:, 1:RUNS], firsts[:, 1:], lasts[:, 0:RUNS - 1], ALU.is_equal))
                link(dve.tensor_tensor(firsts[:, :], firsts[:, :], lasts[:, :], ALU.is_equal))
                link(dve.tensor_tensor(firsts[:, :], firsts[:, :], joins[:, 0:RUNS], ALU.mult))
                link(dve.tensor_scalar(lasts[:, :], firsts[:, :], -1.0, HUGE, ALU.add, ALU.mult))
                link(dve.memset(run_top[:, 0:1], -HUGE))
                link(dve.tensor_tensor_scan(run_top[:, 1:], lasts[:, :], top[:, :], -HUGE, ALU.add, ALU.max))
                link(dve.tensor_tensor(firsts[:, :], run_top[:, 0:RUNS], lasts[:, :], ALU.add))
                dve.tensor_tensor(firsts[:, :], firsts[:, :], run_top[:, 1:], ALU.subtract)
                dve.tensor_tensor(lasts[:, :], top[:, :], run_top[:, 1:], ALU.subtract).then_inc(exp_in, 1)
                dve.wait_ge(exp_out, 2)
                link(dve.tensor_tensor(sums[:, :], sums[:, :], lasts[:, :], ALU.mult))
                link(dve.tensor_tensor_scan(lasts[:, :], firsts[:, :], sums[:, :], 0.0, ALU.mult, ALU.add))
                for g in range(2):
                    dve.wait_ge(back, g + 1)
                    for b in range(EC // 16):
                        last = dve.tensor_copy(runs[:, 16 * b:16 * b + 16, g, :], K.pair[g][:, b * BLK:b * BLK + 16 * ROW].rearrange("p (c a) -> p c a", a=ROW))
                    last.then_inc(laid, 1)

            @block.sync
            def _(sp):
                sp.wait_ge(laid, 2)
                sp.dma_start(run_rows.rearrange("(c p) a -> p c a", p=P), runs[:, :, 0:2, :].rearrange("p c s a -> p c (s a)")).then_inc(stored, 16)
                sp.wait_ge(stored, 16)


def node_scores(K, tag, count, first, end, h, asrc, adst, edge_rows, run_rows):
    nc, a = K.nc, K.a
    sem = lambda name: K.sem(f"{tag}_{name}")
    chain, loaded, idx_ready, ends_in, runs_in, exp_in, exp_out, root_in, root_out = [
        sem(n) for n in ("chain", "loaded", "idx_ready", "ends_in", "runs_in", "exp_in", "exp_out", "root_in", "root_out")]
    W, HE = 1 + EXPERTS1, HEADS * EXPERTS1
    with ExitStack() as ctx:
        sb = lambda n, shape, dt=FP32: ctx.enter_context(nc.sbuf_tensor(f"{tag}_{n}", shape, dt))
        gat = sb("gat", [P, 3, HE])
        end_idx, run_idx, run_f = sb("end_idx", [P, TILES], I32), sb("run_idx", [P, TILES], I32), sb("run_f", [P, TILES])
        has_e, has_c, stat, stat2 = [sb(n, [P, TILES]) for n in ("has_edges", "has_runs", "stat", "stat2")]
        er, cr = sb("edge", [P, TILES, HEADS, 1 + W]), sb("run", [P, TILES, 2, HEADS, W])
        top, w = sb("top", [P, TILES, HEADS]), sb("w", [P, 3, TILES, HEADS])
        agg, sq = sb("agg", [P, TILES, HE]), sb("sq", [P, TILES, HE])
        epsilon = sb("epsilon", [P, 1])
        with nc.Block() as block:
            @block.sync
            def _(sp):
                sp.dma_start(gat[:, :, :], a["L1_ffn_gat"]).then_inc(loaded, 16)

            @block.gpsimd
            def _(pool):
                pool.wait_ge(idx_ready, 2)
                for t in range(TILES):
                    pool.indirect_dma_start(out=er[:, t, :, :].rearrange("p a b -> p (a b)"), out_offset=None, in_=edge_rows,
                                            in_offset=bass.IndirectOffsetOnAxis(ap=end_idx[:, t:t + 1], axis=0)).then_inc(ends_in, 16)
                    pool.indirect_dma_start(out=cr[:, t, :, :, :].rearrange("p s a b -> p (s a b)"), out_offset=None, in_=run_rows,
                                            in_offset=bass.IndirectOffsetOnAxis(ap=run_idx[:, t:t + 1], axis=0)).then_inc(runs_in, 16)

            @block.scalar
            def _(act):
                act.wait_ge(exp_in, 1)
                act.activation(w[:, :, :, :], w[:, :, :, :], ACT.Exp).then_inc(exp_out, 1)
                act.wait_ge(root_in, 1)
                act.activation(stat2[:, :], stat2[:, :], ACT.Sqrt, bias=epsilon[:, 0:1], scale=1.0 / HE).then_inc(root_out, 1)

            @block.vector
            def _(dve):
                link = Link(dve, chain)
                link(dve.tensor_scalar(end_idx[:, :], end[:, :], -1.0, 0.0, ALU.add, ALU.max))
                link(dve.tensor_scalar(run_idx[:, :], end_idx[:, :], LANE_BITS, None, ALU.logical_shift_right))
                link(dve.tensor_copy(run_f[:, :], run_idx[:, :]))
                dve.tensor_scalar(run_idx[:, :], run_f[:, :], -1.0, 0.0, ALU.add, ALU.max).then_inc(idx_ready, 2)
                link(dve.tensor_scalar(has_e[:, :], count[:, :], 0.0, None, ALU.is_gt))
                link(dve.scalar_tensor_tensor(has_c[:, :], run_f[:, :], float(LANE), first[:, :], ALU.mult, ALU.is_gt))
                link(dve.tensor_tensor(has_c[:, :], has_c[:, :], has_e[:, :], ALU.mult))
                link(dve.tensor_tensor(w[:, 2, :, :], asrc[:, :, :], adst[:, :, :], ALU.add))
                link(dve.scalar_tensor_tensor(w[:, 2, :, :], w[:, 2, :, :], 0.2, w[:, 2, :, :], ALU.mult, ALU.max))
                dve.wait_ge(ends_in, 16 * TILES)
                dve.wait_ge(runs_in, 16 * TILES)
                wide = lambda t: t[:, :].unsqueeze(2).broadcast_to([P, TILES, HEADS])
                for n, has, src in ((0, has_e, er[:, :, :, 0]), (1, has_c, cr[:, :, 0, :, 0])):
                    link(dve.tensor_tensor(w[:, n, :, :], src, wide(has), ALU.mult))
                    link(dve.tensor_scalar(has[:, :], has[:, :], -1.0, HUGE, ALU.add, ALU.mult))
                    link(dve.tensor_tensor(w[:, n, :, :], w[:, n, :, :], wide(has), ALU.add))
                link(dve.tensor_tensor(top[:, :, :], w[:, 0, :, :], w[:, 1, :, :], ALU.max))
                link(dve.tensor_tensor(top[:, :, :], top[:, :, :], w[:, 2, :, :], ALU.max))
                dve.tensor_tensor(w[:, :, :, :], w[:, :, :, :], top[:, :, :].unsqueeze(1).broadcast_to([P, 3, TILES, HEADS]), ALU.subtract).then_inc(exp_in, 1)
                link(dve.memset(h[:, :, :, 0], 1.0))
                dve.wait_ge(exp_out, 1)
                spread = lambda n: w[:, n, :, :].unsqueeze(3).broadcast_to([P, TILES, HEADS, W])
                acc, old, own = er[:, :, :, 1:], cr[:, :, 1, :, :], h[:, :, :, :]
                link(dve.tensor_tensor(acc, acc, spread(0), ALU.mult))
                link(dve.tensor_tensor(old, old, spread(1), ALU.mult))
                link(dve.tensor_tensor(own, own, spread(2), ALU.mult))
                link(dve.tensor_tensor(acc, acc, old, ALU.add))
                link(dve.tensor_tensor(acc, acc, own, ALU.add))
                link(dve.tensor_scalar(top[:, :, :], er[:, :, :, 1], 1e-16, None, ALU.add))
                link(dve.reciprocal(top[:, :, :], top[:, :, :]))
                agg4 = agg[:, :, :].rearrange("p t (a b) -> p t a b", b=EXPERTS1)
                link(dve.tensor_tensor(agg4, er[:, :, :, 2:], top[:, :, :].unsqueeze(3).broadcast_to([P, TILES, HEADS, EXPERTS1]), ALU.mult))
                dve.wait_ge(loaded, 16)
                param = lambda n: gat[:, n, :].unsqueeze(1).broadcast_to([P, TILES, HE])
                row = lambda t: t[:, :].unsqueeze(2).broadcast_to([P, TILES, HE])
                link(dve.tensor_tensor(agg[:, :, :], agg[:, :, :], param(0), ALU.add))
                link(dve.memset(epsilon[:, :], 1e-5))
                link(dve.tensor_reduce(stat[:, :], agg[:, :, :], AX.X, ALU.add))
                link(dve.tensor_scalar(stat[:, :], stat[:, :], 1.0 / HE, None, ALU.mult))
                link(dve.tensor_tensor(agg[:, :, :], agg[:, :, :], row(stat), ALU.subtract))
                link(dve.tensor_tensor(sq[:, :, :], agg[:, :, :], agg[:, :, :], ALU.mult))
                dve.tensor_reduce(stat2[:, :], sq[:, :, :], AX.X, ALU.add).then_inc(root_in, 1)
                dve.wait_ge(root_out, 1)
                link(dve.reciprocal(stat2[:, :], stat2[:, :]))
                link(dve.tensor_tensor(agg[:, :, :], agg[:, :, :], row(stat2), ALU.mult))
                link(dve.tensor_tensor(agg[:, :, :], agg[:, :, :], param(1), ALU.mult))
                link(dve.tensor_tensor(agg[:, :, :], agg[:, :, :], param(2), ALU.add))
                link(dve.tensor_reduce(K.scores[:, :, :], agg[:, :, :].rearrange("p t (a b) -> p t b a", b=EXPERTS1), AX.X, ALU.add))
                dve.tensor_scalar(K.scores[:, :, :], K.scores[:, :, :], 1.0 / HEADS, None, ALU.mult)


def metaformer(nc, a, stages=None):
    with ExitStack() as ctx:
        K = Core(nc, a, ctx)
        start(K)
        run = {
            "l0c": lambda: (layernorm(K, "l0n", 1e-6, True), deformable(K, "l0c")),
            "l0f": lambda: (layernorm(K, "l0t", 1e-5, False),
                            moe(K, "l0f", 8, 256, "top2", ("L0_ffn_W1", "L0_ffn_b1", "L0_ffn_W2", "L0_ffn_b2", "L0_ffn_gate_w", "L0_ffn_gate_b"))),
            "l1c": lambda: (layernorm(K, "l1n", 1e-6, True),
                            conv_residual(K, "l1c", a["L1_conv_weight"], a["L1_conv_bias"])),
            "l1f": lambda: (layernorm(K, "l1t", 1e-5, False), graph_attention(K, "gat"),
                            moe(K, "l1f", 4, 256, "given", ("L1_ffn_W1", "L1_ffn_b1", "L1_ffn_W2", "L1_ffn_b2", None, None))),
            "l2c": lambda: (layernorm(K, "l2n", 1e-6, False), state_space(K, "l2c")),
            "l2f": lambda: (layernorm(K, "l2t", 1e-5, False),
                            moe(K, "l2f", 8, 128, "norm2", ("L2_ffn_w1", "L2_ffn_b1", "L2_ffn_w2", "L2_ffn_b2", "L2_ffn_router_w", None))),
            "l3c": lambda: (layernorm(K, "l3n", 1e-6, True), conv_residual(K, "l3c", a["L3_conv_W"])),
            "l3f": lambda: (layernorm(K, "l3t", 1e-5, False),
                            moe(K, "l3f", 8, 512, "first", ("L3_ffn_w1", "L3_ffn_b1", "L3_ffn_w2", "L3_ffn_b2", "L3_ffn_gate_w", "L3_ffn_gate_b"))),
        }
        for stage in stages or ("l0c", "l0f", "l1c", "l1f", "l2c", "l2f", "l3c", "l3f"):
            run[stage]()
            K.release()
        finish(K)


def layouts(v):
    f32 = np.float32
    out = {n: np.ascontiguousarray(v[n]) for n in v}
    for n in ("L1_conv_weight", "L3_conv_W"):
        out[n] = np.ascontiguousarray(v[n].transpose(1, 2, 3, 0).reshape(P, TAPS, P))
    w_off, b_off = v["L0_conv_w_off"].transpose(1, 2, 3, 0).reshape(P, TAPS, 3 * TAPS), v["L0_conv_b_off"]
    out["L0_conv_w_off"], out["L0_conv_b_off"] = np.zeros((P, TAPS, OFF_ROWS), f32), np.zeros((OFF_ROWS, 1), f32)
    y, x = np.divmod(np.arange(POS), SIDE)
    out["position_rows"] = np.zeros((OFF_ROWS, POS), f32)
    for to, src, at in ((DY_ROWS, 0, y), (DX_ROWS, TAPS, x), (MASK_ROWS, 2 * TAPS, 0 * x)):
        out["L0_conv_w_off"][:, :, to:to + TAPS] = w_off[:, :, src:src + TAPS]
        out["L0_conv_b_off"][to:to + TAPS, 0] = b_off[src:src + TAPS]
        out["position_rows"][to:to + TAPS] = at
    q = np.arange(P)
    out["neg_qy"] = -(4.0 * np.arange(CHUNKS)[None, :] + q[:, None] // SIDE).astype(f32)
    out["neg_qx"] = -(q[:, None] % SIDE).astype(f32)
    out["L0_conv_w_conv"] = np.ascontiguousarray(v["L0_conv_w_conv"].reshape(P, TAPS, P).transpose(2, 1, 0).reshape(P, TAPS * P))
    inner = lambda w: np.ascontiguousarray(w.reshape(HALVES, P, -1).transpose(1, 0, 2))
    w_x = v["L2_conv_W_x"]
    bc = w_x[:, DT_RANK:]
    out["L2_conv_W_x"] = inner(np.concatenate([bc, bc, bc, w_x[:, :DT_RANK]], axis=1))
    for n in ("L2_conv_W_out", "L2_conv_conv_w", "L2_conv_A_log"):
        out[n] = inner(v[n])
    for n in ("L2_conv_conv_b", "L2_conv_b_dt", "L2_conv_D"):
        out[n] = inner(v[n])[:, :, 0].copy()
    out["L1_ffn_att"] = np.broadcast_to(np.stack([v["L1_ffn_att_src"].reshape(-1), v["L1_ffn_att_dst"].reshape(-1)]), (P, 2, 16)).copy()
    out["L1_ffn_gat"] = np.broadcast_to(np.stack([v["L1_ffn_b_gat"], v["L1_ffn_ln_gamma"], v["L1_ffn_ln_beta"]]), (P, 3, 16)).copy()
    out["sort_sign"] = (1.0 - 2.0 * ((np.arange(P)[:, None] >> np.arange(LANE_BITS)) & 1)).astype(f32)
    out["column_number"] = np.broadcast_to(np.arange(P, dtype=f32), (P, P)).copy()
    out["strictly_below"] = np.triu(np.ones((P, P), f32), 1)
    out["L1_conv_bias"] = v["L1_conv_bias"].reshape(P, 1)
    for n in ("L0_ffn_b1", "L1_ffn_b1", "L2_ffn_b1", "L3_ffn_b1"):
        out[n] = np.ascontiguousarray(v[n].reshape(-1, P).T)
    out["L2_ffn_router_w"] = np.ascontiguousarray(v["L2_ffn_router_w"].T)
    for n in ("L0_ffn_gate_b", "L3_ffn_gate_b"):
        out[n] = np.broadcast_to(v[n], (P, v[n].size)).copy()
    out["identity"] = np.eye(P, dtype=f32)
    for e in (4, 8):
        out[f"index{e}"] = np.broadcast_to(np.arange(e, dtype=f32) - 64, (P, TILES, e)).copy()
    return out


def kernel(**inputs):
    import concourse.bacc as _bacc
    from concourse.bass_utils import run_bass_kernel_spmd as _run

    nc = _bacc.Bacc("TRN2", target_bir_lowering=False, num_devices=1)
    arrays = layouts({k: np.asarray(x) for k, x in inputs.items()})
    a = {k: nc.dram_tensor("in_" + k, x.shape, mybir.dt.from_np(x.dtype), kind="ExternalInput").ap() for k, x in arrays.items()}
    a["out"] = nc.dram_tensor("out_dram", (IMAGES, P, SIDE, SIDE), FP32, kind="ExternalOutput").ap()
    metaformer(nc, a)
    r = _run(nc, [{"in_" + k: x for k, x in arrays.items()}], core_ids=[0])
    return r.results[0]["out_dram"]
```

```python
from contextlib import ExitStack

import numpy as np

import concourse.bass as bass
from concourse import mybir

FP32 = mybir.dt.float32
I32 = mybir.dt.int32
U32 = mybir.dt.uint32
BF16 = mybir.dt.bfloat16
ALU = mybir.AluOpType
ACT = mybir.ActivationFunctionType
AX = mybir.AxisListType

P = 128
IMAGES, SIDE = 8, 32
POS = SIDE * SIDE
TOKENS = IMAGES * POS
BLK = 512
BLOCKS = TOKENS // BLK
TILES = TOKENS // P
PADDED = SIDE + 2
TAPS = 9
HUGE = 1.0e30


class Link:

    def __init__(self, eng, sem, base=0, apart=False):
        self.eng, self.sem, self.base, self.n, self.apart = eng, sem, base, 0, apart

    def __call__(self, ins):
        self.n += 1
        ins.then_inc(self.sem, 1)
        self.eng.wait_ge(self.sem, self.base + self.n)
        if self.apart:
            self.eng.nop(nofuse=True)


class Core:

    def __init__(self, nc, a, ctx):
        self.nc, self.a, self.ctx, self.sems = nc, a, ctx, []
        self.x = ctx.enter_context(nc.sbuf_tensor("x_act", [P, TOKENS], FP32))
        self.pad = ctx.enter_context(nc.sbuf_tensor("normed", [P, IMAGES * PADDED * PADDED], FP32))
        self.ident = ctx.enter_context(nc.sbuf_tensor("identity", [P, P], FP32))
        self.ones = ctx.enter_context(nc.sbuf_tensor("ones_row", [1, P], FP32))
        self.mean = ctx.enter_context(nc.sbuf_tensor("mean_matrix", [P, P], FP32))
        self.scores = ctx.enter_context(nc.sbuf_tensor("scores", [P, TILES, 4], FP32))
        self.pair = [ctx.enter_context(nc.psum_tensor(f"banks{i}", [P, 2 * BLK], FP32)) for i in range(4)]
        self.bank = [self.pair[i // 2][:, (i % 2) * BLK:(i % 2 + 1) * BLK] for i in range(8)]

    def sem(self, name):
        self.sems.append(self.nc.alloc_semaphore(name=name))
        return self.sems[-1]

    def release(self):
        self.nc.clear_and_free_semaphores(self.sems)
        self.nc.all_engine_barrier()
        self.sems = []

    def image(self, b):
        return self.pad[:, :].rearrange("p (b y x) -> p b y x", b=IMAGES, y=PADDED)[:, b, :, :]


def start(K):
    nc, a = K.nc, K.a
    x_in, const = K.sem("x_in"), K.sem("constants_in")
    with nc.Block() as block:
        @block.sync
        def _(sp):
            for b in range(IMAGES):
                sp.dma_start(K.x[:, b * POS:(b + 1) * POS], a["x"][b].rearrange("c y x -> c (y x)")).then_inc(x_in, 16)
            sp.dma_start(K.ident[:, :], a["identity"]).then_inc(const, 16)
            sp.wait_ge(x_in, 16 * IMAGES)
            sp.wait_ge(const, 16)

        @block.vector
        def _(dve):
            dve.memset(K.mean[:, :], 1.0 / P)
            dve.memset(K.ones[:, :], 1.0)


def finish(K):
    nc, a = K.nc, K.a
    stored = K.sem("stored")
    with nc.Block() as block:
        @block.sync
        def _(sp):
            for b in range(IMAGES):
                sp.dma_start(a["out"][b].rearrange("c y x -> c (y x)"), K.x[:, b * POS:(b + 1) * POS]).then_inc(stored, 16)
            sp.wait_ge(stored, 16 * IMAGES)


def layernorm(K, tag, eps, padded):
    nc = K.nc
    sem = lambda name: K.sem(f"{tag}_{name}")
    mean_ready, centred, squared, var_ready, row_ready = sem("mean_ready"), sem("centred"), sem("squared"), sem("var_ready"), sem("row_ready")
    dealt, rooted, inverted, gathered, spread, normed, zeroed = (
        sem("dealt"), sem("rooted"), sem("inverted"), sem("gathered"), sem("spread"), sem("normed"), sem("zeroed"))

    def view(i, h):
        if padded:
            return K.image(i)[:, 1 + 16 * h:17 + 16 * h, 1:1 + SIDE]
        return K.pad[:, bass.ds(i * POS + h * BLK, BLK)]

    def grid(t):
        return t.rearrange("p (y x) -> p y x", x=SIDE) if padded else t

    with ExitStack() as ctx:
        sq = [ctx.enter_context(nc.sbuf_tensor(f"{tag}_sq{h}", [P, BLK], FP32)) for h in range(2)]
        row = ctx.enter_context(nc.sbuf_tensor(f"{tag}_row", [1, TOKENS], FP32))
        deal = ctx.enter_context(nc.sbuf_tensor(f"{tag}_deal", [P, TILES + 1], FP32))
        mean, var, scale = K.bank[0:2], K.bank[2:4], K.bank[4:6]
        with nc.Block() as block:
            @block.sync
            def _(sp):
                sp.wait_ge(row_ready, BLOCKS)
                sp.dma_start(deal[:, 0:TILES], row[:, :].rearrange("o (p t) -> o p t", p=P)).then_inc(dealt, 16)
                sp.wait_ge(inverted, 1)
                sp.dma_start(row[:, :].rearrange("o (p t) -> o p t", p=P), deal[:, 0:TILES]).then_inc(gathered, 16)

            @block.tensor
            def _(pe):
                with pe.Fori(0, IMAGES) as i:
                    for h in range(2):
                        pe.matmul(mean[h][:, :], K.mean[:, :], K.x[:, bass.ds(i * POS + h * BLK, BLK)], start=True, stop=True).then_inc(mean_ready, 1)
                    for h in range(2):
                        pe.wait_ge(squared, i * 2 + h + 1)
                        pe.matmul(var[h][0:1, :], K.mean[:, 0:1], sq[h][:, :], start=True, stop=True).then_inc(var_ready, 1)
                pe.wait_ge(gathered, 16)
                with pe.Fori(0, IMAGES) as i:
                    for h in range(2):
                        pe.wait_ge(normed, i * 2 + h + 1)
                        pe.nop()
                        pe.matmul(scale[h][:, :], K.ones[0:1, :], row[:, bass.ds(i * POS + h * BLK, BLK)], start=True, stop=True).then_inc(spread, 1)

            @block.scalar
            def _(act):
                with act.Fori(0, IMAGES) as i:
                    for h in range(2):
                        act.wait_ge(centred, i * 2 + h + 1)
                        act.activation(grid(sq[h][:, :]), view(i, h), ACT.Square).then_inc(squared, 1)
                    for h in range(2):
                        act.wait_ge(var_ready, i * 2 + h + 1)
                        act.activation(row[:, bass.ds(i * POS + h * BLK, BLK)], var[h][0:1, :], ACT.Copy).then_inc(row_ready, 1)
                act.wait_ge(dealt, 16)
                act.wait_ge(zeroed, 1)
                act.activation(deal[:, 0:TILES], deal[:, 0:TILES], ACT.Sqrt, bias=deal[:, TILES:TILES + 1]).then_inc(rooted, 1)

            @block.vector
            def _(dve):
                dve.memset(deal[:, TILES:TILES + 1], eps).then_inc(zeroed, 1)
                if padded:
                    dve.memset(K.pad[:, :], 0.0).then_inc(zeroed, 1)
                    dve.wait_ge(zeroed, 2)
                dve.sem_inc(normed, 2)
                with dve.Fori(0, IMAGES) as i:
                    for h in range(2):
                        dve.wait_ge(mean_ready, i * 2 + h + 1)
                        dve.tensor_tensor(view(i, h), grid(K.x[:, bass.ds(i * POS + h * BLK, BLK)]), grid(mean[h][:, :]), ALU.subtract).then_inc(centred, 1)
                dve.wait_ge(rooted, 1)
                dve.reciprocal(deal[:, 0:TILES], deal[:, 0:TILES]).then_inc(inverted, 1)
                with dve.Fori(0, IMAGES) as i:
                    for h in range(2):
                        dve.wait_ge(spread, i * 2 + h + 1)
                        dve.tensor_tensor(view(i, h), view(i, h), grid(scale[h][:, :]), ALU.mult).then_inc(normed, 1)


def conv_taps(pe, K, i, h, out, weights):
    for t in range(TAPS):
        ky, kx = t // 3, t % 3
        rhs = K.image(i)[:, 16 * h + ky:16 * h + ky + 16, kx:kx + SIDE]
        last = pe.matmul(out, weights[:, t, :], rhs, start=(t == 0), stop=(t == TAPS - 1))
    return last


def conv_residual(K, tag, weight, bias=None):
    nc = K.nc
    loaded, w_ready, conv_done, added = K.sem(tag + "_w_loaded"), K.sem(tag + "_w_ready"), K.sem(tag + "_conv_done"), K.sem(tag + "_added")
    chain = K.sem(tag + "_chain")
    extreme, reduced = K.sem(tag + "_extreme"), K.sem(tag + "_reduced")
    with ExitStack() as ctx:
        w = ctx.enter_context(nc.sbuf_tensor(tag + "_w", [P, TAPS, P], FP32))
        bt = ctx.enter_context(nc.sbuf_tensor(tag + "_bias", [P, 1], FP32))
        s = ctx.enter_context(nc.sbuf_tensor(tag + "_scales", [P, 8], FP32))
        acc = K.bank[0:2]
        with nc.Block() as block:
            @block.sync
            def _(sp):
                sp.dma_start(w[:, :, :], weight).then_inc(loaded, 16)
                if bias is not None:
                    sp.dma_start(bt[:, :], bias).then_inc(loaded, 16)

            @block.gpsimd
            def _(pool):
                if bias is not None:
                    pool.wait_ge(extreme, 1)
                    pool.partition_all_reduce(s[:, 2:4], s[:, 0:2], P, bass.bass_isa.ReduceOp.max).then_inc(reduced, 1)

            @block.tensor
            def _(pe):
                pe.wait_ge(w_ready, 1)
                with pe.Fori(0, IMAGES) as i:
                    for h in range(2):
                        pe.wait_ge(added, i * 2 + h + 1)
                        conv_taps(pe, K, i, h, acc[h][:, :], w).then_inc(conv_done, 1)

            @block.vector
            def _(dve):
                dve.wait_ge(loaded, 16 if bias is None else 32)
                if bias is None:
                    dve.memset(bt[:, :], 0.0).then_inc(w_ready, 1)
                    dve.wait_ge(w_ready, 1)
                else:
                    link = Link(dve, chain)
                    flat = w[:, :, :].rearrange("p t o -> p (t o)")
                    link(dve.tensor_reduce(s[:, 0:1], flat, AX.X, ALU.max))
                    link(dve.tensor_reduce(s[:, 1:2], flat, AX.X, ALU.min))
                    dve.tensor_scalar(s[:, 1:2], s[:, 1:2], -1.0, None, ALU.mult).then_inc(extreme, 1)
                    dve.wait_ge(reduced, 1)
                    magic = 12582912.0
                    link(dve.tensor_tensor(s[:, 4:5], s[:, 2:3], s[:, 3:4], ALU.add))
                    link(dve.tensor_scalar(s[:, 4:5], s[:, 4:5], 1.0 / 255.0, None, ALU.mult))
                    link(dve.reciprocal(s[:, 6:7], s[:, 4:5]))
                    link(dve.tensor_tensor(s[:, 5:6], s[:, 2:3], s[:, 6:7], ALU.mult))
                    link(dve.tensor_scalar(s[:, 5:6], s[:, 5:6], -1.0, 255.0, ALU.mult, ALU.add))
                    link(dve.tensor_scalar(s[:, 5:6], s[:, 5:6], 0.0, 255.0, ALU.max, ALU.min))
                    link(dve.tensor_scalar(s[:, 5:6], s[:, 5:6], magic, -magic, ALU.add, ALU.add))
                    link(dve.tensor_scalar(flat, flat, s[:, 6:7], s[:, 5:6], ALU.mult, ALU.add))
                    link(dve.tensor_scalar(flat, flat, 0.0, 255.0, ALU.max, ALU.min))
                    link(dve.tensor_scalar(flat, flat, magic, -magic, ALU.add, ALU.add))
                    dve.tensor_scalar(flat, flat, s[:, 5:6], s[:, 4:5], ALU.subtract, ALU.mult).then_inc(w_ready, 1)
                dve.sem_inc(added, 2)
                with dve.Fori(0, IMAGES) as i:
                    for h in range(2):
                        dve.wait_ge(conv_done, i * 2 + h + 1)
                        blk = K.x[:, bass.ds(i * POS + h * BLK, BLK)]
                        dve.scalar_tensor_tensor(blk, acc[h][:, :], bt[:, 0:1], blk, ALU.add, ALU.add).then_inc(added, 1)


MASK_ROWS, DY_ROWS, DX_ROWS, OFF_ROWS = 0, 32, 64, 96
CHUNKS = POS // P


def deformable(K, tag):
    nc, a = K.nc, K.a
    sem = lambda name: K.sem(f"{tag}_{name}")
    STEPS = 2 * TAPS
    LAG = 2
    ZS = 3
    ZW = TAPS * P // ZS
    ZN = CHUNKS * ZS
    loaded = sem("loaded")
    img_ready, off_made, off_ready, sig_ready = sem("img_ready"), sem("off_made"), sem("off_ready"), sem("sig_ready")
    z_made, z_copied = sem("z_made"), [sem("z_copied_scalar"), sem("z_copied_vector")]
    bc_ready, ax_ready, abs_done, masked = sem("bc_ready"), sem("ax_ready"), sem("abs_done"), sem("masked")
    coarse_ready, rest_ready, middle_ready, fine_ready, grouped, pick_ready = (
        sem("coarse_ready"), sem("rest_ready"), sem("middle_ready"), sem("fine_ready"), sem("grouped"), sem("pick_ready"))
    b_ready, used, added, chain = sem("b_ready"), sem("used"), sem("added"), sem("chain")
    with ExitStack() as ctx:
        sb = lambda n, shape: ctx.enter_context(nc.sbuf_tensor(f"{tag}_{n}", shape, FP32))
        w_off, w_conv = sb("w_off", [P, TAPS, OFF_ROWS]), sb("w_conv", [P, TAPS * P])
        b_off, base = sb("b_off", [OFF_ROWS, 1]), sb("base", [OFF_ROWS, POS])
        neg_qy, neg_qx = sb("neg_qy", [P, CHUNKS]), sb("neg_qx", [P, 1])
        img, off, z = sb("img", [P, POS]), sb("off", [OFF_ROWS, POS]), sb("z", [P, CHUNKS, TAPS * P])
        sb16 = lambda n, shape: ctx.enter_context(nc.sbuf_tensor(f"{tag}_{n}", shape, BF16))
        rest, rows = sb("rest", [OFF_ROWS, POS]), sb16("rows", [3 * 32, 3, POS])
        parts = [sb16(n, [OFF_ROWS, POS]) for n in ("coarse", "middle", "fine")]
        pick = sb16("pick", [3 * 32, 32])
        hats = [sb(f"hats{j}", [P, CHUNKS, BLK]) for j in range(3)]
        hx = [sb(f"hx{j}", [P, BLK]) for j in range(2)]
        hxm = [sb(f"hxm{j}", [P, BLK]) for j in range(2)]
        acc, dy_bank, dx_bank, m_bank = K.bank[0:2], K.bank[2:4], K.bank[4:6], K.bank[6]
        off_bank = [K.bank[7], K.bank[6]]
        z_bank = K.bank[2:6]
        with nc.Block() as block:
            @block.sync
            def _(sp):
                for to, src in ((w_off, "L0_conv_w_off"), (w_conv, "L0_conv_w_conv")):
                    sp.dma_start(to[:, :, :] if to is w_off else to[:, :], a[src]).then_inc(loaded, 16)
                for to, src in ((b_off, "L0_conv_b_off"), (base, "position_rows"), (neg_qy, "neg_qy"), (neg_qx, "neg_qx")):
                    sp.dma_start(to[:, :], a[src]).then_inc(loaded, 16)
                with sp.Fori(0, IMAGES) as i:
                    sp.wait_ge(fine_ready, i + 1)
                    sp.wait_ge(used, i * STEPS + 3)
                    for q in range(3):
                        for m in range(3):
                            sp.dma_start(rows[32 * m:32 * m + 32, q, :], parts[m][32 * q:32 * q + 32, :]).then_inc(grouped, 16)

            @block.tensor
            def _(pe):
                pe.wait_ge(loaded, 96)
                pe.wait_ge(pick_ready, 3)
                pe.sem_inc(used, 3)
                with pe.Fori(0, IMAGES) as i:
                    pe.wait_ge(abs_done, i * STEPS + 2)
                    pe.wait_ge(masked, i * STEPS)
                    pe.nop()
                    for h in range(2):
                        for t in range(TAPS):
                            rhs = K.image(i)[:, 16 * h + t // 3:16 * h + t // 3 + 16, t % 3:t % 3 + SIDE]
                            last = pe.matmul(off_bank[h][0:OFF_ROWS, :], w_off[:, t, :], rhs, start=(t == 0), stop=(t == TAPS - 1))
                        last.then_inc(off_made, 1)
                    pe.wait_ge(img_ready, i + 1)
                    for k in range(ZN):
                        if k >= 4:
                            pe.wait_ge(z_copied[k % 2], i * (ZN // 2) + k // 2 - 1)
                        c, j = k // ZS, k % ZS
                        pe.matmul(z_bank[k % 4][:, 0:ZW], img[:, c * P:(c + 1) * P], w_conv[:, j * ZW:(j + 1) * ZW], start=True, stop=True).then_inc(z_made, 1)
                    for j in range(2):
                        pe.wait_ge(z_copied[j], (i + 1) * (ZN // 2))
                    pe.wait_ge(grouped, (i + 1) * (16 * 9))
                    for s in range(STEPS + LAG):
                        if s < STEPS:
                            h, t = s // TAPS, s % TAPS
                            cols = slice(h * BLK, (h + 1) * BLK)
                            pe.wait_ge(abs_done, i * STEPS + s + 1)
                            pe.wait_ge(masked, i * STEPS + s)
                            for row, bank in ((DX_ROWS, dx_bank[s % 2]), (MASK_ROWS, m_bank), (DY_ROWS, dy_bank[s % 2])):
                                last = pe.matmul(bank[:, :], pick[:, t:t + 1].broadcast_to([3 * 32, P]), rows[:, row // 32, cols], start=True, stop=True)
                            last.then_inc(bc_ready, 1)
                        if s >= LAG:
                            m = s - LAG
                            h, t = m // TAPS, m % TAPS
                            if t == 0:
                                pe.wait_ge(added, i * 2 + h + 1)
                            pe.wait_ge(b_ready, i * STEPS + m + 1)
                            for c in range(CHUNKS):
                                last = pe.matmul(acc[h][:, :], z[:, c, t * P:(t + 1) * P], hats[m % 3][:, c, :], start=(t == 0 and c == 0), stop=(t == TAPS - 1 and c == CHUNKS - 1))
                            last.then_inc(used, 1)

            @block.scalar
            def _(act):
                act.wait_ge(loaded, 96)
                act.sem_inc(abs_done, 2)
                with act.Fori(0, IMAGES) as i:
                    act.wait_ge(off_ready, i * 2 + 2)
                    act.activation(off[MASK_ROWS:MASK_ROWS + TAPS, :], off[MASK_ROWS:MASK_ROWS + TAPS, :], ACT.Sigmoid).then_inc(sig_ready, 1)
                    act.wait_ge(sig_ready, i + 1)
                    act.wait_ge(grouped, i * (16 * 9))
                    act.copy(parts[0][:, :], off[:, :]).then_inc(coarse_ready, 1)
                    for k in range(0, ZN, 2):
                        if k == ZN // 4:
                            act.wait_ge(rest_ready, i + 1)
                            act.copy(parts[1][:, :], rest[:, :]).then_inc(middle_ready, 1)
                        c, j = k // ZS, k % ZS
                        act.wait_ge(z_made, i * ZN + k + 1)
                        act.copy(z[:, c, j * ZW:(j + 1) * ZW], z_bank[k % 4][:, 0:ZW]).then_inc(z_copied[0], 1)
                    for s in range(STEPS):
                        act.wait_ge(bc_ready, i * STEPS + s + 1)
                        act.wait_ge(used, i * STEPS + s + 1)
                        act.activation(hx[s % 2][:, :], dx_bank[s % 2][:, :], ACT.Abs, bias=neg_qx[:, 0:1]).then_inc(ax_ready, 1)
                        for c in range(CHUNKS):
                            last = act.activation(hats[s % 3][:, c, :], dy_bank[s % 2][:, :], ACT.Abs, bias=neg_qy[:, c:c + 1])
                        last.then_inc(abs_done, 1)

            @block.vector
            def _(dve):
                dve.wait_ge(loaded, 96)
                dve.sem_inc(added, 2)
                for m in range(3):
                    dve.tensor_copy(pick[32 * m:32 * m + 32, :], K.ident[32 * m:32 * m + 32, 32 * m:32 * m + 32]).then_inc(pick_ready, 1)

                def residual(i, h):
                    dve.wait_ge(used, i * STEPS + (h + 1) * TAPS + 3)
                    blk = K.x[:, bass.ds(i * POS + h * BLK, BLK)]
                    dve.tensor_tensor(blk, blk, acc[h][:, :], ALU.add).then_inc(added, 1)

                with dve.Fori(0, IMAGES) as i:
                    link = Link(dve, chain, i * 2 * STEPS)
                    dve.tensor_copy(img[:, :].rearrange("p (y x) -> p y x", x=SIDE), K.image(i)[:, 1:1 + SIDE, 1:1 + SIDE]).then_inc(img_ready, 1)
                    for h in range(2):
                        cols = slice(h * BLK, (h + 1) * BLK)
                        dve.wait_ge(off_made, i * 2 + h + 1)
                        dve.scalar_tensor_tensor(off[:, cols], off_bank[h][0:OFF_ROWS, :], b_off[:, 0:1], base[:, cols], ALU.add, ALU.add).then_inc(off_ready, 1)
                    dve.wait_ge(coarse_ready, i + 1)
                    dve.tensor_tensor(rest[:, :], off[:, :], parts[0][:, :], ALU.subtract).then_inc(rest_ready, 1)
                    dve.wait_ge(middle_ready, i + 1)
                    dve.tensor_tensor(parts[2][:, :], rest[:, :], parts[1][:, :], ALU.subtract).then_inc(fine_ready, 1)
                    for k in range(1, ZN, 2):
                        c, j = k // ZS, k % ZS
                        dve.wait_ge(z_made, i * ZN + k + 1)
                        dve.tensor_copy(z[:, c, j * ZW:(j + 1) * ZW], z_bank[k % 4][:, 0:ZW]).then_inc(z_copied[1], 1)
                    for s in range(STEPS):
                        j = s % 2
                        dve.wait_ge(ax_ready, i * STEPS + s + 1)
                        link(dve.tensor_scalar(hx[j][:, :], hx[j][:, :], -1.0, 0.0, ALU.add, ALU.min))
                        dve.wait_ge(b_ready, i * STEPS + s)
                        dve.tensor_tensor(hxm[j][:, :], hx[j][:, :], m_bank[:, :], ALU.mult).then_inc(masked, 1)
                        dve.wait_ge(masked, i * STEPS + s + 1)
                        dve.wait_ge(abs_done, i * STEPS + s + 3)
                        link(dve.tensor_scalar(hats[s % 3][:, :, :], hats[s % 3][:, :, :], -1.0, 0.0, ALU.add, ALU.min))
                        dve.tensor_tensor(hats[s % 3][:, :, :], hats[s % 3][:, :, :], hxm[j][:, :].unsqueeze(1).broadcast_to([P, CHUNKS, BLK]), ALU.mult).then_inc(b_ready, 1)
                        if s == TAPS:
                            residual(i, 0)
                    residual(i, 1)


def first_match(dve, link, hot, v, top, idx, tmp, m):
    n = v.shape[2]
    wide = lambda t: t.unsqueeze(2).broadcast_to([P, v.shape[1], n])
    link(dve.tensor_tensor(tmp, v, wide(top), ALU.is_equal))
    link(dve.tensor_tensor(tmp, tmp, idx, ALU.mult))
    link(dve.tensor_reduce(m, tmp, AX.X, ALU.min))
    link(dve.tensor_tensor(hot, idx, wide(m), ALU.is_equal))


def moe(K, tag, E, F, kind, names):
    nc, a = K.nc, K.a
    C = F // P
    STEPS = E * C
    w1d, b1d, w2d, b2d, gwd, gbd = [a[n] if n else None for n in names]
    s = lambda n: K.sem(f"{tag}_{n}")
    loaded = s("loaded")
    R = 3 * E
    with ExitStack() as ctx:
        sb = lambda n, shape, dt=FP32: ctx.enter_context(nc.sbuf_tensor(f"{tag}_{n}", shape, dt))
        gT, g16 = sb("gT", [R, TOKENS]), sb("g16", [R, TOKENS], BF16)
        L = sb("L", [P, TILES, E])
        with ExitStack() as inner:
            sc = lambda n, shape: inner.enter_context(nc.sbuf_tensor(f"{tag}_{n}", shape, FP32))
            gw, gb = sc("gw", [P, E]), sc("gb", [P, E])
            idx, tmp, hot1, hot2, p, p2 = [sc(n, [P, TILES, E]) for n in ("idx", "tmp", "hot1", "hot2", "p", "p2")]
            m, m1, m2, den = [sc(n, [P, TILES]) for n in ("m", "m1", "m2", "den")]
            parts = sc("parts", [P, TILES, 3, E])
            coarse, middle = [inner.enter_context(nc.sbuf_tensor(f"{tag}_{n}", [P, TILES, E], BF16)) for n in ("coarse", "middle")]
            hot3 = sc("hot3", [P, TILES, 3, E]) if kind == "first" else None
            hotT = sc("hotT", [R, TOKENS]) if kind == "first" else None
            zero = sc("zero", [R, 1]) if kind == "first" else None
            logits, shifted, exped, chain = s("logits"), s("shifted"), s("exped"), s("chain")
            gated, turned, copied, idx_in = s("gated"), s("turned"), s("copied"), s("idx_in")
            wide = lambda t: t[:, :].unsqueeze(2).broadcast_to([P, TILES, E])
            turns = [(parts, gT)] + ([(hot3, hotT)] if kind == "first" else [])
            with nc.Block() as block:
                @block.sync
                def _(sp):
                    if kind != "given":
                        sp.dma_start(gw[:, :], gwd).then_inc(loaded, 16)
                    sp.dma_start(idx[:, :, :], a[f"index{E}"]).then_inc(idx_in, 16)
                    if gbd is not None:
                        sp.dma_start(gb[:, :], gbd).then_inc(idx_in, 16)

                @block.tensor
                def _(pe):
                    if kind != "given":
                        pe.wait_ge(loaded, 16)
                        for t in range(TILES):
                            last = pe.matmul(K.bank[0][:, t * E:(t + 1) * E], K.pad[:, t * P:(t + 1) * P], gw[:, :], start=True, stop=True)
                        last.then_inc(logits, 1)
                    pe.wait_ge(gated, 1)
                    n = 0
                    for src, _ in turns:
                        for g in range(BLOCKS):
                            if n >= 2:
                                pe.wait_ge(copied, n - 1)
                            for t in range(4):
                                last = pe.transpose(K.bank[1 + n % 2][0:R, t * P:(t + 1) * P], src[:, 4 * g + t, :, :].rearrange("p m e -> p (m e)"), K.ident[:, :])
                            last.then_inc(turned, 1)
                            n += 1

                @block.scalar
                def _(act):
                    act.wait_ge(shifted, 1)
                    act.activation(p[:, :, :], tmp[:, :, :], ACT.Exp).then_inc(exped, 1)
                    n = 0
                    for _, dst in turns:
                        for g in range(BLOCKS):
                            act.wait_ge(turned, n + 1)
                            act.copy(dst[:, g * BLK:(g + 1) * BLK], K.bank[1 + n % 2][0:R, :]).then_inc(copied, 1)
                            n += 1

                @block.vector
                def _(dve):
                    link = Link(dve, chain)
                    v3 = lambda t: t[:, :, :]
                    dve.wait_ge(idx_in, 32 if gbd is not None else 16)
                    if kind == "given":
                        link(dve.tensor_copy(v3(L), K.scores[:, :, :]))
                        link(dve.tensor_reduce(m1[:, :], v3(L), AX.X, ALU.max))
                        first_match(dve, link, v3(hot1), v3(L), m1[:, :], v3(idx), v3(tmp), m[:, :])
                        link(dve.scalar_tensor_tensor(v3(p2), v3(hot1), -HUGE, v3(L), ALU.mult, ALU.add))
                        link(dve.tensor_reduce(m2[:, :], v3(p2), AX.X, ALU.max))
                        first_match(dve, link, v3(hot2), v3(p2), m2[:, :], v3(idx), v3(tmp), m[:, :])
                        dve.tensor_tensor(tmp[:, :, :], v3(L), wide(m1), ALU.subtract).then_inc(shifted, 1)
                        dve.wait_ge(exped, 1)
                        link(dve.tensor_tensor(v3(hot1), v3(hot1), v3(hot2), ALU.add))
                        link(dve.tensor_tensor(v3(p), v3(p), v3(hot1), ALU.mult))
                        link(dve.tensor_reduce(den[:, :], v3(p), AX.X, ALU.add))
                        link(dve.reciprocal(den[:, :], den[:, :]))
                        link(dve.tensor_tensor(v3(L), v3(p), wide(den), ALU.mult))
                    else:
                        dve.wait_ge(logits, 1)
                        ps = K.bank[0][:, 0:TILES * E].rearrange("p (t e) -> p t e", e=E)
                        if gbd is not None:
                            link(dve.tensor_tensor(v3(L), ps, gb[:, :].unsqueeze(1).broadcast_to([P, TILES, E]), ALU.add))
                        else:
                            link(dve.tensor_copy(v3(L), ps))
                        link(dve.tensor_reduce(m1[:, :], v3(L), AX.X, ALU.max))
                        dve.tensor_tensor(tmp[:, :, :], v3(L), wide(m1), ALU.subtract).then_inc(shifted, 1)
                        dve.wait_ge(exped, 1)
                        link(dve.tensor_reduce(den[:, :], v3(p), AX.X, ALU.add))
                        link(dve.reciprocal(den[:, :], den[:, :]))
                        link(dve.tensor_tensor(v3(p), v3(p), wide(den), ALU.mult))
                        link(dve.tensor_reduce(m1[:, :], v3(p), AX.X, ALU.max))
                        first_match(dve, link, v3(hot1), v3(p), m1[:, :], v3(idx), v3(tmp), m[:, :])
                        if kind == "first":
                            link(dve.tensor_tensor(v3(L), v3(p), v3(hot1), ALU.mult))
                        else:
                            link(dve.scalar_tensor_tensor(v3(p2), v3(hot1), -2.0, v3(p), ALU.mult, ALU.add))
                            link(dve.tensor_reduce(m2[:, :], v3(p2), AX.X, ALU.max))
                            first_match(dve, link, v3(hot2), v3(p2), m2[:, :], v3(idx), v3(tmp), m[:, :])
                            link(dve.tensor_tensor(v3(hot1), v3(hot1), v3(hot2), ALU.add))
                            if kind == "top2":
                                link(dve.tensor_tensor(v3(L), v3(p), v3(hot1), ALU.mult))
                            else:
                                link(dve.tensor_tensor(v3(p), v3(p), v3(hot1), ALU.mult))
                                link(dve.tensor_tensor(den[:, :], m1[:, :], m2[:, :], ALU.add))
                                link(dve.tensor_scalar(den[:, :], den[:, :], 1e-12, None, ALU.max))
                                link(dve.reciprocal(den[:, :], den[:, :]))
                                link(dve.tensor_tensor(v3(L), v3(p), wide(den), ALU.mult))
                    link(dve.tensor_copy(coarse[:, :, :], v3(L)))
                    link(dve.tensor_tensor(v3(tmp), v3(L), coarse[:, :, :], ALU.subtract))
                    link(dve.tensor_copy(middle[:, :, :], v3(tmp)))
                    dve.tensor_copy(parts[:, :, 0, :], coarse[:, :, :])
                    dve.tensor_copy(parts[:, :, 1, :], middle[:, :, :])
                    if kind == "first":
                        dve.tensor_copy(hot3[:, :, :, :], hot1[:, :, :].unsqueeze(2).broadcast_to([P, TILES, 3, E]))
                    dve.tensor_tensor(parts[:, :, 2, :], v3(tmp), middle[:, :, :], ALU.subtract).then_inc(gated, 1)
                    if kind != "first":
                        for g in range(BLOCKS):
                            dve.wait_ge(copied, g + 1)
                            dve.tensor_copy(g16[:, g * BLK:(g + 1) * BLK], gT[:, g * BLK:(g + 1) * BLK])
                    if kind == "first":
                        capacity = float(-(-5 * TOKENS // (4 * E)))
                        link(dve.memset(zero[:, :], 0.0))
                        dve.wait_ge(copied, 2 * BLOCKS)
                        link(dve.tensor_tensor_scan(hotT[:, :], hotT[:, :], zero[:, :].broadcast_to([R, TOKENS]), 0.0, ALU.add, ALU.add))
                        link(dve.scalar_tensor_tensor(gT[:, :], hotT[:, :], capacity, gT[:, :], ALU.is_le, ALU.mult))
                        dve.tensor_copy(g16[:, :], gT[:, :])

        w1, w2 = sb("w1", [P, E, F]), sb("w2", [P, STEPS, P])
        b1, b2 = sb("b1", [P, STEPS]), sb("b2", [R, P])
        pick32, pick = sb("pick32", [R, E]), sb("pick", [R, E], BF16)
        hid = [ctx.enter_context(nc.sbuf_tensor(f"{tag}_hidden{j}", [P, BLK], FP32)) for j in range(3)]
        hg = [ctx.enter_context(nc.sbuf_tensor(f"{tag}_gated{j}", [P, BLK], FP32)) for j in range(3)]
        fix = [ctx.enter_context(nc.sbuf_tensor(f"{tag}_fix{j}", [P, BLK], FP32)) for j in range(3)]
        gate_bank, h_bank, y_bank = [K.bank[0], K.bank[1], K.bank[7]], K.bank[2:5], K.bank[5:7]
        gate_spread, hid_ready, act_done, hid_gated, y_ready, added, ychain = (
            s("gate_spread"), s("hidden_ready"), s("activated"), s("hidden_gated"), s("y_ready"), s("added"), s("ychain"))
        wload, pick_in, pick_ready = s("weights_in"), s("pick_in"), s("pick_ready")
        LAG = 2
        with nc.Block() as block:
            @block.sync
            def _(sp):
                sp.dma_start(w1[:, :, :], w1d.rearrange("e d f -> d e f")).then_inc(wload, 16)
                sp.dma_start(w2[:, :, :], w2d.rearrange("e (c f) d -> f (e c) d", f=P)).then_inc(wload, 16)
                sp.dma_start(b1[:, :], b1d).then_inc(wload, 16)
                for m in range(3):
                    sp.dma_start(b2[m * E:(m + 1) * E, :], b2d).then_inc(wload, 16)
                sp.dma_start(pick32[:, :], a[f"pick{E}"]).then_inc(pick_in, 16)

            @block.tensor
            def _(pe):
                pe.wait_ge(wload, 16 * 6)
                pe.wait_ge(pick_ready, 1)
                with pe.Fori(0, IMAGES) as i:
                    for h in range(2):
                        n = i * 2 + h
                        cols = bass.ds(i * POS + h * BLK, BLK)
                        pe.wait_ge(added, n + 1)
                        for k in range(STEPS + LAG):
                            if k < STEPS:
                                e = k // C
                                if k % C == 0 and e >= 3:
                                    pe.wait_ge(hid_gated, n * STEPS + (e - 2) * C)
                                pe.matmul(h_bank[k % 3][:, :], w1[:, e, (k % C) * P:(k % C + 1) * P], K.pad[:, cols], start=True, stop=True).then_inc(hid_ready, 1)
                                if k % C == 0:
                                    pe.matmul(gate_bank[e % 3][:, :], pick[:, e:e + 1].broadcast_to([R, P]), g16[:, cols], start=True, stop=True).then_inc(gate_spread, 1)
                            if k >= LAG:
                                j = k - LAG
                                pe.wait_ge(hid_gated, n * STEPS + j + 1)
                                pe.matmul(y_bank[h][:, :], w2[:, j, :], hg[j % 3][:, :], start=(j == 0), stop=False)
                        pe.matmul(y_bank[h][:, :], b2[:, :], gT[:, cols], start=False, stop=True).then_inc(y_ready, 1)

            @block.scalar
            def _(act):
                act.wait_ge(wload, 16 * 6)
                with act.Fori(0, IMAGES) as i:
                    for h in range(2):
                        n = i * 2 + h
                        for k in range(STEPS):
                            act.wait_ge(hid_ready, n * STEPS + k + 1)
                            act.activation(hid[k % 3][:, :], h_bank[k % 3][:, :], ACT.Relu if kind == "first" else ACT.Gelu, bias=b1[:, k:k + 1]).then_inc(act_done, 1)

            @block.vector
            def _(dve):
                dve.sem_inc(added, 2)
                dve.wait_ge(pick_in, 16)
                dve.tensor_copy(pick[:, :], pick32[:, :]).then_inc(pick_ready, 1)
                with dve.Fori(0, IMAGES) as i:
                    for h in range(2):
                        n = i * 2 + h
                        for k in range(STEPS):
                            e = k // C
                            dve.wait_ge(gate_spread, n * E + e + 1)
                            dve.wait_ge(act_done, n * STEPS + k + 1)
                            dve.tensor_tensor(hg[k % 3][:, :], hid[k % 3][:, :], gate_bank[e % 3][:, :], ALU.mult).then_inc(hid_gated, 1)
                        dve.wait_ge(y_ready, n + 1)
                        blk = K.x[:, bass.ds(i * POS + h * BLK, BLK)]
                        if kind == "first":
                            link = Link(dve, ychain, n * 7, apart=True)
                            y = y_bank[h][:, :]
                            clean, tested, other = [f[:, :] for f in fix]
                            dve.wait_ge(added, n + 2)
                            link(dve.tensor_copy(other, y))
                            link(dve.tensor_tensor(tested, other, other, ALU.is_equal))
                            link(dve.tensor_scalar(other, y, -1e4, 1e4, ALU.max, ALU.min))
                            link(dve.memset(clean, 0.0))
                            link(dve.copy_predicated(clean, tested.bitcast(U32), other))
                            link(dve.tensor_scalar(tested, y, 0.0, 0.0, ALU.mult, ALU.is_equal))
                            link(dve.copy_predicated(clean, tested.bitcast(U32), y))
                            dve.tensor_tensor(blk, blk, clean, ALU.add).then_inc(added, 1)
                            continue
                        if kind == "norm2":
                            link = Link(dve, ychain, n)
                            link(dve.tensor_tensor(blk, blk, K.pad[:, bass.ds(i * POS + h * BLK, BLK)], ALU.add))
                        dve.tensor_tensor(blk, blk, y_bank[h][:, :], ALU.add).then_inc(added, 1)


D_INNER, D_STATE, D_CONV, DT_RANK = 256, 16, 4, 8
HALVES = D_INNER // P
DIRECTIONS = 4
DT_ROWS = 96


def flipped(t, d):
    g = t.rearrange("p (y x) -> p y x", x=SIDE)
    if d == 0:
        return g
    if d == 1:
        return g[:, :, ::-1]
    return g[:, ::-1, :] if d == 2 else g[:, ::-1, ::-1]


def state_space(K, tag):
    nc, a = K.nc, K.a
    sem = lambda name: K.sem(f"{tag}_{name}")
    EXP_AND_LN = "natural_log_exp_and_others"
    STEPS, STATES_AHEAD, RING = HALVES * D_STATE, 2, 4
    loaded, const_ready, chain_v, chain_a = sem("loaded"), sem("const_ready"), sem("chain_vector"), sem("chain_act")
    made, freed = sem("shared_bank_made"), sem("shared_bank_freed")
    xm_ready, first_tap, conv_done, xs_ready = sem("xm_ready"), sem("first_tap"), sem("conv_done"), sem("xs_ready")
    low_ready, coarse_ready, rest_ready, finer_ready, split_done = sem("low_ready"), sem("coarse_ready"), sem("rest_ready"), sem("finer_ready"), sem("split_done")
    log_ready, dt_ready, prepared, sg_ready = sem("log_ready"), sem("dt_ready"), sem("prepared"), sem("sg_ready")
    b_ready, c_spread, decay_ready = sem("b_ready"), sem("c_spread"), sem("decay_ready")
    fed, scanned, weighted, summed = sem("fed"), sem("scanned"), sem("weighted"), sem("summed")
    y_out, y_gated, added = sem("y_out"), sem("y_gated"), sem("added")

    PREP = {"dbl": 17, "dt0": 21, "dt1": 23}
    PREP_IMAGE = {"xm0": 1, "xm1": 3, "gate0": 9, "gate1": 11}
    ahead = {name: n for n, name in enumerate(("xm0", "xm1", "dbl", "dt0", "dt1", "b0", "b1"))}
    AHEAD = len(ahead)
    use = {}
    for d in range(DIRECTIONS):
        for k in range(STEPS):
            if k % HALVES == 0 and not (d == DIRECTIONS - 1 and k == STEPS - HALVES):
                use[d, k] = len(use)
            for name, at in list(PREP.items()) + (list(PREP_IMAGE.items()) if d == DIRECTIONS - 1 else []):
                if at == k:
                    use[d, name] = len(use)
    use[DIRECTIONS - 1, "out"] = len(use)
    use[DIRECTIONS - 1, STEPS - HALVES] = len(use)
    PER_IMAGE = len(use)

    with ExitStack() as ctx:
        sb = lambda n, shape, dt=FP32: ctx.enter_context(nc.sbuf_tensor(f"{tag}_{n}", shape, dt))
        w_in, w_x, w_dt, w_out = sb("w_in", [P, 2 * D_INNER]), sb("w_x", [P, HALVES, DT_ROWS + DT_RANK]), sb("w_dt", [DT_ROWS + DT_RANK, D_INNER]), sb("w_out", [P, HALVES, P])
        conv_w, conv_b, b_dt, dd = sb("conv_w", [P, HALVES, D_CONV]), sb("conv_b", [P, HALVES]), sb("b_dt", [P, HALVES]), sb("d", [P, HALVES])
        decay_rate = sb("decay_rate", [P, HALVES, D_STATE])
        pick = sb("pick", [3 * 32, 32], BF16)
        xm, xp = sb("xm", [P, HALVES, POS]), sb("xp", [P, D_CONV - 1 + POS])
        xs, dt, dtx = [[sb(f"{n}{j}", [P, HALVES, POS]) for j in range(2)] for n in ("xs", "dt", "dtx")]
        rest, coarse = sb("rest", [DT_ROWS + DT_RANK, POS]), sb("coarse", [3 * 32, POS], BF16)
        parts = [sb(f"parts{j}", [3 * 32, POS], BF16) for j in range(2)]
        decay, b_all = [[sb(f"{n}{j}", [P, POS]) for j in range(2)] for n in ("decay", "b_all")]
        st = [sb(f"state{j}", [P, POS]) for j in range(RING)]
        out = [sb(f"weighted{j}", [P, POS]) for j in range(2)]
        y, sg = sb("y", [P, HALVES, POS]), sb("sg", [P, HALVES, POS])
        bank, c_bank, y_bank = K.pair[0], K.pair[1], K.pair[2:4]

        def both(pe, to, rows, pieces):
            for half in range(2):
                cols = slice(half * BLK, (half + 1) * BLK)
                for n, (w, rhs) in enumerate(pieces):
                    last = pe.matmul(to[rows, cols], w, rhs(half), start=(n == 0), stop=(n == len(pieces) - 1))
            return last

        with nc.Block() as block:
            @block.sync
            def _(sp):
                for to, src in ((w_in[:, :], "L2_conv_W_in"), (w_x[:, :, :], "L2_conv_W_x"), (w_dt[DT_ROWS:DT_ROWS + DT_RANK, :], "L2_conv_W_dt"), (w_out[:, :, :], "L2_conv_W_out"),
                                (conv_w[:, :, :], "L2_conv_conv_w"), (conv_b[:, :], "L2_conv_conv_b"), (b_dt[:, :], "L2_conv_b_dt"), (dd[:, :], "L2_conv_D"), (decay_rate[:, :, :], "L2_conv_A_log")):
                    sp.dma_start(to, a[src]).then_inc(loaded, 16)

            @block.gpsimd
            def _(pool):
                pool.memset(xp[:, 0:D_CONV - 1], 0.0).then_inc(const_ready, 1)
                pool.sem_inc(fed, RING)

                def dt_x(q, j, h):
                    pool.wait_ge(dt_ready, q * HALVES + h + 1)
                    pool.nop(nofuse=True)
                    pool.tensor_tensor(dtx[j][:, h, :], dt[j][:, h, :], xs[j][:, h, :], ALU.mult).then_inc(prepared, 1)

                dt_x(0, 0, 0)
                dt_x(0, 0, 1)
                with pool.Fori(0, IMAGES) as i:
                    for d in range(DIRECTIONS):
                        g, j = i * DIRECTIONS + d, d % 2
                        pool.wait_ge(prepared, (g + 1) * HALVES)
                        for k in range(STEPS):
                            s, h = k // HALVES, k % HALVES
                            pool.wait_ge(b_ready, g * D_STATE + s + 1)
                            pool.wait_ge(weighted, g * STEPS + k + 1)
                            pool.nop(nofuse=True)
                            pool.tensor_tensor(st[k % RING][:, :], dtx[j][:, h, :], b_all[s % 2][:, :], ALU.mult).then_inc(fed, 1)
                            if k in (28, 30):
                                dt_x(g + 1, 1 - j, (k - 28) // 2)

            @block.tensor
            def _(pe):
                pe.wait_ge(loaded, 16 * 9)
                pe.wait_ge(const_ready, 5)
                pe.sem_inc(summed, 2)

                def project(which, image, n):
                    pe.wait_ge(freed, n)
                    both(pe, bank, slice(0, P), [(w_in[:, which * P:(which + 1) * P], lambda half: K.pad[:, bass.ds(image * POS + half * BLK, BLK)])]).then_inc(made, 1)

                def rows_of(q, j, n):
                    pe.wait_ge(xs_ready, (q + 1) * HALVES)
                    pe.wait_ge(freed, n)
                    both(pe, bank, slice(0, DT_ROWS + DT_RANK), [(w_x[:, h, :], lambda half, h=h: xs[j][:, h, half * BLK:(half + 1) * BLK]) for h in range(HALVES)]).then_inc(made, 1)

                def dt_of(q, h, n):
                    pe.wait_ge(low_ready, q + 1)
                    pe.wait_ge(freed, n)
                    rows = slice(DT_ROWS, DT_ROWS + DT_RANK)
                    both(pe, bank, slice(0, P), [(w_dt[rows, h * P:(h + 1) * P], lambda half: rest[rows, half * BLK:(half + 1) * BLK])]).then_inc(made, 1)

                def spread(to, j, row):
                    return both(pe, to, slice(0, P), [(pick[:, row:row + 1].broadcast_to([3 * 32, P]), lambda half: parts[j][:, half * BLK:(half + 1) * BLK])])

                def spread_b(q, j, s, n):
                    pe.wait_ge(split_done, q + 1)
                    pe.wait_ge(freed, n)
                    spread(bank, j, s).then_inc(made, 1)

                project(0, 0, ahead["xm0"])
                project(1, 0, ahead["xm1"])
                rows_of(0, 0, ahead["dbl"])
                dt_of(0, 0, ahead["dt0"])
                dt_of(0, 1, ahead["dt1"])
                spread_b(0, 0, 0, ahead["b0"])
                spread_b(0, 0, 1, ahead["b1"])
                with pe.Fori(0, IMAGES) as i:
                    for d in range(DIRECTIONS):
                        g, j, base = i * DIRECTIONS + d, d % 2, i * PER_IMAGE + AHEAD
                        for k in range(STEPS + 1):
                            pe.wait_ge(weighted, g * STEPS + k + RING)
                            if k < STEPS and k % HALVES == 0:
                                spread(c_bank, j, D_STATE + k // HALVES).then_inc(c_spread, 1)
                            if k >= 1:
                                s, h = (k - 1) // HALVES, (k - 1) % HALVES
                                if s == 0:
                                    pe.wait_ge(y_out, g * HALVES + h + 1)
                                for half in range(2):
                                    cols = slice(half * BLK, (half + 1) * BLK)
                                    last = pe.matmul(y_bank[h][:, cols], K.ident[:, :], out[(k - 1) % 2][:, cols], start=(s == 0), stop=(s == D_STATE - 1))
                                last.then_inc(summed, 1)
                            if (d, k) in use and not (d == DIRECTIONS - 1 and k == STEPS - HALVES):
                                s = k // HALVES + STATES_AHEAD
                                q = s // D_STATE
                                spread_b(g + q, j if q == 0 else 1 - j, s % D_STATE, base + use[d, k])
                            if d == DIRECTIONS - 1 and k in PREP_IMAGE.values():
                                name, which, image = {1: ("xm0", 0, i + 1), 3: ("xm1", 1, i + 1), 9: ("gate0", 2, i), 11: ("gate1", 3, i)}[k]
                                project(which, image, base + use[d, name])
                            if k == PREP["dbl"]:
                                rows_of(g + 1, 1 - j, base + use[d, "dbl"])
                            if k == PREP["dt0"]:
                                dt_of(g + 1, 0, base + use[d, "dt0"])
                            if k == PREP["dt1"]:
                                dt_of(g + 1, 1, base + use[d, "dt1"])
                    pe.wait_ge(y_gated, i + 2)
                    last_d = DIRECTIONS - 1
                    pe.wait_ge(freed, base + use[last_d, "out"])
                    both(pe, bank, slice(0, P), [(w_out[:, h, :], lambda half, h=h: y[:, h, half * BLK:(half + 1) * BLK]) for h in range(HALVES)]).then_inc(made, 1)
                    spread_b(i * DIRECTIONS + DIRECTIONS, 0, 1, base + use[last_d, STEPS - HALVES])

            @block.scalar
            def _(act):
                act.wait_ge(loaded, 16 * 9)
                act.activation(decay_rate[:, :, :], decay_rate[:, :, :], ACT.Exp).then_inc(chain_a, 1)
                act.wait_ge(chain_a, 1)
                act.mul(decay_rate[:, :, :], decay_rate[:, :, :], -1.0).then_inc(chain_a, 1)
                act.wait_ge(chain_a, 2)
                act.wait_ge(const_ready, 5)
                PER_SEQ = 2 + 3 * HALVES
                at = lambda q, n: q * PER_SEQ + 2 + n

                def link(ins, n):
                    ins.then_inc(chain_a, 1)
                    act.wait_ge(chain_a, n)

                def take_xm(h, image, n):
                    act.wait_ge(made, n + 1)
                    act.copy(xm[:, h, :], bank[:, :]).then_inc(xm_ready, 1)
                    act.wait_ge(xm_ready, image * HALVES + h + 1)
                    act.sem_inc(freed, 1)

                def turn_xm(q, d, h, first=False):
                    if not (first and h == 0):
                        act.wait_ge(conv_done, q * HALVES + h)
                    link(act.copy(xp[:, D_CONV - 1:].rearrange("p (y x) -> p y x", x=SIDE), flipped(xm[:, h, :], d)), at(q, h + 1))

                def first_product(q, j, h):
                    act.wait_ge(y_out, q * HALVES)
                    act.mul(xs[j][:, h, :], xp[:, 0:POS], conv_w[:, h, 0:1]).then_inc(first_tap, 1)

                def silu_xs(q, j):
                    for h in range(HALVES):
                        act.wait_ge(conv_done, q * HALVES + h + 1)
                        act.activation(xs[j][:, h, :], xs[j][:, h, :], ACT.Silu, bias=conv_b[:, h:h + 1]).then_inc(xs_ready, 1)
                    act.preload_act_table_set(EXP_AND_LN)

                def take_rows(q, j, n, first=False):
                    act.wait_ge(made, n + 1)
                    if not first:
                        act.wait_ge(split_done, q)
                    act.copy(rest[:, :], bank[0:DT_ROWS + DT_RANK, :]).then_inc(low_ready, 1)
                    act.wait_ge(low_ready, q + 1)
                    act.sem_inc(freed, 1)
                    act.copy(coarse[:, :], rest[0:96, :]).then_inc(coarse_ready, 1)

                def split_rest(q, j):
                    act.wait_ge(rest_ready, q + 1)
                    act.copy(parts[j][0:32, :], coarse[0:32, :])
                    act.copy(parts[j][32:64, :], rest[32:64, :])
                    act.copy(coarse[64:96, :], rest[64:96, :]).then_inc(finer_ready, 1)

                def take_dt(q, j, h, n):
                    act.wait_ge(made, n + 1)
                    act.activation(dt[j][:, h, :], bank[:, :], ACT.Relu, bias=b_dt[:, h:h + 1])
                    link(act.activation(dtx[j][:, h, :], bank[:, :], ACT.Abs, bias=b_dt[:, h:h + 1]), at(q, 3 + 3 * h))
                    act.sem_inc(freed, 1)

                def log_dt(q, j, h):
                    link(act.activation(dtx[j][:, h, :], dtx[j][:, h, :], ACT.Exp, scale=-1.0), at(q, 4 + 3 * h))
                    act.activation(dtx[j][:, h, :], dtx[j][:, h, :], ACT.Ln, bias=1.0).then_inc(log_ready, 1)
                    act.sem_inc(chain_a, 1)

                def take_b(q, s, n):
                    act.wait_ge(made, n + 1)
                    act.wait_ge(fed, q * STEPS + s * HALVES + 2)
                    act.copy(b_all[s % 2][:, :], bank[:, :]).then_inc(b_ready, 1)
                    act.wait_ge(b_ready, q * D_STATE + s + 1)
                    act.sem_inc(freed, 1)

                take_xm(0, 0, ahead["xm0"])
                take_xm(1, 0, ahead["xm1"])
                for h in range(HALVES):
                    turn_xm(0, 0, h, first=True)
                    first_product(0, 0, h)
                silu_xs(0, 0)
                take_rows(0, 0, ahead["dbl"], first=True)
                split_rest(0, 0)
                for h in range(HALVES):
                    take_dt(0, 0, h, ahead[f"dt{h}"])
                    log_dt(0, 0, h)
                take_b(0, 0, ahead["b0"])
                with act.Fori(0, IMAGES) as i:
                    for d in range(DIRECTIONS):
                        g, j, base = i * DIRECTIONS + d, d % 2, i * PER_IMAGE + AHEAD
                        act.wait_ge(dt_ready, (g + 1) * HALVES)
                        for k in range(STEPS):
                            s, h = k // HALVES, k % HALVES
                            act.wait_ge(scanned, g * STEPS + k + 1)
                            act.activation(decay[k % 2][:, :], dt[j][:, h, :], ACT.Exp, scale=decay_rate[:, h, s:s + 1]).then_inc(decay_ready, 1)
                            if h == 0:
                                if k >= HALVES:
                                    n = base + use[d, k - HALVES]
                                else:
                                    n = base + use[d - 1, STEPS - HALVES] if d else base - 1
                                q = (s + 1) // D_STATE
                                take_b(g + q, (s + 1) % D_STATE, n)
                            if d == DIRECTIONS - 1 and k - 2 in (PREP_IMAGE["gate0"], PREP_IMAGE["gate1"]):
                                hh = (k - 2 - PREP_IMAGE["gate0"]) // 2
                                act.wait_ge(made, base + use[d, f"gate{hh}"] + 1)
                                act.wait_ge(y_gated, i + 1)
                                act.activation(sg[:, hh, :], bank[:, :], ACT.Silu).then_inc(sg_ready, 1)
                                act.preload_act_table_set(EXP_AND_LN)
                                act.wait_ge(sg_ready, i * HALVES + hh + 1)
                                act.sem_inc(freed, 1)
                            if d == DIRECTIONS - 1 and k - 2 in (PREP_IMAGE["xm0"], PREP_IMAGE["xm1"]):
                                hh = (k - 2 - PREP_IMAGE["xm0"]) // 2
                                take_xm(hh, i + 1, base + use[d, f"xm{hh}"])
                            if k in (6, 10):
                                turn_xm(g + 1, (d + 1) % DIRECTIONS, (k - 6) // 4)
                            if k in (7, 11):
                                first_product(g + 1, 1 - j, (k - 7) // 4)
                            if k == 15:
                                silu_xs(g + 1, 1 - j)
                            if k == PREP["dbl"] + 2:
                                take_rows(g + 1, 1 - j, base + use[d, "dbl"])
                            if k == PREP["dbl"] + 4:
                                split_rest(g + 1, 1 - j)
                            if k in (PREP["dt0"] + 2, PREP["dt1"] + 2):
                                hh = (k - 2 - PREP["dt0"]) // 2
                                take_dt(g + 1, 1 - j, hh, base + use[d, f"dt{hh}"])
                            if k in (24, 26):
                                log_dt(g + 1, 1 - j, (k - 24) // 2)

            @block.vector
            def _(dve):
                TAPS_LEFT = D_CONV - 1
                for m in range(3):
                    dve.tensor_copy(pick[32 * m:32 * m + 32, :], K.ident[32 * m:32 * m + 32, 32 * m:32 * m + 32]).then_inc(const_ready, 1)
                dve.memset(K.pad[:, TOKENS:TOKENS + POS], 0.0).then_inc(const_ready, 1)
                dve.sem_inc(scanned, 2)
                dve.sem_inc(weighted, RING)
                dve.sem_inc(y_out, 2)
                dve.sem_inc(y_gated, 1)
                dve.wait_ge(loaded, 16 * 9)
                dve.wait_ge(const_ready, 5)

                def conv(q, j, h):
                    m = q * HALVES + h
                    dve.wait_ge(first_tap, m + 1)
                    link = Link(dve, chain_v, m * (TAPS_LEFT - 1))
                    for t in range(1, D_CONV):
                        ins = dve.scalar_tensor_tensor(xs[j][:, h, :], xp[:, t:t + POS], conv_w[:, h, t:t + 1], xs[j][:, h, :], ALU.mult, ALU.add)
                        if t < D_CONV - 1:
                            link(ins)
                    ins.then_inc(conv_done, 1)

                def leave_rest(q):
                    dve.wait_ge(coarse_ready, q + 1)
                    dve.tensor_tensor(rest[0:96, :], rest[0:96, :], coarse[:, :], ALU.subtract).then_inc(rest_ready, 1)

                def last_part(q, j):
                    dve.wait_ge(finer_ready, q + 1)
                    dve.tensor_tensor(parts[j][64:96, :], rest[64:96, :], coarse[64:96, :], ALU.subtract).then_inc(split_done, 1)

                def dt_half(q, j, h):
                    dve.wait_ge(log_ready, q * HALVES + h + 1)
                    dve.tensor_tensor(dt[j][:, h, :], dt[j][:, h, :], dtx[j][:, h, :], ALU.add).then_inc(dt_ready, 1)

                def take_y(i, d, h):
                    g, j = i * DIRECTIONS + d, d % 2
                    dve.wait_ge(summed, g * STEPS + STEPS - HALVES + h + 1 + 2)
                    to = flipped(y[:, h, :], d)
                    grid = lambda t: t.rearrange("p (y x) -> p y x", x=SIDE)
                    if d == 0:
                        dve.scalar_tensor_tensor(to, grid(xs[j][:, h, :]), dd[:, h:h + 1], grid(y_bank[h][:, :]), ALU.mult, ALU.add).then_inc(y_out, 1)
                    else:
                        dve.scalar_tensor_tensor(xs[j][:, h, :], xs[j][:, h, :], dd[:, h:h + 1], y_bank[h][:, :], ALU.mult, ALU.add).then_inc(added, 1)
                        dve.wait_ge(added, i * (HALVES * (DIRECTIONS - 1)) + (d - 1) * HALVES + h + 1)
                        dve.tensor_tensor(to, to, grid(xs[j][:, h, :]), ALU.add).then_inc(y_out, 1)

                conv(0, 0, 0)
                conv(0, 0, 1)
                leave_rest(0)
                last_part(0, 0)
                dt_half(0, 0, 0)
                dt_half(0, 0, 1)
                with dve.Fori(0, IMAGES) as i:
                    for d in range(DIRECTIONS):
                        g, j = i * DIRECTIONS + d, d % 2
                        for k in range(STEPS + 1):
                            if k < STEPS:
                                dve.wait_ge(decay_ready, g * STEPS + k + 1)
                                dve.wait_ge(fed, g * STEPS + k + 1 + RING)
                                dve.tensor_tensor_scan(st[k % RING][:, :], decay[k % 2][:, :], st[k % RING][:, :], 0.0, ALU.mult, ALU.add).then_inc(scanned, 1)
                            if d > 0 and k in (1, 2):
                                take_y(i, d - 1, k - 1)
                            if k >= 1:
                                s = (k - 1) // HALVES
                                dve.wait_ge(c_spread, g * D_STATE + s + 1)
                                dve.wait_ge(scanned, g * STEPS + k + 2)
                                dve.wait_ge(summed, g * STEPS + k)
                                dve.tensor_tensor(out[(k - 1) % 2][:, :], st[(k - 1) % RING][:, :], c_bank[:, :], ALU.mult).then_inc(weighted, 1)
                            if k in (8, 12):
                                conv(g + 1, 1 - j, (k - 8) // 4)
                            if k == 20:
                                leave_rest(g + 1)
                            if k == 23:
                                last_part(g + 1, 1 - j)
                            if k in (26, 28):
                                dt_half(g + 1, 1 - j, (k - 26) // 2)
                    for h in range(HALVES):
                        take_y(i, DIRECTIONS - 1, h)
                    dve.wait_ge(sg_ready, (i + 1) * HALVES)
                    dve.wait_ge(y_out, (i + 1) * DIRECTIONS * HALVES + 2)
                    dve.tensor_tensor(y[:, :, :], y[:, :, :], sg[:, :, :], ALU.mult).then_inc(y_gated, 1)
                    dve.wait_ge(made, i * PER_IMAGE + AHEAD + use[DIRECTIONS - 1, "out"] + 1)
                    blk = K.x[:, bass.ds(i * POS, POS)]
                    dve.scalar_tensor_tensor(blk, bank[:, :], 1.0 / DIRECTIONS, blk, ALU.mult, ALU.add).then_inc(freed, 1)


EDGES = 524288
LANE = 128
CHUNK = P * LANE
EC = EDGES // CHUNK
RUNS = EDGES // LANE
COLS = EDGES // P
HEADS, EXPERTS1 = 4, 4
ROW = HEADS * (1 + EXPERTS1)
STATE = HEADS * (2 + EXPERTS1)
NODE_BITS, EDGE_BITS, LANE_BITS = 13, 19, 7
KEY_BASE = 0x20000000
SCAT_SKIP = 1 << 22


def sort_plan():
    plan = []
    for k in range(1, EDGE_BITS + 1):
        if k == LANE_BITS:
            plan.append(("sign", "N", 0, 0, k))
        if k > LANE_BITS:
            plan.append(("turn", "T", 0, 0, k))
            plan += [("stage", "T", j - LANE_BITS, k - LANE_BITS if k < EDGE_BITS else None, k) for j in range(k - 1, LANE_BITS - 1, -1)]
            plan.append(("turn", "N", 0, 0, k))
        for j in range(min(k, LANE_BITS) - 1, -1, -1):
            bit = k if k < LANE_BITS else None if k < 2 * LANE_BITS or k == EDGE_BITS else k - LANE_BITS
            plan.append(("stage", "N", j, bit, k))
    return plan


def compare(dve, src, dst, bit, direction):
    low = 1 << bit
    if direction is None:
        a, b = [t.rearrange("p (m h l) -> p m h l", h=2, l=low) for t in (src, dst)]
        dve.tensor_tensor(b[:, :, 0, :], a[:, :, 0, :], a[:, :, 1, :], ALU.min)
        return dve.tensor_tensor(b[:, :, 1, :], a[:, :, 0, :], a[:, :, 1, :], ALU.max)
    mid = 1 << (direction - 1 - bit)
    a, b = [t.rearrange("p (o d m h l) -> p o d m h l", d=2, m=mid, h=2, l=low) for t in (src, dst)]
    for d in range(2):
        x, z = a[:, :, d, :, 0, :], a[:, :, d, :, 1, :]
        dve.tensor_tensor(b[:, :, d, :, 0, :], x, z, ALU.max if d else ALU.min)
        last = dve.tensor_tensor(b[:, :, d, :, 1, :], x, z, ALU.min if d else ALU.max)
    return last


def sort_edges(K, tag, keys, tables):
    nc, a = K.nc, K.a
    sem = lambda name: K.sem(f"{tag}_{name}")
    loaded, steps, turned, moved = sem("edges_loaded"), sem("steps"), sem("turned"), sem("moved")
    zeros_made, cleared = sem("zeros_made"), sem("tables_cleared")
    plan = sort_plan()
    with ExitStack() as ctx:
        raw = [ctx.enter_context(nc.sbuf_tensor(f"{tag}_raw{j}", [P, COLS], I32)) for j in range(2)]
        sign = ctx.enter_context(nc.sbuf_tensor(f"{tag}_sign", [P, LANE_BITS], FP32))
        ZERO_ROWS = 64
        zeros = ctx.enter_context(nc.sbuf_tensor(f"{tag}_zeros", [P, ZERO_ROWS * max(t.shape[1] for t in tables)], FP32))
        PREP = 9
        with nc.Block() as block:
            @block.sync
            def _(sp):
                for j in range(2):
                    sp.dma_start(raw[j][:, :], a["L1_ffn_edge_index"][j].rearrange("(p f) -> p f", p=P)).then_inc(loaded, 16)
                sp.dma_start(sign[:, :], a["sort_sign"]).then_inc(loaded, 16)
                sp.wait_ge(zeros_made, 1)
                for table in tables:
                    n, width = EDGES // P // ZERO_ROWS, ZERO_ROWS * table.shape[1]
                    sp.dma_start(table.rearrange("(p n e) f -> p n (e f)", p=P, n=n), zeros[:, 0:width].unsqueeze(1).broadcast_to([P, n, width])).then_inc(cleared, 16)
                sp.wait_ge(cleared, 16 * len(tables))

            @block.gpsimd
            def _(pool):
                pool.memset(zeros[:, :], 0.0).then_inc(zeros_made, 1)

            @block.tensor
            def _(pe):
                n, cur, turns = PREP, 0, 0
                for what, layout, bit, direction, k in plan:
                    if what == "turn":
                        pe.wait_ge(steps, n)
                        if turns:
                            pe.wait_ge(moved, 2 * turns)
                        for q in range(4):
                            for c in range(8):
                                at = (8 * q + c) * P
                                last = pe.transpose(K.pair[q][:, c * P:(c + 1) * P], keys[cur][:, at:at + P], K.ident[:, :])
                            last.then_inc(turned, 1)
                        turns += 1
                    n += 1
                    cur = 1 - cur

            def move(eng, scalar, layout, k, q, dst):
                out, src = dst[:, q * 8 * P:(q + 1) * 8 * P], K.pair[q][:, :]
                if layout == "T" and LANE_BITS <= k - 1 < 2 * LANE_BITS:
                    low = 1 << (k - 1 - LANE_BITS)
                    o, s = [t.rearrange("p (m d l) -> p m d l", d=2, l=low) for t in (out, src)]
                    if scalar:
                        eng.copy(o[:, :, 0, :], s[:, :, 0, :])
                        return eng.mul(o[:, :, 1, :], s[:, :, 1, :], -1.0)
                    eng.tensor_copy(o[:, :, 0, :], s[:, :, 0, :])
                    return eng.tensor_scalar(o[:, :, 1, :], s[:, :, 1, :], -1.0, None, ALU.mult)
                if layout == "N" and k < 2 * LANE_BITS:
                    col = sign[:, k - LANE_BITS:k - LANE_BITS + 1]
                    return eng.mul(out, src, col) if scalar else eng.tensor_scalar(out, src, col, None, ALU.mult)
                return eng.copy(out, src) if scalar else eng.tensor_copy(out, src)

            @block.scalar
            def _(act):
                cur, turns = 0, 0
                for what, layout, bit, direction, k in plan:
                    if what == "turn":
                        for q in (2, 3):
                            act.wait_ge(turned, 4 * turns + q + 1)
                            move(act, True, layout, k, q, keys[1 - cur]).then_inc(moved, 1)
                        turns += 1
                    cur = 1 - cur

            @block.vector
            def _(dve):
                link = Link(dve, steps)
                dve.wait_ge(loaded, 48)
                x, z = keys[0][:, :], keys[1][:, :]
                rs, rd = raw[0][:, :], raw[1][:, :]
                link(dve.tensor_copy(x, rd))
                link(dve.tensor_scalar(z, x, 0.0, None, ALU.is_ge))
                link(dve.scalar_tensor_tensor(z, x, float(TOKENS), z, ALU.is_lt, ALU.mult))
                link(dve.scalar_tensor_tensor(z, x, -float(TOKENS), z, ALU.add, ALU.mult))
                link(dve.tensor_scalar(rd, z, float(TOKENS), None, ALU.add))
                dve.tensor_scalar(z, rs, 0.0, float(TOKENS), ALU.is_lt, ALU.mult)
                link(dve.tensor_scalar(rd, rd, NODE_BITS, KEY_BASE, ALU.logical_shift_left, ALU.bitwise_or))
                link(dve.tensor_tensor(z, z, rs, ALU.add))
                link(dve.tensor_scalar(rs, z, 0.0, float(TOKENS - 1), ALU.max, ALU.min))
                link(dve.tensor_tensor(x.bitcast(I32), rs, rd, ALU.bitwise_or))
                assert link.n == PREP
                cur, turns = 0, 0
                for what, layout, bit, direction, k in plan:
                    src, dst = keys[cur][:, :], keys[1 - cur][:, :]
                    if what == "stage":
                        link(compare(dve, src, dst, bit, direction))
                    elif what == "sign":
                        link(dve.tensor_scalar(dst, src, sign[:, 0:1], None, ALU.mult))
                    else:
                        for q in (0, 1):
                            dve.wait_ge(turned, 4 * turns + q + 1)
                            last = move(dve, False, layout, k, q, keys[1 - cur])
                        link(last)
                        turns += 1
                        dve.wait_ge(moved, 2 * turns)
                    cur = 1 - cur
    return len(plan) % 2


def graph_attention(K, tag):
    nc, a = K.nc, K.a
    sem = lambda name: K.sem(f"{tag}_{name}")
    dram = lambda n, shape: nc.dram_tensor(f"{tag}_{n}", shape, FP32, kind="Internal").ap()
    node_rows, dst_rows = dram("node_rows", (TOKENS, ROW)), dram("dst_rows", (TOKENS, HEADS))
    dst_at_start, edge_rows = dram("dst_at_start", (EDGES, HEADS)), dram("edge_rows", (EDGES, STATE))
    run_rows = dram("run_rows", (RUNS, 2 * ROW))
    with ExitStack() as ctx:
        sb = lambda n, shape, dt=FP32: ctx.enter_context(nc.sbuf_tensor(f"{tag}_{n}", shape, dt))
        count, first, end = sb("count", [P, TILES]), sb("first", [P, TILES]), sb("end", [P, TILES])
        chunks = sb("chunks", [P, 1], I32)
        h, asrc, adst = sb("h", [P, TILES, HEADS, 1 + EXPERTS1]), sb("asrc", [P, TILES, HEADS]), sb("adst", [P, TILES, HEADS])
        runs = sb("runs", [P, EC, 4, ROW])
        with ExitStack() as outer:
            src_idx = outer.enter_context(nc.sbuf_tensor(f"{tag}_src_idx", [P, EC + 2, LANE], I32))
            dstf = outer.enter_context(nc.sbuf_tensor(f"{tag}_dstf", [P, EC + 2, LANE], FP32))
            with ExitStack() as inner:
                keys = [inner.enter_context(nc.sbuf_tensor(f"{tag}_keys{j}", [P, COLS], FP32)) for j in range(2)]
                at = sort_edges(K, tag + "s", keys, (dst_at_start, edge_rows))
                count_edges(K, tag + "c", keys[at], keys[1 - at], src_idx, dstf, count, first, end, chunks)
            node_tables(K, tag + "t", h, asrc, adst, node_rows, dst_rows)
            place_starts(K, tag + "p", count, first, adst, dst_at_start)
            edge_pass(K, tag + "e", src_idx, dstf, node_rows, dst_rows, dst_at_start, edge_rows, runs, chunks)
        join_runs(K, tag + "j", runs, run_rows)
        node_scores(K, tag + "n", count, first, end, h, asrc, adst, edge_rows, run_rows)


def busy_chunks(eng, chunks, known=None):
    if known is not None:
        eng.wait_ge(known, 1)
    return eng.value_load(chunks[0:1, 0:1], min_val=1, max_val=EC)


def count_edges(K, tag, keys, lo, src_idx, dstf, count, first, end, chunks):
    nc, a = K.nc, K.a
    sem = lambda name: K.sem(f"{tag}_{name}")
    chain, loaded, hot_ready, hot_used, bank_free, added, summed = sem("chain"), sem("loaded"), sem("hot_ready"), sem("hot_used"), sem("bank_free"), sem("added"), sem("summed")
    all_ones, counted_real, chunks_known = sem("all_ones"), sem("counted_real"), sem("chunks_known")
    G = 16
    GROUPS = LANE // G
    FIRST_OTHER = float(np.array([KEY_BASE + (TOKENS << NODE_BITS)], np.int32).view(np.float32)[0])
    with ExitStack() as ctx:
        sb = lambda n, shape, dt=FP32: ctx.enter_context(nc.sbuf_tensor(f"{tag}_{n}", shape, dt))
        hi = keys
        iota, below = sb("iota", [P, P]), sb("below", [P, P])
        ones, zero = sb("ones", [P, P]), sb("zero", [P, TILES])
        hot_lo = [sb(f"hot_lo{j}", [P, G, P], BF16) for j in range(2)]
        hot_hi = [sb(f"hot_hi{j}", [P, G, TILES], BF16) for j in range(2)]
        total, real = sb("total", [P, TILES]), sb("real", [P, 1])
        with nc.Block() as block:
            @block.sync
            def _(sp):
                sp.dma_start(iota[:, :], a["column_number"]).then_inc(loaded, 16)
                sp.dma_start(below[:, :], a["strictly_below"]).then_inc(loaded, 16)

            @block.tensor
            def _(pe):
                pe.wait_ge(all_ones, 1)
                pe.matmul(K.bank[1][:, 0:1], ones[:, :], real[:, :], start=True, stop=True).then_inc(counted_real, 1)
                busy = busy_chunks(pe, chunks, chunks_known)
                with pe.Fori(0, EC) as c:
                    with pe.If(busy > c):
                        pe.wait_ge(bank_free, c + 1)
                        for g in range(GROUPS):
                            pe.wait_ge(hot_ready, c * GROUPS + g + 1)
                            for n in range(G):
                                last = pe.matmul(K.bank[0][:, 0:TILES], hot_lo[g % 2][:, n, :], hot_hi[g % 2][:, n, :], start=(g == 0 and n == 0), stop=(g == GROUPS - 1 and n == G - 1))
                            last.then_inc(hot_used, 1)
                    with pe.Else():
                        pe.nop()
                pe.wait_ge(summed, 1)
                pe.matmul(K.bank[2][:, 0:TILES], below[:, :], count[:, :], start=True, stop=True)
                pe.matmul(K.bank[3][:, 0:TILES], ones[:, :], count[:, :], start=True, stop=True).then_inc(summed, 1)

            @block.vector
            def _(dve):
                link = Link(dve, chain)
                bits = keys[:, :].bitcast(I32)
                flat = lambda t: t[:, 0:EC, :].rearrange("p c f -> p (c f)")
                dve.memset(src_idx[:, EC:, :], 0)
                dve.memset(dstf[:, EC:, :], 0.0)
                link(dve.tensor_scalar(lo[:, :], keys[:, :], FIRST_OTHER, None, ALU.is_lt))
                link(dve.tensor_reduce(real[:, :], lo[:, :], AX.X, ALU.add))
                dve.memset(ones[:, :], 1.0).then_inc(all_ones, 1)
                dve.wait_ge(counted_real, 1)
                link(dve.tensor_scalar(real[:, :], K.bank[1][:, 0:1], 1.0, float(CHUNK - 1), ALU.max, ALU.add))
                link(dve.tensor_copy(chunks[:, :], real[:, :]))
                dve.tensor_scalar(chunks[:, :], chunks[:, :], (CHUNK - 1).bit_length(), None, ALU.logical_shift_right).then_inc(chunks_known, 1)
                link(dve.tensor_scalar(flat(src_idx), bits, TOKENS - 1, None, ALU.bitwise_and))
                link(dve.tensor_scalar(bits, bits, NODE_BITS, 2 * TOKENS - 1, ALU.logical_shift_right, ALU.bitwise_and))
                link(dve.tensor_copy(flat(dstf), bits))
                link(dve.tensor_scalar(lo[:, :].bitcast(I32), bits, P - 1, None, ALU.bitwise_and))
                link(dve.tensor_scalar(hi[:, :].bitcast(I32), bits, 7, None, ALU.logical_shift_right))
                link(dve.tensor_copy(lo[:, :], lo[:, :].bitcast(I32)))
                link(dve.tensor_copy(hi[:, :], hi[:, :].bitcast(I32)))
                link(dve.memset(count[:, :], 0.0))
                link(dve.memset(zero[:, :], 0.0))
                dve.wait_ge(loaded, 32)
                busy = busy_chunks(dve, chunks, chunks_known)
                n0 = link.n
                dve.sem_inc(hot_used, 2)
                dve.sem_inc(bank_free, 1)
                with dve.Fori(0, EC) as c:
                    with dve.If(busy > c):
                        for g in range(GROUPS):
                            def one_hot(out, v, n):
                                at = v[:, bass.ds(c * LANE + g * G, G)].unsqueeze(2).broadcast_to([P, G, n])
                                return dve.tensor_tensor(out, at, iota[:, 0:n].unsqueeze(1).broadcast_to([P, G, n]), ALU.is_equal)
                            dve.wait_ge(hot_used, c * GROUPS + g + 1)
                            one_hot(hot_lo[g % 2][:, :, :], lo, P)
                            one_hot(hot_hi[g % 2][:, :, :], hi, TILES).then_inc(hot_ready, 1)
                        dve.wait_ge(hot_used, c * GROUPS + GROUPS + 2)
                        dve.tensor_tensor(count[:, :], count[:, :], K.bank[0][:, 0:TILES], ALU.add).then_inc(added, 1)
                        dve.wait_ge(added, c + 1)
                        dve.sem_inc(bank_free, 1)
                    with dve.Else():
                        dve.nop()
                dve.sem_inc(summed, 1)
                dve.wait_ge(summed, 2)
                link = Link(dve, chain, n0)
                link(dve.tensor_copy(total[:, :], K.bank[3][:, 0:TILES]))
                link(dve.tensor_tensor_scan(first[:, :], total[:, :], zero[:, :], 0.0, ALU.add, ALU.add))
                link(dve.tensor_tensor(first[:, :], first[:, :], total[:, :], ALU.subtract))
                link(dve.tensor_tensor(first[:, :], first[:, :], K.bank[2][:, 0:TILES], ALU.add))
                link(dve.tensor_tensor(end[:, :], first[:, :], count[:, :], ALU.add))


def node_tables(K, tag, h, asrc, adst, node_rows, dst_rows):
    nc, a = K.nc, K.a
    sem = lambda name: K.sem(f"{tag}_{name}")
    loaded, made, chain, stored = sem("loaded"), sem("made"), sem("chain"), sem("stored")
    HE = HEADS * EXPERTS1
    with ExitStack() as ctx:
        sb = lambda n, shape, dt=FP32: ctx.enter_context(nc.sbuf_tensor(f"{tag}_{n}", shape, dt))
        w, att = sb("w", [P, HE]), sb("att", [P, 2, HE])
        prod = sb("prod", [P, TILES, HEADS, EXPERTS1])
        with nc.Block() as block:
            @block.sync
            def _(sp):
                sp.dma_start(w[:, :], a["L1_ffn_W_gat"]).then_inc(loaded, 16)
                sp.dma_start(att[:, :, :], a["L1_ffn_att"]).then_inc(loaded, 16)
                sp.wait_ge(chain, 6)
                sp.dma_start(node_rows.rearrange("(t p) f -> p t f", p=P), h[:, :, :, :].rearrange("p t a b -> p t (a b)")).then_inc(stored, 16)
                sp.dma_start(dst_rows.rearrange("(t p) f -> p t f", p=P), adst[:, :, :]).then_inc(stored, 16)
                sp.wait_ge(stored, 16 * 2)

            @block.tensor
            def _(pe):
                pe.wait_ge(loaded, 32)
                for t in range(TILES):
                    last = pe.matmul(K.pair[0][:, t * HE:(t + 1) * HE], K.pad[:, t * P:(t + 1) * P], w[:, :], start=True, stop=True)
                last.then_inc(made, 1)

            @block.vector
            def _(dve):
                link = Link(dve, chain)
                dve.wait_ge(loaded, 32)
                dve.wait_ge(made, 1)
                ps = K.pair[0][:, :].rearrange("p (t a b) -> p t a b", a=HEADS, b=EXPERTS1)
                link(dve.tensor_copy(h[:, :, :, 1:], ps))
                for n, to in ((0, asrc), (1, adst)):
                    weights = att[:, n, :].rearrange("p (a b) -> p a b", b=EXPERTS1).unsqueeze(1).broadcast_to([P, TILES, HEADS, EXPERTS1])
                    link(dve.tensor_tensor(prod[:, :, :, :], h[:, :, :, 1:], weights, ALU.mult))
                    link(dve.tensor_reduce(to[:, :, :], prod[:, :, :, :], AX.X, ALU.add))
                link(dve.tensor_copy(h[:, :, :, 0], asrc[:, :, :]))


def place_starts(K, tag, count, first, adst, dst_at_start):
    nc = K.nc
    sem = lambda name: K.sem(f"{tag}_{name}")
    chain, placed = sem("chain"), sem("placed")
    with ExitStack() as ctx:
        t = ctx.enter_context(nc.sbuf_tensor(f"{tag}_t", [P, TILES], FP32))
        idx = ctx.enter_context(nc.sbuf_tensor(f"{tag}_idx", [P, TILES], I32))
        with nc.Block() as block:
            @block.vector
            def _(dve):
                link = Link(dve, chain)
                link(dve.tensor_scalar(t[:, :], count[:, :], 0.0, float(SCAT_SKIP), ALU.is_equal, ALU.mult))
                link(dve.tensor_tensor(idx[:, :], t[:, :], first[:, :], ALU.add))

            @block.gpsimd
            def _(pool):
                pool.wait_ge(chain, 2)
                for n in range(TILES):
                    pool.indirect_dma_start(out=dst_at_start, out_offset=bass.IndirectOffsetOnAxis(ap=idx[:, n:n + 1], axis=0),
                                            in_=adst[:, n, :], in_offset=None, bounds_check=EDGES - 1, oob_is_err=False).then_inc(placed, 16)
                pool.wait_ge(placed, 16 * TILES)


def edge_pass(K, tag, src_idx, dstf, node_rows, dst_rows, dst_at_start, edge_rows, runs, chunks):
    nc = K.nc
    sem = lambda name: K.sem(f"{tag}_{name}")
    W = 1 + EXPERTS1
    idx_ready, rows_in, start_in, used, chain = sem("idx_ready"), [sem("rows_in0"), sem("rows_in1")], [sem("start_in0"), sem("start_in1")], sem("used"), sem("chain")
    exp_in, exp_out, stored, first_in = sem("exp_in"), sem("exp_out"), [sem("stored0"), sem("stored1")], [sem("first_in0"), sem("first_in1")]
    with ExitStack() as ctx:
        sb = lambda n, shape, dt=FP32: ctx.enter_context(nc.sbuf_tensor(f"{tag}_{n}", shape, dt))
        idx = [sb(f"idx{j}", [P, LANE + 1], I32) for j in range(2)]
        rows = [sb(f"rows{j}", [P, LANE, HEADS, W]) for j in range(2)]
        start = [sb(f"start{j}", [P, LANE, HEADS]) for j in range(2)]
        begin = [sb(f"begin{j}", [P, HEADS]) for j in range(2)]
        keep, reset = sb("keep", [P, LANE]), sb("reset", [P, LANE])
        e, ex = sb("e", [P, HEADS, LANE]), [sb(f"ex{j}", [P, 2, HEADS, LANE]) for j in range(2)]
        m = sb("m", [P, HEADS, LANE + 1])
        out = [sb(f"out{j}", [P, LANE, HEADS, 1 + W]) for j in range(2)]
        LINKS = 10 + 2 * HEADS
        with nc.Block() as block:
            @block.gpsimd
            def _(pool):
                busy = busy_chunks(pool, chunks)
                with pool.Fori(0, EC // 2) as i:
                    for j in range(2):
                        c = i * 2 + j
                        with pool.If(busy > c):
                            pool.wait_ge(idx_ready, c + 1)
                            pool.wait_ge(used, c + 1)
                            pool.nop(nofuse=True)
                            pool.indirect_dma_start(out=begin[j][:, :], out_offset=None, in_=dst_rows,
                                                    in_offset=bass.IndirectOffsetOnAxis(ap=idx[j][:, LANE:LANE + 1], axis=0)).then_inc(first_in[j], 16)
                            for f in range(LANE):
                                pool.indirect_dma_start(out=rows[j][:, f, :, :].rearrange("p a b -> p (a b)"), out_offset=None, in_=node_rows,
                                                        in_offset=bass.IndirectOffsetOnAxis(ap=idx[j][:, f:f + 1], axis=0)).then_inc(rows_in[j], 16)
                        with pool.Else():
                            pool.nop()

            @block.sync
            def _(sp):
                starts = dst_at_start.rearrange("(c p f) a -> c p (f a)", p=P, f=LANE)
                outs = edge_rows.rearrange("(c p f) a -> c p (f a)", p=P, f=LANE)
                busy = busy_chunks(sp, chunks)
                with sp.Fori(0, EC // 2) as i:
                    for j in range(2):
                        c = i * 2 + j
                        with sp.If(busy > c):
                            sp.wait_ge(used, c + 1)
                            sp.dma_start(start[j][:, :, :].rearrange("p f a -> p (f a)"), starts[c]).then_inc(start_in[j], 16)
                        with sp.Else():
                            sp.nop()
                    for j in range(2):
                        c = i * 2 + j
                        with sp.If(busy > c):
                            sp.wait_ge(used, c + 3)
                            sp.dma_start(outs[c], out[j][:, :, :, :].rearrange("p f a b -> p (f a b)")).then_inc(stored[j], 16)
                            sp.wait_ge(stored[j], (i + 1) * 16)
                            sp.nop(nofuse=True)
                        with sp.Else():
                            sp.nop()

            @block.scalar
            def _(act):
                busy = busy_chunks(act, chunks)
                with act.Fori(0, EC // 2) as i:
                    for j in range(2):
                        c = i * 2 + j
                        with act.If(busy > c):
                            act.wait_ge(exp_in, c + 1)
                            act.activation(ex[j][:, :, :, :], ex[j][:, :, :, :], ACT.Exp).then_inc(exp_out, 1)
                        with act.Else():
                            act.nop()

            @block.vector
            def _(dve):
                dve.sem_inc(used, 2)
                dve.memset(m[:, :, 0:1], -HUGE)
                dve.memset(keep[:, 0:1], 0.0).then_inc(chain, 1)
                dve.wait_ge(chain, 1)

                def take_indices(c, j):
                    dve.tensor_copy(idx[j][:, 0:LANE], src_idx[:, c, :])
                    dve.tensor_scalar(idx[j][:, LANE:LANE + 1], dstf[:, c, 0:1], float(TOKENS - 1), None, ALU.min).then_inc(idx_ready, 1)

                busy = busy_chunks(dve, chunks)
                dve.memset(runs[:, :, :, :], 0.0).then_inc(chain, 1)
                dve.wait_ge(chain, 2)
                take_indices(0, 0)
                take_indices(1, 1)
                with dve.Fori(0, EC // 2) as i:
                    for j in range(2):
                        c = i * 2 + j
                        with dve.If(busy > c):
                            link = Link(dve, chain, c * LINKS + 2)
                            dcol = dstf[:, c, :]
                            link(dve.tensor_tensor(keep[:, 1:LANE], dcol[:, 1:LANE], dcol[:, 0:LANE - 1], ALU.is_equal))
                            link(dve.tensor_scalar(reset[:, :], keep[:, :], -1.0, HUGE, ALU.add, ALU.mult))
                            dve.wait_ge(start_in[j], (i + 1) * 16)
                            dve.wait_ge(first_in[j], (i + 1) * 16)
                            link(dve.tensor_copy(start[j][:, 0, :], begin[j][:, :]))
                            for a in range(HEADS):
                                link(dve.tensor_tensor_scan(e[:, a, :], keep[:, :], start[j][:, :, a], 0.0, ALU.mult, ALU.add))
                            dve.wait_ge(rows_in[j], (i + 1) * (16 * LANE))
                            link(dve.tensor_tensor(e[:, :, :], e[:, :, :], rows[j][:, :, :, 0].rearrange("p f a -> p a f"), ALU.add))
                            link(dve.scalar_tensor_tensor(e[:, :, :], e[:, :, :], 0.2, e[:, :, :], ALU.mult, ALU.max))
                            for a in range(HEADS):
                                link(dve.tensor_tensor_scan(m[:, a, 1:], reset[:, :], e[:, a, :], -HUGE, ALU.add, ALU.max))
                            both = ex[j]
                            dve.tensor_tensor(both[:, 1, :, :], e[:, :, :], m[:, :, 1:], ALU.subtract)
                            link(dve.tensor_tensor(both[:, 0, :, :], m[:, :, 0:LANE], reset[:, :].unsqueeze(1).broadcast_to([P, HEADS, LANE]), ALU.add))
                            dve.tensor_tensor(both[:, 0, :, :], both[:, 0, :, :], m[:, :, 1:], ALU.subtract).then_inc(exp_in, 1)
                            link(dve.memset(rows[j][:, :, :, 0], 1.0))
                            dve.wait_ge(stored[j], i * 16)
                            link(dve.tensor_copy(out[j][:, :, :, 0].rearrange("p f a -> p a f"), m[:, :, 1:]))
                            dve.wait_ge(exp_out, c + 1)
                            for a in range(HEADS):
                                last = dve.tensor_tensor(rows[j][:, :, a, :], rows[j][:, :, a, :], both[:, 1, a, :].unsqueeze(2).broadcast_to([P, LANE, W]), ALU.mult)
                            link(last)
                            for a in range(HEADS):
                                for b in range(W):
                                    last = dve.tensor_tensor_scan(out[j][:, :, a, 1 + b], both[:, 0, a, :], rows[j][:, :, a, b], 0.0, ALU.mult, ALU.add)
                            link(last)
                            assert link.n == LINKS
                            end = lambda n: runs[:, c, n, :].rearrange("p (a b) -> p a b", b=W)
                            dve.tensor_copy(end(0), m[:, :, LANE:LANE + 1].broadcast_to([P, HEADS, W]))
                            dve.tensor_copy(end(1), out[j][:, LANE - 1, :, 1:])
                            dve.tensor_copy(runs[:, c, 2, :], dstf[:, c, 0:1].broadcast_to([P, ROW]))
                            dve.tensor_copy(runs[:, c, 3, :], dstf[:, c, LANE - 1:LANE].broadcast_to([P, ROW])).then_inc(used, 1)
                            dve.wait_ge(used, c + 3)
                            take_indices(c + 2, j)
                        with dve.Else():
                            dve.nop()


def join_runs(K, tag, runs, run_rows):
    nc = K.nc
    sem = lambda name: K.sem(f"{tag}_{name}")
    turned, taken, chain, exp_in, exp_out, back, laid, stored = (
        sem("turned"), sem("taken"), sem("chain"), sem("exp_in"), sem("exp_out"), sem("back"), sem("laid"), sem("stored"))
    with ExitStack() as ctx:
        t = [ctx.enter_context(nc.sbuf_tensor(f"{tag}_{n}", [ROW, RUNS], FP32)) for n in ("top", "sums", "firsts", "lasts")]
        run_top = ctx.enter_context(nc.sbuf_tensor(f"{tag}_run_top", [ROW, RUNS + 1], FP32))
        top, sums, firsts, lasts = t
        GROUPS = EC // 8
        with nc.Block() as block:
            @block.tensor
            def _(pe):
                n = 0
                for s in range(4):
                    for q in range(GROUPS):
                        if n >= 4:
                            pe.wait_ge(taken, n - 3)
                        for c in range(8):
                            last = pe.transpose(K.pair[n % 4][0:ROW, c * P:(c + 1) * P], runs[:, 8 * q + c, s, :], K.ident[:, :])
                        last.then_inc(turned, 1)
                        n += 1
                pe.wait_ge(chain, 10)
                pe.wait_ge(taken, n)
                for g in range(2):
                    src = run_top[:, 1:] if g == 0 else lasts[:, :]
                    for c in range(EC):
                        at = c // 16 * BLK + c % 16 * ROW
                        last = pe.transpose(K.pair[g][:, at:at + ROW], src[:, c * P:(c + 1) * P], K.ident[0:ROW, 0:ROW])
                    last.then_inc(back, 1)

            @block.scalar
            def _(act):
                n = 0
                for s in range(4):
                    for q in range(GROUPS):
                        act.wait_ge(turned, n + 1)
                        act.copy(t[s][:, q * 8 * P:(q + 1) * 8 * P], K.pair[n % 4][0:ROW, :]).then_inc(taken, 1)
                        n += 1
                act.wait_ge(exp_in, 1)
                act.activation(firsts[:, :], firsts[:, :], ACT.Exp).then_inc(exp_out, 1)
                act.activation(lasts[:, :], lasts[:, :], ACT.Exp).then_inc(exp_out, 1)

            @block.vector
            def _(dve):
                link = Link(dve, chain)
                dve.wait_ge(taken, 4 * GROUPS)
                joins = run_top
                link(dve.memset(joins[:, 0:1], 0.0))
                link(dve.tensor_tensor(joins[:, 1:RUNS], firsts[:, 1:], lasts[:, 0:RUNS - 1], ALU.is_equal))
                link(dve.tensor_tensor(firsts[:, :], firsts[:, :], lasts[:, :], ALU.is_equal))
                link(dve.tensor_tensor(firsts[:, :], firsts[:, :], joins[:, 0:RUNS], ALU.mult))
                link(dve.tensor_scalar(lasts[:, :], firsts[:, :], -1.0, HUGE, ALU.add, ALU.mult))
                link(dve.memset(run_top[:, 0:1], -HUGE))
                link(dve.tensor_tensor_scan(run_top[:, 1:], lasts[:, :], top[:, :], -HUGE, ALU.add, ALU.max))
                link(dve.tensor_tensor(firsts[:, :], run_top[:, 0:RUNS], lasts[:, :], ALU.add))
                dve.tensor_tensor(firsts[:, :], firsts[:, :], run_top[:, 1:], ALU.subtract)
                dve.tensor_tensor(lasts[:, :], top[:, :], run_top[:, 1:], ALU.subtract).then_inc(exp_in, 1)
                dve.wait_ge(exp_out, 2)
                link(dve.tensor_tensor(sums[:, :], sums[:, :], lasts[:, :], ALU.mult))
                link(dve.tensor_tensor_scan(lasts[:, :], firsts[:, :], sums[:, :], 0.0, ALU.mult, ALU.add))
                for g in range(2):
                    dve.wait_ge(back, g + 1)
                    for b in range(EC // 16):
                        last = dve.tensor_copy(runs[:, 16 * b:16 * b + 16, g, :], K.pair[g][:, b * BLK:b * BLK + 16 * ROW].rearrange("p (c a) -> p c a", a=ROW))
                    last.then_inc(laid, 1)

            @block.sync
            def _(sp):
                sp.wait_ge(laid, 2)
                sp.dma_start(run_rows.rearrange("(c p) a -> p c a", p=P), runs[:, :, 0:2, :].rearrange("p c s a -> p c (s a)")).then_inc(stored, 16)
                sp.wait_ge(stored, 16)


def node_scores(K, tag, count, first, end, h, asrc, adst, edge_rows, run_rows):
    nc, a = K.nc, K.a
    sem = lambda name: K.sem(f"{tag}_{name}")
    chain, loaded, idx_ready, ends_in, runs_in, exp_in, exp_out, root_in, root_out = [
        sem(n) for n in ("chain", "loaded", "idx_ready", "ends_in", "runs_in", "exp_in", "exp_out", "root_in", "root_out")]
    W, HE = 1 + EXPERTS1, HEADS * EXPERTS1
    with ExitStack() as ctx:
        sb = lambda n, shape, dt=FP32: ctx.enter_context(nc.sbuf_tensor(f"{tag}_{n}", shape, dt))
        gat = sb("gat", [P, 3, HE])
        end_idx, run_idx, run_f = sb("end_idx", [P, TILES], I32), sb("run_idx", [P, TILES], I32), sb("run_f", [P, TILES])
        has_e, has_c, stat, stat2 = [sb(n, [P, TILES]) for n in ("has_edges", "has_runs", "stat", "stat2")]
        er, cr = sb("edge", [P, TILES, HEADS, 1 + W]), sb("run", [P, TILES, 2, HEADS, W])
        top, w = sb("top", [P, TILES, HEADS]), sb("w", [P, 3, TILES, HEADS])
        agg, sq = sb("agg", [P, TILES, HE]), sb("sq", [P, TILES, HE])
        epsilon = sb("epsilon", [P, 1])
        with nc.Block() as block:
            @block.sync
            def _(sp):
                sp.dma_start(gat[:, :, :], a["L1_ffn_gat"]).then_inc(loaded, 16)

            @block.gpsimd
            def _(pool):
                pool.wait_ge(idx_ready, 2)
                for t in range(TILES):
                    pool.indirect_dma_start(out=er[:, t, :, :].rearrange("p a b -> p (a b)"), out_offset=None, in_=edge_rows,
                                            in_offset=bass.IndirectOffsetOnAxis(ap=end_idx[:, t:t + 1], axis=0)).then_inc(ends_in, 16)
                    pool.indirect_dma_start(out=cr[:, t, :, :, :].rearrange("p s a b -> p (s a b)"), out_offset=None, in_=run_rows,
                                            in_offset=bass.IndirectOffsetOnAxis(ap=run_idx[:, t:t + 1], axis=0)).then_inc(runs_in, 16)

            @block.scalar
            def _(act):
                act.wait_ge(exp_in, 1)
                act.activation(w[:, :, :, :], w[:, :, :, :], ACT.Exp).then_inc(exp_out, 1)
                act.wait_ge(root_in, 1)
                act.activation(stat2[:, :], stat2[:, :], ACT.Sqrt, bias=epsilon[:, 0:1], scale=1.0 / HE).then_inc(root_out, 1)

            @block.vector
            def _(dve):
                link = Link(dve, chain)
                link(dve.tensor_scalar(end_idx[:, :], end[:, :], -1.0, 0.0, ALU.add, ALU.max))
                link(dve.tensor_scalar(run_idx[:, :], end_idx[:, :], LANE_BITS, None, ALU.logical_shift_right))
                link(dve.tensor_copy(run_f[:, :], run_idx[:, :]))
                dve.tensor_scalar(run_idx[:, :], run_f[:, :], -1.0, 0.0, ALU.add, ALU.max).then_inc(idx_ready, 2)
                link(dve.tensor_scalar(has_e[:, :], count[:, :], 0.0, None, ALU.is_gt))
                link(dve.scalar_tensor_tensor(has_c[:, :], run_f[:, :], float(LANE), first[:, :], ALU.mult, ALU.is_gt))
                link(dve.tensor_tensor(has_c[:, :], has_c[:, :], has_e[:, :], ALU.mult))
                link(dve.tensor_tensor(w[:, 2, :, :], asrc[:, :, :], adst[:, :, :], ALU.add))
                link(dve.scalar_tensor_tensor(w[:, 2, :, :], w[:, 2, :, :], 0.2, w[:, 2, :, :], ALU.mult, ALU.max))
                dve.wait_ge(ends_in, 16 * TILES)
                dve.wait_ge(runs_in, 16 * TILES)
                wide = lambda t: t[:, :].unsqueeze(2).broadcast_to([P, TILES, HEADS])
                for n, has, src in ((0, has_e, er[:, :, :, 0]), (1, has_c, cr[:, :, 0, :, 0])):
                    link(dve.tensor_tensor(w[:, n, :, :], src, wide(has), ALU.mult))
                    link(dve.tensor_scalar(has[:, :], has[:, :], -1.0, HUGE, ALU.add, ALU.mult))
                    link(dve.tensor_tensor(w[:, n, :, :], w[:, n, :, :], wide(has), ALU.add))
                link(dve.tensor_tensor(top[:, :, :], w[:, 0, :, :], w[:, 1, :, :], ALU.max))
                link(dve.tensor_tensor(top[:, :, :], top[:, :, :], w[:, 2, :, :], ALU.max))
                dve.tensor_tensor(w[:, :, :, :], w[:, :, :, :], top[:, :, :].unsqueeze(1).broadcast_to([P, 3, TILES, HEADS]), ALU.subtract).then_inc(exp_in, 1)
                link(dve.memset(h[:, :, :, 0], 1.0))
                dve.wait_ge(exp_out, 1)
                spread = lambda n: w[:, n, :, :].unsqueeze(3).broadcast_to([P, TILES, HEADS, W])
                acc, old, own = er[:, :, :, 1:], cr[:, :, 1, :, :], h[:, :, :, :]
                link(dve.tensor_tensor(acc, acc, spread(0), ALU.mult))
                link(dve.tensor_tensor(old, old, spread(1), ALU.mult))
                link(dve.tensor_tensor(own, own, spread(2), ALU.mult))
                link(dve.tensor_tensor(acc, acc, old, ALU.add))
                link(dve.tensor_tensor(acc, acc, own, ALU.add))
                link(dve.tensor_scalar(top[:, :, :], er[:, :, :, 1], 1e-16, None, ALU.add))
                link(dve.reciprocal(top[:, :, :], top[:, :, :]))
                agg4 = agg[:, :, :].rearrange("p t (a b) -> p t a b", b=EXPERTS1)
                link(dve.tensor_tensor(agg4, er[:, :, :, 2:], top[:, :, :].unsqueeze(3).broadcast_to([P, TILES, HEADS, EXPERTS1]), ALU.mult))
                dve.wait_ge(loaded, 16)
                param = lambda n: gat[:, n, :].unsqueeze(1).broadcast_to([P, TILES, HE])
                row = lambda t: t[:, :].unsqueeze(2).broadcast_to([P, TILES, HE])
                link(dve.tensor_tensor(agg[:, :, :], agg[:, :, :], param(0), ALU.add))
                link(dve.memset(epsilon[:, :], 1e-5))
                link(dve.tensor_reduce(stat[:, :], agg[:, :, :], AX.X, ALU.add))
                link(dve.tensor_scalar(stat[:, :], stat[:, :], 1.0 / HE, None, ALU.mult))
                link(dve.tensor_tensor(agg[:, :, :], agg[:, :, :], row(stat), ALU.subtract))
                link(dve.tensor_tensor(sq[:, :, :], agg[:, :, :], agg[:, :, :], ALU.mult))
                dve.tensor_reduce(stat2[:, :], sq[:, :, :], AX.X, ALU.add).then_inc(root_in, 1)
                dve.wait_ge(root_out, 1)
                link(dve.reciprocal(stat2[:, :], stat2[:, :]))
                link(dve.tensor_tensor(agg[:, :, :], agg[:, :, :], row(stat2), ALU.mult))
                link(dve.tensor_tensor(agg[:, :, :], agg[:, :, :], param(1), ALU.mult))
                link(dve.tensor_tensor(agg[:, :, :], agg[:, :, :], param(2), ALU.add))
                link(dve.tensor_reduce(K.scores[:, :, :], agg[:, :, :].rearrange("p t (a b) -> p t b a", b=EXPERTS1), AX.X, ALU.add))
                dve.tensor_scalar(K.scores[:, :, :], K.scores[:, :, :], 1.0 / HEADS, None, ALU.mult)


def metaformer(nc, a, stages=None):
    with ExitStack() as ctx:
        K = Core(nc, a, ctx)
        start(K)
        run = {
            "l0c": lambda: (layernorm(K, "l0n", 1e-6, True), deformable(K, "l0c")),
            "l0f": lambda: (layernorm(K, "l0t", 1e-5, False),
                            moe(K, "l0f", 8, 256, "top2", ("L0_ffn_W1", "L0_ffn_b1", "L0_ffn_W2", "L0_ffn_b2", "L0_ffn_gate_w", "L0_ffn_gate_b"))),
            "l1c": lambda: (layernorm(K, "l1n", 1e-6, True),
                            conv_residual(K, "l1c", a["L1_conv_weight"], a["L1_conv_bias"])),
            "l1f": lambda: (layernorm(K, "l1t", 1e-5, False), graph_attention(K, "gat"),
                            moe(K, "l1f", 4, 256, "given", ("L1_ffn_W1", "L1_ffn_b1", "L1_ffn_W2", "L1_ffn_b2", None, None))),
            "l2c": lambda: (layernorm(K, "l2n", 1e-6, False), state_space(K, "l2c")),
            "l2f": lambda: (layernorm(K, "l2t", 1e-5, False),
                            moe(K, "l2f", 8, 128, "norm2", ("L2_ffn_w1", "L2_ffn_b1", "L2_ffn_w2", "L2_ffn_b2", "L2_ffn_router_w", None))),
            "l3c": lambda: (layernorm(K, "l3n", 1e-6, True), conv_residual(K, "l3c", a["L3_conv_W"])),
            "l3f": lambda: (layernorm(K, "l3t", 1e-5, False),
                            moe(K, "l3f", 8, 512, "first", ("L3_ffn_w1", "L3_ffn_b1", "L3_ffn_w2", "L3_ffn_b2", "L3_ffn_gate_w", "L3_ffn_gate_b"))),
        }
        for stage in stages or ("l0c", "l0f", "l1c", "l1f", "l2c", "l2f", "l3c", "l3f"):
            run[stage]()
            K.release()
        finish(K)


def layouts(v):
    f32 = np.float32
    out = {n: np.ascontiguousarray(v[n]) for n in v}
    for n in ("L1_conv_weight", "L3_conv_W"):
        out[n] = np.ascontiguousarray(v[n].transpose(1, 2, 3, 0).reshape(P, TAPS, P))
    w_off, b_off = v["L0_conv_w_off"].transpose(1, 2, 3, 0).reshape(P, TAPS, 3 * TAPS), v["L0_conv_b_off"]
    out["L0_conv_w_off"], out["L0_conv_b_off"] = np.zeros((P, TAPS, OFF_ROWS), f32), np.zeros((OFF_ROWS, 1), f32)
    y, x = np.divmod(np.arange(POS), SIDE)
    out["position_rows"] = np.zeros((OFF_ROWS, POS), f32)
    for to, src, at in ((DY_ROWS, 0, y), (DX_ROWS, TAPS, x), (MASK_ROWS, 2 * TAPS, 0 * x)):
        out["L0_conv_w_off"][:, :, to:to + TAPS] = w_off[:, :, src:src + TAPS]
        out["L0_conv_b_off"][to:to + TAPS, 0] = b_off[src:src + TAPS]
        out["position_rows"][to:to + TAPS] = at
    q = np.arange(P)
    out["neg_qy"] = -(4.0 * np.arange(CHUNKS)[None, :] + q[:, None] // SIDE).astype(f32)
    out["neg_qx"] = -(q[:, None] % SIDE).astype(f32)
    out["L0_conv_w_conv"] = np.ascontiguousarray(v["L0_conv_w_conv"].reshape(P, TAPS, P).transpose(2, 1, 0).reshape(P, TAPS * P))
    inner = lambda w: np.ascontiguousarray(w.reshape(HALVES, P, -1).transpose(1, 0, 2))
    w_x = v["L2_conv_W_x"]
    bc = w_x[:, DT_RANK:]
    out["L2_conv_W_x"] = inner(np.concatenate([bc, bc, bc, w_x[:, :DT_RANK]], axis=1))
    for n in ("L2_conv_W_out", "L2_conv_conv_w", "L2_conv_A_log"):
        out[n] = inner(v[n])
    for n in ("L2_conv_conv_b", "L2_conv_b_dt", "L2_conv_D"):
        out[n] = inner(v[n])[:, :, 0].copy()
    out["L1_ffn_att"] = np.broadcast_to(np.stack([v["L1_ffn_att_src"].reshape(-1), v["L1_ffn_att_dst"].reshape(-1)]), (P, 2, 16)).copy()
    out["L1_ffn_gat"] = np.broadcast_to(np.stack([v["L1_ffn_b_gat"], v["L1_ffn_ln_gamma"], v["L1_ffn_ln_beta"]]), (P, 3, 16)).copy()
    out["sort_sign"] = (1.0 - 2.0 * ((np.arange(P)[:, None] >> np.arange(LANE_BITS)) & 1)).astype(f32)
    out["column_number"] = np.broadcast_to(np.arange(P, dtype=f32), (P, P)).copy()
    out["strictly_below"] = np.triu(np.ones((P, P), f32), 1)
    out["L1_conv_bias"] = v["L1_conv_bias"].reshape(P, 1)
    for n in ("L0_ffn_b1", "L1_ffn_b1", "L2_ffn_b1", "L3_ffn_b1"):
        out[n] = np.ascontiguousarray(v[n].reshape(-1, P).T)
    out["L2_ffn_router_w"] = np.ascontiguousarray(v["L2_ffn_router_w"].T)
    for n in ("L0_ffn_gate_b", "L3_ffn_gate_b"):
        out[n] = np.broadcast_to(v[n], (P, v[n].size)).copy()
    out["identity"] = np.eye(P, dtype=f32)
    for e in (4, 8):
        out[f"pick{e}"] = np.tile(np.eye(e, dtype=f32), (3, 1))
        out[f"index{e}"] = np.broadcast_to(np.arange(e, dtype=f32) - 64, (P, TILES, e)).copy()
    return out


def kernel(**inputs):
    import concourse.bacc as _bacc
    from concourse.bass_utils import run_bass_kernel_spmd as _run

    nc = _bacc.Bacc("TRN2", target_bir_lowering=False, num_devices=1)
    arrays = layouts({k: np.asarray(x) for k, x in inputs.items()})
    a = {k: nc.dram_tensor("in_" + k, x.shape, mybir.dt.from_np(x.dtype), kind="ExternalInput").ap() for k, x in arrays.items()}
    a["out"] = nc.dram_tensor("out_dram", (IMAGES, P, SIDE, SIDE), FP32, kind="ExternalOutput").ap()
    metaformer(nc, a)
    r = _run(nc, [{"in_" + k: x for k, x in arrays.items()}], core_ids=[0])
    return r.results[0]["out_dram"]
```
